# Optimizing a Trainium2 kernel written in Bass

```python
import numpy as np
import jax
import jax.numpy as jnp

def _softmax(x, axis=-1):
    return jax.nn.softmax(x, axis=axis)

def _gelu(x):
    return jax.nn.gelu(x, approximate=True)

def _silu(x):
    return jax.nn.silu(x)

def _sigmoid(x):
    return jax.nn.sigmoid(x)

def _layernorm(x, axis=-1, eps=1e-05):
    m = jnp.mean(x, axis=axis, keepdims=True)
    v = jnp.var(x, axis=axis, keepdims=True)
    return (x - m) / jnp.sqrt(v + eps)

def _scatter_add(tgt, idx, src, axis=0):
    return tgt.at[idx].add(src)

def _segment_sum(src, seg, n):
    return jax.ops.segment_sum(src, seg, n)
kernel_name = 'mk_xattn_ffn_d1_seqx_r2_69ca5d'

def setup_inputs(seed: int=0):
    np.random.seed(seed)
    _w = jnp.asarray

    def _rec_inputs():
        import jax
        import jax.numpy as jnp
        _rk = jax.random.key(seed)
        x = 7.22e-05 + 1 * jax.random.normal(jax.random.fold_in(_rk, 1), (1, 4096, 512), jnp.float32)
        _lenS = 4096 - jax.random.randint(jax.random.fold_in(_rk, 7), (1,), 0, max(1, 4096 // 4) + 1, jnp.int32)
        _lenS2 = 3202 - jax.random.randint(jax.random.fold_in(_rk, 8), (1,), 0, max(1, 3202 // 4) + 1, jnp.int32)
        _ctx_768P = jax.random.normal(jax.random.fold_in(_rk, 11), (1, 16, 384), jnp.float32)
        _ctx_768c = jax.random.dirichlet(jax.random.fold_in(_rk, 511), 0.3 * jnp.ones((16,), jnp.float32), (1, 3202))
        _ctx_768t = jnp.einsum('bsk,bkd->bsd', _ctx_768c, _ctx_768P)
        _ctx_768t = _ctx_768t * jax.lax.rsqrt(jnp.mean(jnp.square(_ctx_768t)) + 1e-12) * 0.953939
        ctx_768 = 3.88148e-05 + 0.999967 * (_ctx_768t + 0.3 * jax.random.normal(jax.random.fold_in(_rk, 611), (1, 3202, 384), jnp.float32))
        _validS = jnp.arange(4096)[None, :] < _lenS[:, None]
        _validS2 = jnp.arange(3202)[None, :] < _lenS2[:, None]
        _causal = jnp.tril(jnp.ones((4096, 4096), dtype=bool))
        mask_BxS_bf1 = jnp.ones((1, 4096), dtype=bool)
        mask_BxS2_bf1 = jnp.ones((1, 3202), dtype=bool)
        return (x, ctx_768, mask_BxS_bf1, mask_BxS2_bf1)
    x, ctx_768, mask_BxS_bf1, mask_BxS2_bf1 = _rec_inputs()

    def _L0_xattn_setup():
        import jax, jax.numpy as jnp
        import numpy as np
        B, T, DT, G, DV = (16, 256, 512, 288, 384)
        H, DH = (4, 32)
        INNER = H * DH
        HID = 4 * DT
        N_STATE = 64
        K_TOP = 32

        def layernorm(x, g, b, eps=1e-05):
            m = x.mean(-1, keepdims=True)
            v = x.var(-1, keepdims=True)
            return (x - m) * jax.lax.rsqrt(v + eps) * g + b

        def s4d(x, log_dt, A_re, A_im, C_re, C_im, D_skip):
            Bb, L, D = x.shape
            dt = jnp.exp(log_dt)
            A = A_re + 1j * A_im
            C = C_re + 1j * C_im
            dtA = dt[:, None] * A
            dC = C * (jnp.exp(dtA) - 1.0) / A
            powers = jnp.exp(dtA[:, :, None] * jnp.arange(L))
            K = 2.0 * jnp.einsum('dn,dnl->dl', dC, powers).real
            n = 2 * L
            Kf = jnp.fft.rfft(K, n=n, axis=-1)
            xf = jnp.fft.rfft(x, n=n, axis=1)
            y = jnp.fft.irfft(xf * Kf.T[None], n=n, axis=1)[:, :L]
            return y + x * D_skip
        key = jax.random.key(seed)
        ks = jax.random.split(key, 16)
        s = 0.02
        inp = {'x_text': jax.random.normal(ks[0], (B, T, DT), jnp.float32), 'x_vision': jax.random.normal(ks[1], (B, G, DV), jnp.float32), 'text_mask': jnp.ones((B, T), bool), 'vision_mask': jnp.ones((B, G), bool), 'Wq': jax.random.normal(ks[2], (DT, INNER), jnp.float32) * s, 'Wk': jax.random.normal(ks[3], (DV, INNER), jnp.float32) * s, 'Wv': jax.random.normal(ks[4], (DV, DT), jnp.float32) * s, 'W_film_in': jax.random.normal(ks[5], (DT, 2 * DT), jnp.float32) * s, 'b_film_in': jnp.zeros((2 * DT,), jnp.float32), 'W_film_out': jax.random.normal(ks[6], (DT, 2 * DT), jnp.float32) * s, 'b_film_out': jnp.zeros((2 * DT,), jnp.float32), 'g_norm_in': jnp.ones((DT,), jnp.float32), 'b_norm_in': jnp.zeros((DT,), jnp.float32), 'g_norm_out': jnp.ones((DT,), jnp.float32), 'b_norm_out': jnp.zeros((DT,), jnp.float32), 'g_ffn': jnp.ones((DT,), jnp.float32), 'b_ffn': jnp.zeros((DT,), jnp.float32), 'W1': jax.random.normal(ks[7], (DT, HID), jnp.float32) * s, 'b1': jnp.zeros((HID,), jnp.float32), 'W2': jax.random.normal(ks[8], (HID, DT), jnp.float32) * s, 'b2': jnp.zeros((DT,), jnp.float32), 'log_dt': jnp.log(0.001) + jax.random.uniform(ks[9], (DT,), jnp.float32) * (jnp.log(0.1) - jnp.log(0.001)), 'A_re': -0.5 * jnp.ones((DT, N_STATE), jnp.float32), 'A_im': jnp.tile(jnp.pi * jnp.arange(N_STATE, dtype=jnp.float32), (DT, 1)), 'C_re': jax.random.normal(ks[10], (DT, N_STATE), jnp.float32) * 0.5 ** 0.5, 'C_im': jax.random.normal(ks[11], (DT, N_STATE), jnp.float32) * 0.5 ** 0.5, 'D_skip': jax.random.normal(ks[12], (DT,), jnp.float32), 'mod_gate': jnp.array(0.5, jnp.float32)}
        return inp
    _L0_xattn_all = _L0_xattn_setup()
    _L0_xattn_in = {k: v for k, v in _L0_xattn_all.items() if k in ('Wq', 'Wk', 'Wv', 'W_film_in', 'b_film_in', 'W_film_out', 'b_film_out', 'g_norm_in', 'b_norm_in', 'g_norm_out', 'b_norm_out', 'g_ffn', 'b_ffn', 'W1', 'b1', 'W2', 'b2', 'log_dt', 'A_re', 'A_im', 'C_re', 'C_im', 'D_skip', 'mod_gate')}
    del _L0_xattn_all

    def _L0_ffn_setup():
        import jax, jax.numpy as jnp
        import numpy as np
        B, S, D_MODEL, D_HIDDEN = (4, 1024, 512, 2048)

        def act_quant(x):
            scale = 127.0 / jnp.clip(jnp.max(jnp.abs(x), axis=-1, keepdims=True), 1e-05)
            return jnp.clip(jnp.round(x * scale), -128, 127) / scale

        def weight_quant(w):
            scale = 1.0 / jnp.clip(jnp.mean(jnp.abs(w)), 1e-05)
            return jnp.clip(jnp.round(w * scale), -1, 1) / scale

        def bit_linear(x, w):
            xq = x + jax.lax.stop_gradient(act_quant(x) - x)
            wq = w + jax.lax.stop_gradient(weight_quant(w) - w)
            return jnp.einsum('bsd,hd->bsh', xq, wq)

        def depthwise_conv1d(x_bcl, w, b):
            y = jax.lax.conv_general_dilated(x_bcl, w, window_strides=(1,), padding=[(1, 1)], dimension_numbers=('NCH', 'OIH', 'NCH'), feature_group_count=x_bcl.shape[1])
            return y + b[None, :, None]
        key = jax.random.key(seed)
        ks = jax.random.split(key, 5)
        lim1 = 1.0 / np.sqrt(D_MODEL)
        lim2 = 1.0 / np.sqrt(D_HIDDEN)
        limc = 1.0 / np.sqrt(3.0)
        return {'x': jax.random.normal(ks[0], (B, S, D_MODEL), dtype=jnp.float32), 'w1': jax.random.uniform(ks[1], (D_HIDDEN, D_MODEL), jnp.float32, -lim1, lim1), 'conv_w': jax.random.uniform(ks[2], (D_HIDDEN, 1, 3), jnp.float32, -limc, limc), 'conv_b': jax.random.uniform(ks[3], (D_HIDDEN,), jnp.float32, -limc, limc), 'w2': jax.random.uniform(ks[4], (D_MODEL, D_HIDDEN), jnp.float32, -lim2, lim2)}
    _L0_ffn_all = _L0_ffn_setup()
    _L0_ffn_in = {k: v for k, v in _L0_ffn_all.items() if k in ('w1', 'conv_w', 'conv_b', 'w2')}
    del _L0_ffn_all
    return {'x': x, 'ctx_768': ctx_768, 'mask_BxS_bf1': mask_BxS_bf1, 'mask_BxS2_bf1': mask_BxS2_bf1, 'L0_xattn_Wq': _L0_xattn_in['Wq'], 'L0_xattn_Wk': _L0_xattn_in['Wk'], 'L0_xattn_Wv': _L0_xattn_in['Wv'], 'L0_xattn_W_film_in': _L0_xattn_in['W_film_in'], 'L0_xattn_b_film_in': _L0_xattn_in['b_film_in'], 'L0_xattn_W_film_out': _L0_xattn_in['W_film_out'], 'L0_xattn_b_film_out': _L0_xattn_in['b_film_out'], 'L0_xattn_g_norm_in': _L0_xattn_in['g_norm_in'], 'L0_xattn_b_norm_in': _L0_xattn_in['b_norm_in'], 'L0_xattn_g_norm_out': _L0_xattn_in['g_norm_out'], 'L0_xattn_b_norm_out': _L0_xattn_in['b_norm_out'], 'L0_xattn_g_ffn': _L0_xattn_in['g_ffn'], 'L0_xattn_b_ffn': _L0_xattn_in['b_ffn'], 'L0_xattn_W1': _L0_xattn_in['W1'], 'L0_xattn_b1': _L0_xattn_in['b1'], 'L0_xattn_W2': _L0_xattn_in['W2'], 'L0_xattn_b2': _L0_xattn_in['b2'], 'L0_xattn_log_dt': _L0_xattn_in['log_dt'], 'L0_xattn_A_re': _L0_xattn_in['A_re'], 'L0_xattn_A_im': _L0_xattn_in['A_im'], 'L0_xattn_C_re': _L0_xattn_in['C_re'], 'L0_xattn_C_im': _L0_xattn_in['C_im'], 'L0_xattn_D_skip': _L0_xattn_in['D_skip'], 'L0_xattn_mod_gate': _L0_xattn_in['mod_gate'], 'L0_ffn_w1': _L0_ffn_in['w1'], 'L0_ffn_conv_w': _L0_ffn_in['conv_w'], 'L0_ffn_conv_b': _L0_ffn_in['conv_b'], 'L0_ffn_w2': _L0_ffn_in['w2']}

def reference(x, ctx_768, mask_BxS_bf1, mask_BxS2_bf1, L0_xattn_Wq, L0_xattn_Wk, L0_xattn_Wv, L0_xattn_W_film_in, L0_xattn_b_film_in, L0_xattn_W_film_out, L0_xattn_b_film_out, L0_xattn_g_norm_in, L0_xattn_b_norm_in, L0_xattn_g_norm_out, L0_xattn_b_norm_out, L0_xattn_g_ffn, L0_xattn_b_ffn, L0_xattn_W1, L0_xattn_b1, L0_xattn_W2, L0_xattn_b2, L0_xattn_log_dt, L0_xattn_A_re, L0_xattn_A_im, L0_xattn_C_re, L0_xattn_C_im, L0_xattn_D_skip, L0_xattn_mod_gate, L0_ffn_w1, L0_ffn_conv_w, L0_ffn_conv_b, L0_ffn_w2):
    import jax
    import jax.numpy as jnp

    def _L0_xattn_ref(x_text, x_vision, text_mask, vision_mask, Wq, Wk, Wv, W_film_in, b_film_in, W_film_out, b_film_out, g_norm_in, b_norm_in, g_norm_out, b_norm_out, g_ffn, b_ffn, W1, b1, W2, b2, log_dt, A_re, A_im, C_re, C_im, D_skip, mod_gate):
        import jax, jax.numpy as jnp
        import numpy as np
        B, T, DT, G, DV = (16, 256, 512, 288, 384)
        H, DH = (4, 32)
        INNER = H * DH
        HID = 4 * DT
        N_STATE = 64
        K_TOP = 32

        def layernorm(x, g, b, eps=1e-05):
            m = x.mean(-1, keepdims=True)
            v = x.var(-1, keepdims=True)
            return (x - m) * jax.lax.rsqrt(v + eps) * g + b

        def s4d(x, log_dt, A_re, A_im, C_re, C_im, D_skip):
            Bb, L, D = x.shape
            dt = jnp.exp(log_dt)
            A = A_re + 1j * A_im
            C = C_re + 1j * C_im
            dtA = dt[:, None] * A
            dC = C * (jnp.exp(dtA) - 1.0) / A
            powers = jnp.exp(dtA[:, :, None] * jnp.arange(L))
            K = 2.0 * jnp.einsum('dn,dnl->dl', dC, powers).real
            n = 2 * L
            Kf = jnp.fft.rfft(K, n=n, axis=-1)
            xf = jnp.fft.rfft(x, n=n, axis=1)
            y = jnp.fft.irfft(xf * Kf.T[None], n=n, axis=1)[:, :L]
            return y + x * D_skip
        Bb, Tt, D = x_text.shape
        Gg = x_vision.shape[1]
        Q = (x_text @ Wq).reshape(Bb, Tt, H, DH)
        K = (x_vision @ Wk).reshape(Bb, Gg, H, DH)
        scores = jnp.einsum('bthd,bghd->bhtg', Q, K) / np.sqrt(DH).astype(np.float32)
        scores = jnp.where(vision_mask[:, None, None, :], scores, -jnp.inf)
        topv, topi = jax.lax.top_k(scores, K_TOP)
        probs = jax.nn.softmax(topv, axis=-1)
        bi = jnp.arange(Bb)[:, None, None, None]
        hi = jnp.arange(H)[None, :, None, None]
        ti = jnp.arange(Tt)[None, None, :, None]
        attn = jnp.zeros_like(scores).at[bi, hi, ti, topi].set(probs)
        attn_mean = attn.mean(axis=1)
        V = x_vision @ Wv
        c_t = jnp.einsum('btg,bgd->btd', attn_mean, V)
        c_t = c_t * text_mask[..., None]
        x = layernorm(x_text, g_norm_in, b_norm_in)
        scale_in, shift_in = jnp.split(c_t @ W_film_in + b_film_in, 2, axis=-1)
        x = x * (1.0 + mod_gate * scale_in) + mod_gate * shift_in
        y = s4d(x, log_dt, A_re, A_im, C_re, C_im, D_skip)
        scale_out, shift_out = jnp.split(c_t @ W_film_out + b_film_out, 2, axis=-1)
        y = y * (1.0 + mod_gate * scale_out) + mod_gate * shift_out
        xt = x_text + y
        h = layernorm(xt, g_ffn, b_ffn)
        h = jax.nn.gelu(h @ W1 + b1, approximate=False) @ W2 + b2
        xt = xt + h
        return layernorm(xt, g_norm_out, b_norm_out)

    def _L0_ffn_ref(x, w1, conv_w, conv_b, w2):
        import jax, jax.numpy as jnp
        import numpy as np
        B, S, D_MODEL, D_HIDDEN = (4, 1024, 512, 2048)

        def act_quant(x):
            scale = 127.0 / jnp.clip(jnp.max(jnp.abs(x), axis=-1, keepdims=True), 1e-05)
            return jnp.clip(jnp.round(x * scale), -128, 127) / scale

        def weight_quant(w):
            scale = 1.0 / jnp.clip(jnp.mean(jnp.abs(w)), 1e-05)
            return jnp.clip(jnp.round(w * scale), -1, 1) / scale

        def bit_linear(x, w):
            xq = x + jax.lax.stop_gradient(act_quant(x) - x)
            wq = w + jax.lax.stop_gradient(weight_quant(w) - w)
            return jnp.einsum('bsd,hd->bsh', xq, wq)

        def depthwise_conv1d(x_bcl, w, b):
            y = jax.lax.conv_general_dilated(x_bcl, w, window_strides=(1,), padding=[(1, 1)], dimension_numbers=('NCH', 'OIH', 'NCH'), feature_group_count=x_bcl.shape[1])
            return y + b[None, :, None]
        h = bit_linear(x, w1)
        h = depthwise_conv1d(h.transpose(0, 2, 1), conv_w, conv_b)
        h = h.transpose(0, 2, 1)
        h = jax.nn.silu(h)
        return bit_linear(h, w2)
    x = x + _L0_xattn_ref(_layernorm(x, axis=-1), ctx_768, mask_BxS_bf1, mask_BxS2_bf1, L0_xattn_Wq, L0_xattn_Wk, L0_xattn_Wv, L0_xattn_W_film_in, L0_xattn_b_film_in, L0_xattn_W_film_out, L0_xattn_b_film_out, L0_xattn_g_norm_in, L0_xattn_b_norm_in, L0_xattn_g_norm_out, L0_xattn_b_norm_out, L0_xattn_g_ffn, L0_xattn_b_ffn, L0_xattn_W1, L0_xattn_b1, L0_xattn_W2, L0_xattn_b2, L0_xattn_log_dt, L0_xattn_A_re, L0_xattn_A_im, L0_xattn_C_re, L0_xattn_C_im, L0_xattn_D_skip, L0_xattn_mod_gate)
    x = x + _L0_ffn_ref(_layernorm(x, axis=-1), L0_ffn_w1, L0_ffn_conv_w, L0_ffn_conv_b, L0_ffn_w2)
    return x

_drawn_inputs = setup_inputs


def setup_inputs(seed=0):
    import zlib

    import numpy as np

    out = dict(_drawn_inputs(seed))
    spreads = {'L0_xattn_b_film_in': (0.0, 0.1),
     'L0_xattn_b_film_out': (0.0, 0.277),
     'L0_xattn_g_norm_in': (1.0, 0.2),
     'L0_xattn_b_norm_in': (0.0, 0.1),
     'L0_xattn_g_norm_out': (1.0, 0.2),
     'L0_xattn_b_norm_out': (0.0, 0.1),
     'L0_xattn_g_ffn': (1.0, 0.6),
     'L0_xattn_b_ffn': (0.0, 0.8),
     'L0_xattn_b1': (0.0, 0.523),
     'L0_xattn_b2': (0.0, 0.283),
     'L0_xattn_A_re': (-0.5, 0.2)}
    factors = {}
    for name, (base, spread) in spreads.items():
        noise = np.random.default_rng([zlib.crc32(name.encode()), seed]).standard_normal(out[name].shape)
        drawn = base * np.exp(spread * noise) if base else spread * noise
        out[name] = jnp.asarray(drawn.astype(out[name].dtype))
    for name, factor in factors.items():
        out[name] = (out[name] * factor).astype(out[name].dtype)
    return out
```

```python
import math
from contextlib import ExitStack

import numpy as np

import concourse.bass as bass
from concourse import mybir

F32 = mybir.dt.float32
BF16 = mybir.dt.bfloat16
F32R = mybir.dt.float32r
I32 = mybir.dt.int32
U8 = mybir.dt.uint8
ALU = mybir.AluOpType
ACT = mybir.ActivationFunctionType
AX = mybir.AxisListType

P = 128
T, D = 4096, 512
G, DV = 3202, 384
H, DH = 4, 32
INNER = H * DH
TOP = 32
HID = 2048
NS = 64
TILES = T // P
GC = -(-G // P)
GLAST = G - (GC - 1) * P
DC = D // P
VC = DV // P
QUAD = 4
EPS = 1e-5
SCALE = 1.0 / math.sqrt(DH)
SEGS = 32
SEG = G // SEGS
CAND = SEGS * 8
LOWEST = -3.0e38
MASKED = 1.0e30
BANK = 512
SCORE_CHUNKS = -(-G // BANK)
ROUND = 1.5 * 2 ** 23


def phase_scope(nc):
    scope = ExitStack()

    def sb(name, shape, dt=F32):
        return scope.enter_context(nc.sbuf_tensor(name, shape, dt))

    def ps(name, shape, dt=F32):
        return scope.enter_context(nc.psum_tensor(name, shape, dt))

    return scope, sb, ps


I8 = mybir.dt.int8


def before(m, b):
    return (m, 0) if b else (m - 1, 1)


def after(m, b):
    return (m + 1, 0) if b else (m, 1)


def normalise_quad(nc, x, out, stats, mv, rstd, std_wanted, std_ready, turn):
    for k in range(QUAD):
        nc.vector.bn_stats(stats[:, k, :], x[:, k, :])
    nc.vector.drain()
    for k in range(QUAD):
        last = nc.vector.bn_aggr(mv[:, k, :], stats[:, k, :])
    last.then_inc(std_wanted, 1)
    nc.vector.wait_ge(std_ready, turn + 1)
    nc.vector.reciprocal(rstd[:], rstd[:])
    nc.vector.drain()
    for k in range(QUAD):
        last = nc.vector.tensor_scalar(out[:, k, :], x[:, k, :], mv[:, k, 0:1], rstd[:, k:k + 1],
                                       ALU.subtract, ALU.mult)
    return last


def key_rows(h):
    at = h % 2 * 2 * DH
    return slice(at, at + DH), slice(at + DH, at + 2 * DH), slice(h * DH, (h + 1) * DH)


def prepare_attention(nc, sem, const, a, KT, dram):
    scope, sb, ps = phase_scope(nc)
    ident, eps = const["ident"], const["eps"]
    x_q = a["x"].rearrange("(q k p) d -> q p k d", k=QUAD, p=P)
    xt_q = dram["xt"].rearrange("(q k p) d -> q p k d", k=QUAD, p=P)
    ctx_q = a["ctx"][0:24 * P, :].rearrange("(q k p) c -> q p k c", k=QUAD, p=P)
    with scope:
        wq = sb("wq", [P, DC, INNER])
        wk = sb("wk", [P, VC, INNER])
        x_in = sb("x_in", [P, 2, QUAD, D])
        xt = sb("xt_prep", [P, 2, QUAD, D])
        xtT = sb("xtT_prep", [P, DC, QUAD * P])
        qt = sb("qt_prep", [P, 2, 2, QUAD * P], F32R)
        stats = sb("stats_prep", [P, QUAD, 6])
        mv = sb("mv_prep", [P, QUAD, 2])
        rstd = sb("rstd_prep", [P, QUAD])
        cx = sb("cx_prep", [P, 2, QUAD, DV])
        cxT = sb("cxT_prep", [P, VC, QUAD * P])
        tp = ps("tp_prep", [P, DC, BANK])
        qp = ps("qp_prep", [P, BANK])
        kp = ps("kp_prep", [P, BANK])
        quads = T // (QUAD * P)
        cquads = 24 // QUAD
        s = {n: sem("prep_" + n) for n in (
            "weights_in", "x_loaded0", "x_loaded1", "x_read", "std_wanted", "std_ready", "xt_ready", "xt_turned", "xtT_ready",
            "q_done", "q_copied", "q_stored", "xt_stored", "stored", "cx_loaded0", "cx_loaded1", "cx_turned", "cxT_ready", "k_done",
            "k_high", "k_copied", "xt_transposed")}

        with nc.Block() as block:
            @block.sync
            def _(sp):
                sp.dma_start(wq[:], a["Wq"].rearrange("(c p) n -> p c n", p=P)).then_inc(s["weights_in"], 16)
                sp.dma_start(wk[:], a["Wk"].rearrange("(c p) n -> p c n", p=P)).then_inc(s["weights_in"], 16)

                with sp.Fori(0, quads // 2) as i:
                    for b in range(2):
                        q = 2 * i + b
                        sp.wait_ge(s["x_read"], q + 1)
                        sp.dma_start(x_in[:, b], x_q[q, :, :, :]).then_inc(s[f"x_loaded{b}"], 16)
                with sp.Fori(0, cquads // 2) as i:
                    for b in range(2):
                        sp.wait_ge(s["cx_turned"], 2 * i + b + 1)
                        sp.dma_start(cx[:, b], ctx_q[2 * i + b, :, :, :]).then_inc(s[f"cx_loaded{b}"], 16)
                sp.wait_ge(s["cx_turned"], cquads + 1)
                sp.dma_start(cx[:, 0, 0, :], a["ctx"][24 * P:25 * P, :]).then_inc(s["cx_loaded0"], 16)
                sp.dma_start(cx[0:GLAST, 0, 1, :], a["ctx"][25 * P:G, :]).then_inc(s["cx_loaded0"], 16)

            @block.gpsimd
            def _(pool):
                with pool.Fori(0, quads // 2) as i:
                    for b in range(2):
                        q = 2 * i + b
                        pool.wait_ge(s["xt_ready"], q + 1)
                        pool.dma_start(xt_q[q, :, :, :], xt[:, b]).then_inc(s["xt_stored"], 16)
                        pool.wait_ge(s["q_copied"], q + 1)
                        pool.dma_start(dram["qt"][:, :, bass.ts(q, QUAD * P)].rearrange("c p t -> p c t"), qt[:, b].bitcast(F32)).then_inc(s["q_stored"], 16)
                        pool.wait_ge(s["xt_stored"], 16 * (q + 1))
                        pool.wait_ge(s["q_stored"], 16 * (q + 1))
                        pool.sem_inc(s["stored"], 1)

            @block.vector
            def _(dve):
                dve.sem_inc(s["x_read"], 2)
                dve.sem_inc(s["stored"], 2)
                with dve.Fori(0, quads // 2) as i:
                    for b in range(2):
                        q = 2 * i + b
                        dve.wait_ge(s[f"x_loaded{b}"], 16 * (i + 1))
                        dve.wait_ge(s["stored"], q + 1)
                        normalise_quad(nc, x_in[:, b], xt[:, b], stats, mv, rstd, s["std_wanted"], s["std_ready"],
                                       q).then_inc(s["xt_ready"], 1)
                        dve.drain()
                        dve.sem_inc(s["x_read"], 1)
                        dve.wait_ge(s["q_done"], q + 1)
                        nc.vector.tensor_copy(qt[:, b, 0], qp[:])
                        dve.drain()
                        nc.vector.tensor_tensor(qt[:, b, 1], qp[:], qt[:, b, 0].bitcast(F32), ALU.subtract).then_inc(s["q_copied"], 1)
                for q in range(cquads + 1):
                    w = QUAD * P if q < cquads else P + GLAST
                    dve.wait_ge(s["k_high"], q + 1)
                    for h in range(H):
                        high, low, src = key_rows(h)
                        last = nc.vector.tensor_tensor(KT[low, h // 2, q * BANK:q * BANK + w], kp[src, 0:w],
                                                       KT[high, h // 2, q * BANK:q * BANK + w].bitcast(F32), ALU.subtract)
                    last.then_inc(s["k_copied"], 1)

            @block.scalar
            def _(act):
                with act.Fori(0, quads) as q:
                    act.wait_ge(s["std_wanted"], q + 1)
                    nc.scalar.activation(rstd[:], mv[:, :, 1], ACT.Sqrt, bias=eps[:, 0:1]).then_inc(s["std_ready"], 1)
                    act.wait_ge(s["xt_turned"], q + 1)
                    nc.scalar.activation(xtT[:], tp[:], ACT.Copy).then_inc(s["xtT_ready"], 1)
                for q in range(cquads + 1):
                    w = QUAD * P if q < cquads else P + GLAST
                    act.wait_ge(s["cx_turned"], q + 3)
                    nc.scalar.activation(cxT[:, :, 0:w], tp[:, 0:VC, 0:w], ACT.Copy).then_inc(s["cxT_ready"], 1)
                    act.wait_ge(s["k_done"], q + 1)
                    for h in range(H):
                        high, _, src = key_rows(h)
                        last = nc.scalar.activation(KT[high, h // 2, q * BANK:q * BANK + w], kp[src, 0:w], ACT.Copy)
                    last.then_inc(s["k_high"], 1)

            @block.tensor
            def _(pe):
                pe.sem_inc(s["cx_turned"], 2)
                pe.wait_ge(s["weights_in"], 32)
                with pe.Fori(0, quads // 2) as i:
                    for b in range(2):
                        q = 2 * i + b
                        pe.wait_ge(s["xt_ready"], q + 1)
                        for c in range(DC):
                            for k in range(QUAD):
                                last = nc.tensor.transpose(tp[:, c, k * P:(k + 1) * P], xt[:, b, k, c * P:(c + 1) * P],
                                                           ident[:])
                        last.then_inc(s["xt_turned"], 1)
                        pe.wait_ge(s["xtT_ready"], q + 1)
                        for c in range(DC):
                            last = nc.tensor.matmul(qp[:], lhsT=wq[:, c, :], rhs=xtT[:, c, :], start=(c == 0),
                                                    stop=(c == DC - 1))
                        last.then_inc(s["q_done"], 1)
                for q in range(cquads + 1):
                    parts = [(k, P) for k in range(QUAD)] if q < cquads else [(0, P), (1, GLAST)]
                    w = sum(n for _, n in parts)
                    pe.wait_ge(s[f"cx_loaded{q % 2}"], 16 * (q // 2 + 1) if q < cquads else 16 * (q // 2 + 2))
                    for c in range(VC):
                        for k, n in parts:
                            last = nc.tensor.transpose(tp[:, c, k * P:k * P + n], cx[0:n, q % 2, k, c * P:(c + 1) * P],
                                                       ident[0:n, 0:n])
                    last.then_inc(s["cx_turned"], 1)
                    pe.wait_ge(s["cxT_ready"], q + 1)
                    if q:
                        pe.wait_ge(s["k_copied"], q)
                    for c in range(VC):
                        last = nc.tensor.matmul(kp[:, 0:w], lhsT=wk[:, c, :], rhs=cxT[:, c, 0:w], start=(c == 0),
                                                stop=(c == VC - 1))
                    last.then_inc(s["k_done"], 1)


def attention(nc, sem, const, a, KT, dram):
    scope, sb, ps = phase_scope(nc)
    ident, ones = const["ident"], const["ones"]
    with scope:
        ctx = sb("ctx", [P, GC, DV])
        hidden = sb("hidden", [P, G], I8)
        S = sb("S", [P, 2, H, G])
        E = sb("E", [P, 2, G])
        attnT = sb("attnT", [P, 2, 4, P])
        q = sb("q", [P, 2, H // 2, P], F32R)
        cand = sb("cand", [P, H, CAND])
        tops = sb("tops", [P, 2, H, TOP])
        seg8 = sb("seg8", [P, H])
        left = sb("left", [P, H])
        bad = sb("bad", [P, H])
        badi = sb("badi", [1, H + 1], I32)
        masked = sb("masked", [1, 1], I32)
        mrow = sb("mrow", [1, 1])
        tmask8 = sb("tmask8", [P, TILES], U8)
        tmask = sb("tmask", [P, TILES])
        nmax = sb("nmax", [P, H])
        etop = sb("etop", [P, H, TOP], BF16)
        den = sb("den", [P, H])
        lden = sb("lden", [P, H])
        ebias = sb("ebias", [P, 2, H])
        u = sb("u", [P, DV])
        score = [ps(f"score{k}", [P, 2, BANK]) for k in range(2)]
        tp = [ps(f"turn{k}", [P, 4, P]) for k in range(2)]
        up = ps("up", [P, BANK])
        fp = ps("fp", [P, BANK])
        mask8 = E[:, 0, :].bitcast(U8)[:, 0:G]
        s = {n: sem("attn_" + n) for n in (
            "ctx_in", "mask_in", "tmask_ready", "q_in", "q_free", "score_done", "score_copied", "flags_wanted",
            "flags_done", "tops_final", "lden_ready", "ebias_ready", "e_ready", "e_used", "pair_summed", "summed", "turned",
            "turn_copied", "times_done", "u_copied", "u_stored", "u_free", "passed")}
        ORDER = (1, 3, 2, 0)
        HALVES = -(-SCORE_CHUNKS // 2)
        GROUPS = H * HALVES
        TURNS = SCORE_CHUNKS

        def chunk(j):
            return slice(j * BANK, min((j + 1) * BANK, G))

        with nc.Block() as block:
            @block.sync
            def _(sp):
                sp.dma_start(mask8, a["mask2"].partition_broadcast(P)).then_inc(s["mask_in"], 16)
                sp.dma_start(tmask8[:], a["mask1"].rearrange("(n p) -> p n", p=P), allow_slow_non_contiguous=True).then_inc(s["mask_in"], 16)
                qd = dram["qt"].rearrange("c (p e d) t -> e d c p t", e=2, d=DH)
                with sp.Fori(0, TILES) as n:
                    sp.wait_ge(s["q_free"], n + 1)
                    for e in range(2):
                        for r in range(2):
                            at = (2 * e + r) * DH
                            sp.dma_start(q[at:at + DH].bitcast(F32), qd[e, :, :, :, bass.ts(n, P)]).then_inc(s["q_in"], 16)

            @block.gpsimd
            def _(pool):
                def bias(m, b):
                    pool.wait_ge(s["lden_ready"], 2 * m + b + 1)
                    nc.gpsimd.tensor_tensor(ebias[:, b, :], nmax[:], lden[:], ALU.subtract).then_inc(s["ebias_ready"], 1)

                def sums(m, b):
                    n = 2 * m + b
                    pool.wait_ge(s["e_used"], H * n + 4)
                    nc.gpsimd.tensor_tensor(S[:, b, 0, :], S[:, b, 0, :], S[:, b, 1, :], ALU.add).then_inc(s["pair_summed"], 1)
                    pool.wait_ge(s["e_used"], H * n + 6)
                    nc.gpsimd.tensor_tensor(S[:, b, 2, :], S[:, b, 2, :], S[:, b, 3, :], ALU.add).then_inc(s["pair_summed"], 1)
                    pool.drain()
                    for j in range(SCORE_CHUNKS):
                        nc.gpsimd.tensor_tensor(S[:, b, 0, chunk(j)], S[:, b, 0, chunk(j)], S[:, b, 2, chunk(j)],
                                                ALU.add).then_inc(s["summed"], 1)

                def store(m, b):
                    n = 2 * m + b
                    pool.wait_ge(s["u_copied"], n + 2)
                    pool.dma_start(dram["u"][bass.ts(n, P), :], u[:]).then_inc(s["u_stored"], 16)
                    pool.wait_ge(s["u_stored"], 16 * (n + 1))
                    pool.sem_inc(s["u_free"], 1)

                def turn(m, b):
                    bias(*before(m, b))
                    sums(*before(m, b))
                    store(*before(m, b))

                turn(0, 1)
                with pool.Fori(0, (TILES - 2) // 2) as i:
                    turn(i + 1, 0)
                    turn(i + 1, 1)
                turn(TILES // 2, 0)

            @block.vector
            def _(dve):
                dve.wait_ge(s["mask_in"], 32)
                nc.vector.tensor_scalar(hidden[:], mask8, 1.0, None, ALU.subtract)
                nc.vector.tensor_reduce(mrow[:], mask8[0:1, :], AX.X, ALU.min)
                nc.vector.tensor_copy(tmask[:], tmask8[:]).then_inc(s["tmask_ready"], 1)
                dve.drain()
                nc.vector.tensor_scalar(mrow[:], mrow[:], -1.0, 1.0, ALU.mult, ALU.add)
                dve.drain()
                nc.vector.tensor_copy(masked[:], mrow[:])
                dve.drain()
                any_masked = dve.value_load(masked[0:1, 0:1], min_val=0, max_val=1)

                def arrived(n, groups):
                    dve.wait_ge(s["score_copied"], GROUPS * n + groups + 2)
                    dve.sem_inc(s["passed"], 1)

                def segments(m, b, h):
                    n = 2 * m + b
                    arrived(n, HALVES * (ORDER.index(h) + 1))
                    with dve.If(any_masked > 0):
                        nc.vector.scalar_tensor_tensor(S[:, b, h, :], hidden[:], MASKED, S[:, b, h, :], ALU.mult, ALU.add)
                        dve.drain()
                    for k in range(SEGS):
                        end = (k + 1) * SEG if k < SEGS - 1 else G
                        nc.vector.max(cand[:, h, 8 * k:8 * k + 8], S[:, b, h, k * SEG:end])

                def keep_top(m, b, h):
                    dve.wait_ge(s["e_ready"], H * (2 * m + b) + h + 1)
                    nc.vector.scalar_tensor_tensor(S[:, b, h, :], S[:, b, h, :], tops[:, b, h, TOP - 1:TOP], E[:, h % 2, :],
                                                   ALU.is_ge, ALU.mult).then_inc(s["e_used"], 1)

                def exact(b, h):
                    src, rest = S[:, b, h, :], E[:, 0, :]
                    for r in range(TOP // 8):
                        nc.vector.max(tops[:, b, h, 8 * r:8 * r + 8], src)
                        dve.drain()
                        nc.vector.match_replace(rest, tops[:, b, h, 8 * r:8 * r + 8], src, LOWEST)
                        dve.drain()
                        src = rest
                    nc.vector.tensor_tensor(rest, rest, S[:, b, h, :], ALU.is_equal)
                    dve.drain()
                    nc.vector.scalar_tensor_tensor(S[:, b, h, :], rest, LOWEST, S[:, b, h, :], ALU.mult, ALU.add)
                    dve.drain()

                def thresholds(m, b):
                    dve.drain()
                    nc.vector.tensor_reduce(seg8[:], cand[:, :, 7::8], AX.X, ALU.max)
                    for r in range(TOP // 8):
                        for h in range(H):
                            nc.vector.max(tops[:, b, h, 8 * r:8 * r + 8], cand[:, h, :])
                        dve.drain()
                        if r < TOP // 8 - 1:
                            for h in range(H):
                                nc.vector.match_replace(cand[:, h, :], tops[:, b, h, 8 * r:8 * r + 8], cand[:, h, :], LOWEST)
                            dve.drain()
                    for h in range(H):
                        nc.vector.tensor_scalar(cand[:, h, :], cand[:, h, :], tops[:, b, h, TOP - 1:TOP], 0.0,
                                                ALU.is_ge, ALU.add, accum_out=left[:, h:h + 1])
                    nc.vector.tensor_tensor(bad[:], seg8[:], tops[:, b, :, TOP - 1], ALU.is_ge)
                    dve.drain()
                    nc.vector.scalar_tensor_tensor(bad[:], left[:], 8.0, bad[:], ALU.not_equal, ALU.add).then_inc(s["flags_wanted"], 1)

                def check(m, b):
                    dve.wait_ge(s["flags_done"], 2 * m + b + 1)
                    nc.vector.tensor_copy(badi[0:1, 0:H], fp[0:1, 0:H])
                    nc.vector.tensor_reduce(badi[0:1, H:H + 1], fp[0:1, 0:H], AX.X, ALU.max)
                    dve.drain()
                    some = dve.value_load(badi[0:1, H:H + 1], min_val=0, max_val=2 * P)
                    with dve.If(some > 0):
                        for h in range(H):
                            this = dve.value_load(badi[0:1, h:h + 1], min_val=0, max_val=2 * P)
                            with dve.If(this > 0):
                                exact(b, h)
                    dve.drain()
                    dve.sem_inc(s["tops_final"], 1)

                def turn(m, b, first=False):
                    segments(m, b, ORDER[0])
                    if not first:
                        check(*before(m, b))
                    segments(m, b, ORDER[1])
                    if not first:
                        for h in range(H):
                            keep_top(*before(m, b), h)
                    segments(m, b, ORDER[2])
                    segments(m, b, ORDER[3])
                    thresholds(m, b)

                dve.sem_inc(s["e_used"], 2)
                turn(0, 0, first=True)
                with dve.Fori(0, (TILES - 2) // 2) as i:
                    turn(i, 1)
                    turn(i + 1, 0)
                turn(TILES // 2 - 1, 1)
                check(TILES // 2 - 1, 1)
                for h in range(H):
                    keep_top(TILES // 2 - 1, 1, h)

            @block.scalar
            def _(act):
                act.dma_start(ctx[:, 0:GC - 1, :], a["ctx"][0:(GC - 1) * P, :].rearrange("(k p) c -> p k c", p=P)).then_inc(s["ctx_in"], 16)
                act.dma_start(ctx[0:GLAST, GC - 1, :], a["ctx"][(GC - 1) * P:G, :]).then_inc(s["ctx_in"], 16)
                act.sem_inc(s["score_copied"], 2)
                act.sem_inc(s["turn_copied"], 2)
                act.sem_inc(s["u_free"], 1)
                act.sem_inc(s["u_copied"], 1)

                def copy_scores(m, b, h):
                    n = 2 * m + b
                    for k in range(HALVES):
                        act.wait_ge(s["score_done"], GROUPS * n + HALVES * ORDER.index(h) + k + 1)
                        w = min(2 * BANK, G - 2 * BANK * k)
                        nc.scalar.activation(S[:, b, h, 2 * BANK * k:2 * BANK * k + w],
                                             score[k % 2][:, :, :].rearrange("p c k -> p (c k)")[:, 0:w],
                                             ACT.Copy).then_inc(s["score_copied"], 1)

                def probabilities(m, b):
                    n = 2 * m + b
                    act.wait_ge(s["tops_final"], n + 1)
                    nc.scalar.mul(nmax[:], tops[:, b, :, 0], -SCALE)
                    act.drain()
                    for h in range(H):
                        nc.scalar.activation(etop[:, h, :], tops[:, b, h, :], ACT.Exp, bias=nmax[:, h:h + 1], scale=SCALE,
                                             accum_out=den[:, h:h + 1])
                    act.drain()
                    nc.scalar.activation(lden[:], den[:], ACT.Ln, scale=float(H)).then_inc(s["lden_ready"], 1)
                    act.wait_ge(s["ebias_ready"], n + 1)
                    for h in range(H):
                        act.wait_ge(s["e_used"], H * n + h + 1)
                        nc.scalar.activation(E[:, h % 2, :], S[:, b, h, :], ACT.Exp, bias=ebias[:, b, h:h + 1],
                                             scale=SCALE).then_inc(s["e_ready"], 1)

                def copy_turned(m, b, g):
                    n = 2 * m + b
                    act.wait_ge(s["turned"], TURNS * n + g + 1)
                    act.wait_ge(s["times_done"], TURNS * n + g + 1)
                    w = min(4, GC - 4 * g)
                    e = (TURNS * b + g) % 2
                    if g < TURNS - 1:
                        nc.scalar.activation(attnT[:, e], tp[e][:], ACT.Copy).then_inc(s["turn_copied"], 1)
                    else:
                        nc.scalar.activation(attnT[:, e, 0:w - 1, :], tp[e][:, 0:w - 1, :], ACT.Copy)
                        nc.scalar.activation(attnT[0:GLAST, e, w - 1, :], tp[e][0:GLAST, w - 1, :], ACT.Copy).then_inc(s["turn_copied"], 1)

                def copy_context(m, b):
                    n = 2 * m + b
                    act.wait_ge(s["times_done"], TURNS * (n + 1) + 2)
                    act.wait_ge(s["u_free"], n + 1)
                    nc.scalar.activation(u[:], up[:, 0:DV], ACT.Copy, scale=tmask[:, bass.ds(n, 1)]).then_inc(s["u_copied"], 1)

                act.wait_ge(s["tmask_ready"], 1)
                for h in ORDER:
                    copy_scores(0, 0, h)
                for h in ORDER:
                    copy_scores(0, 1, h)

                def turn(m, b, last=False):
                    probabilities(*before(m, b))
                    if not last:
                        copy_scores(*after(m, b), ORDER[0])
                        copy_scores(*after(m, b), ORDER[1])
                    for g in range(TURNS):
                        copy_turned(*before(m, b), g)
                    if not last:
                        copy_scores(*after(m, b), ORDER[2])
                    copy_context(*before(m, b))
                    if not last:
                        copy_scores(*after(m, b), ORDER[3])

                turn(0, 1)
                with act.Fori(0, (TILES - 4) // 2) as i:
                    turn(i + 1, 0)
                    turn(i + 1, 1)
                turn(TILES // 2 - 1, 0)
                turn(TILES // 2 - 1, 1, last=True)
                turn(TILES // 2, 0, last=True)

            @block.tensor
            def _(pe):
                pe.sem_inc(s["times_done"], 2)
                pe.sem_inc(s["q_free"], 1)

                def scores(m, b, h):
                    n = 2 * m + b
                    at = slice(h % 2 * 2 * DH, (h % 2 + 1) * 2 * DH)
                    if h == ORDER[0]:
                        pe.wait_ge(s["q_in"], 16 * 4 * (n + 1))
                    for k in range(HALVES):
                        pe.wait_ge(s["score_copied"], GROUPS * n + HALVES * ORDER.index(h) + k + 1)
                        for j in range(2 * k, min(2 * k + 2, SCORE_CHUNKS)):
                            w = chunk(j).stop - chunk(j).start
                            for part in range(2):
                                last = nc.tensor.matmul(score[k % 2][:, j % 2, 0:w], lhsT=q[at, part, h // 2, :],
                                                        rhs=KT[at, h // 2, chunk(j)], start=(part == 0), stop=(part == 1))
                        last.then_inc(s["score_done"], 1)

                def scores_end():
                    pe.drain()
                    pe.sem_inc(s["q_free"], 1)

                def flags(m, b):
                    pe.wait_ge(s["flags_wanted"], 2 * m + b + 1)
                    nc.tensor.matmul(fp[0:1, 0:H], lhsT=ones[:, 0:1], rhs=bad[:], start=True, stop=True).then_inc(s["flags_done"], 1)

                def turn_attention(m, b, g):
                    n = 2 * m + b
                    pe.wait_ge(s["summed"], TURNS * n + g + 1)
                    pe.wait_ge(s["turn_copied"], TURNS * n + g + 1)
                    e = (TURNS * b + g) % 2
                    for c in range(4 * g, min(4 * g + 4, GC)):
                        w = P if c < GC - 1 else GLAST
                        last = nc.tensor.transpose(tp[e][0:w, c - 4 * g, :], S[:, b, 0, c * P:c * P + w], ident[:])
                    last.then_inc(s["turned"], 1)

                def times_context(m, b, g):
                    n = 2 * m + b
                    pe.wait_ge(s["turn_copied"], TURNS * n + g + 3)
                    if g == 0:
                        pe.wait_ge(s["u_copied"], n + 1)
                    e = (TURNS * b + g) % 2
                    for c in range(4 * g, min(4 * g + 4, GC)):
                        w = P if c < GC - 1 else GLAST
                        last = nc.tensor.matmul(up[:, 0:DV], lhsT=attnT[0:w, e, c - 4 * g, :], rhs=ctx[0:w, c, :],
                                                start=(c == 0), stop=(c == GC - 1))
                    last.then_inc(s["times_done"], 1)

                def turn(m, b, last=False, beyond=False):
                    old, new = before(m, b), after(m, b)
                    if not last:
                        pe.wait_ge(s["pair_summed"], 2 * (2 * m + b) - 1)
                        scores(*new, ORDER[0])
                        pe.wait_ge(s["pair_summed"], 2 * (2 * m + b))
                        scores(*new, ORDER[1])
                    turn_attention(*old, 0)
                    for g in range(TURNS):
                        if g < TURNS - 1:
                            turn_attention(*old, g + 1)
                        if g == TURNS - 2 and not beyond:
                            flags(m, b)
                        if g == TURNS - 1 and not last:
                            scores(*new, ORDER[2])
                        times_context(*old, g)
                    if not last:
                        scores(*new, ORDER[3])
                        scores_end()

                pe.wait_ge(s["ctx_in"], 32)
                for h in ORDER:
                    scores(0, 0, h)
                scores_end()
                for h in ORDER:
                    scores(0, 1, h)
                scores_end()
                flags(0, 0)
                turn(0, 1)
                with pe.Fori(0, (TILES - 4) // 2) as i:
                    turn(i + 1, 0)
                    turn(i + 1, 1)
                turn(TILES // 2 - 1, 0)
                turn(TILES // 2 - 1, 1, last=True)
                turn(TILES // 2, 0, last=True, beyond=True)


def film_weights(nc, sem, const, a, side, wf, fb):
    scope, sb, ps = phase_scope(nc)
    with scope:
        tag = "film_" + side
        wv = sb(tag + "_wv", [P, VC, D])
        wvT = sb(tag + "_wvT", [P, DC, DV])
        w = sb(tag + "_w", [P, DC, 2 * D])
        gate = sb(tag + "_gate", [P, 1])
        tp = ps(tag + "_tp", [P, VC, BANK])
        mp = [ps(f"{tag}_mp{k}", [P, BANK]) for k in range(2)]
        s = {n: sem(f"{tag}_{n}") for n in ("in", "turned", "turn_copied", "multiplied", "copied", "offset")}
        products = [(c, half) for c in range(VC) for half in range(2)]

        with nc.Block() as block:
            @block.sync
            def _(sp):
                sp.dma_start(wv[:], a["Wv"].rearrange("(c p) n -> p c n", p=P)).then_inc(s["in"], 16)
                sp.dma_start(gate[:], a["mod_gate"].partition_broadcast(P)).then_inc(s["in"], 16)
                sp.dma_start(fb[:], a["b_film_" + side].partition_broadcast(P)).then_inc(s["in"], 16)
                sp.dma_start(w[:], a["W_film_" + side].rearrange("(c p) n -> p c n", p=P)).then_inc(s["in"], 16)

            @block.vector
            def _(dve):
                dve.wait_ge(s["in"], 64)
                nc.vector.tensor_scalar(fb[:, 0:D], fb[:, 0:D], gate[:, 0:1], 1.0, ALU.mult, ALU.add)
                nc.vector.tensor_scalar(fb[:, D:2 * D], fb[:, D:2 * D], gate[:, 0:1], None, ALU.mult).then_inc(s["offset"], 1)
                dve.wait_ge(s["offset"], 1)

            @block.tensor
            def _(pe):
                pe.wait_ge(s["in"], 64)
                for c in range(VC):
                    for k in range(DC):
                        last = nc.tensor.transpose(tp[:, c, k * P:(k + 1) * P], wv[:, c, k * P:(k + 1) * P], const["ident"][:])
                last.then_inc(s["turned"], 1)
                pe.wait_ge(s["turn_copied"], 1)
                for j, (c, half) in enumerate(products):
                    if j >= 2:
                        pe.wait_ge(s["copied"], j - 1)
                    for k in range(DC):
                        last = nc.tensor.matmul(mp[j % 2][:], lhsT=wvT[:, k, c * P:(c + 1) * P],
                                                rhs=w[:, k, half * D:(half + 1) * D], start=(k == 0), stop=(k == DC - 1))
                    last.then_inc(s["multiplied"], 1)

            @block.scalar
            def _(act):
                act.wait_ge(s["turned"], 1)
                for c in range(VC):
                    last = nc.scalar.activation(wvT[:, :, c * P:(c + 1) * P], tp[:, c, :].rearrange("p (k q) -> p k q", q=P), ACT.Copy)
                last.then_inc(s["turn_copied"], 1)
                act.wait_ge(s["in"], 64)
                for j, (c, half) in enumerate(products):
                    act.wait_ge(s["multiplied"], j + 1)
                    nc.scalar.activation(wf[:, c, half * D:(half + 1) * D], mp[j % 2][:], ACT.Copy,
                                         scale=gate[:, 0:1]).then_inc(s["copied"], 1)
                act.wait_ge(s["copied"], len(products))


def modulate(nc, sem, const, a, wf, fb, X, dram):
    scope, sb, ps = phase_scope(nc)
    with scope:
        u = sb("mod_u", [P, 2, DV])
        xt = sb("mod_xt", [P, 2, D])
        uT = sb("mod_uT", [P, 2, VC, P])
        xn = sb("mod_xn", [P, 2, D])
        gain = sb("mod_gain", [P, D])
        offset = sb("mod_offset", [P, D])
        sc = sb("mod_scale", [P, D])
        sh = sb("mod_shift", [P, 2, D])
        xm = sb("mod_xm", [P, 2, D])
        stats = sb("mod_stats", [P, 6])
        mv = sb("mod_mv", [P, 2])
        rstd = sb("mod_rstd", [P, 1])
        tp = [ps(f"mod_tp{k}", [P, VC, P]) for k in range(2)]
        fp = [ps(f"mod_film{k}", [P, 2, BANK]) for k in range(2)]
        rp = [ps(f"mod_rev{k}", [P, BANK]) for k in range(2)]
        s = {n: sem("mod_" + n) for n in (
            "rows_in", "in0", "in1", "xt_read", "u_turned", "uT_ready", "film_done", "film_read", "std_wanted", "std_ready",
            "normed", "affine", "xm_ready", "reversed", "X_ready", "passed")}

        with nc.Block() as block:
            @block.sync
            def _(sp):
                sp.dma_start(gain[:], a["g_norm_in"].partition_broadcast(P)).then_inc(s["rows_in"], 16)
                sp.dma_start(offset[:], a["b_norm_in"].partition_broadcast(P)).then_inc(s["rows_in"], 16)
                with sp.Fori(0, TILES // 2) as i:
                    for b in range(2):
                        n = 2 * i + b
                        sp.wait_ge(s["xt_read"], n + 1)
                        sp.dma_start(xt[:, b], dram["xt"][bass.ts(n, P), :]).then_inc(s[f"in{b}"], 16)
                        sp.wait_ge(s["u_turned"], n + 1)
                        sp.dma_start(u[:, b], dram["u"][bass.ts(n, P), :]).then_inc(s[f"in{b}"], 16)

            @block.gpsimd
            def _(pool):
                pool.wait_ge(s["rows_in"], 32)
                with pool.Fori(0, TILES // 2) as i:
                    for b in range(2):
                        pool.wait_ge(s["normed"], 2 * i + b + 1)
                        nc.gpsimd.tensor_tensor(xn[:, b], xn[:, b], gain[:], ALU.mult)
                        pool.drain()
                        nc.gpsimd.tensor_tensor(xn[:, b], xn[:, b], offset[:], ALU.add).then_inc(s["affine"], 1)

            @block.vector
            def _(dve):
                dve.sem_inc(s["xt_read"], 2)

                def normalise(m, b):
                    n = 2 * m + b
                    dve.wait_ge(s[f"in{b}"], 32 * (m + 1))
                    nc.vector.bn_stats(stats[:], xt[:, b, :])
                    dve.drain()
                    nc.vector.bn_aggr(mv[:], stats[:]).then_inc(s["std_wanted"], 1)
                    dve.wait_ge(s["std_ready"], n + 1)
                    nc.vector.reciprocal(rstd[:], rstd[:])
                    dve.drain()
                    nc.vector.tensor_scalar(xn[:, b], xt[:, b], mv[:, 0:1], rstd[:, 0:1], ALU.subtract, ALU.mult).then_inc(s["normed"], 1)
                    dve.drain()
                    dve.sem_inc(s["xt_read"], 1)

                def film(m, b):
                    n = 2 * m + b
                    dve.drain()
                    dve.wait_ge(s["film_done"], n + 1)
                    nc.vector.tensor_tensor(sc[:], fp[b][:, 0, :], fb[:, 0:D], ALU.add)
                    nc.vector.tensor_tensor(sh[:, b], fp[b][:, 1, :], fb[:, D:2 * D], ALU.add).then_inc(s["film_read"], 1)
                    dve.drain()
                    dve.wait_ge(s["affine"], n + 1)
                    nc.vector.tensor_tensor(sc[:], xn[:, b], sc[:], ALU.mult)
                    dve.drain()
                    dve.wait_ge(s["reversed"], n + 1)
                    nc.vector.tensor_tensor(xm[:, b], sc[:], sh[:, b], ALU.add).then_inc(s["xm_ready"], 1)

                normalise(0, 0)
                with dve.Fori(0, TILES // 2 - 1) as i:
                    for b in range(2):
                        normalise(*after(i, b))
                        film(i, b)
                normalise(TILES // 2 - 1, 1)
                film(TILES // 2 - 1, 0)
                film(TILES // 2 - 1, 1)

            @block.scalar
            def _(act):
                act.sem_inc(s["X_ready"], 2)

                def root(m, b):
                    act.wait_ge(s["std_wanted"], 2 * m + b + 1)
                    nc.scalar.activation(rstd[:], mv[:, 1:2], ACT.Sqrt, bias=const["eps"][:, 0:1]).then_inc(s["std_ready"], 1)

                def copy_u(m, b):
                    act.wait_ge(s["u_turned"], 2 * m + b + 3)
                    nc.scalar.activation(uT[:, b], tp[b][:], ACT.Copy).then_inc(s["uT_ready"], 1)

                def copy_x(m, b):
                    n = 2 * m + b
                    act.wait_ge(s["reversed"], n + 3)
                    act.sem_inc(s["passed"], 1)
                    nc.scalar.activation(X[:, bass.ds(n, 1), :], rp[b][:].unsqueeze(1), ACT.Copy).then_inc(s["X_ready"], 1)

                root(0, 0)
                copy_u(0, 0)
                root(0, 1)
                copy_u(0, 1)
                with act.Fori(0, TILES // 2 - 1) as i:
                    for b in range(2):
                        root(i + 1, b)
                        copy_u(i + 1, b)
                        copy_x(i, b)
                copy_x(TILES // 2 - 1, 0)
                copy_x(TILES // 2 - 1, 1)
                act.wait_ge(s["X_ready"], TILES + 2)

            @block.tensor
            def _(pe):
                pe.sem_inc(s["u_turned"], 2)
                pe.sem_inc(s["reversed"], 2)

                def turn_u(m, b):
                    pe.wait_ge(s[f"in{b}"], 32 * (m + 1))
                    for c in range(VC):
                        last = nc.tensor.transpose(tp[b][:, c, :], u[:, b, c * P:(c + 1) * P], const["ident"][:])
                    last.then_inc(s["u_turned"], 1)

                def film(m, b):
                    n = 2 * m + b
                    pe.wait_ge(s["uT_ready"], n + 1)
                    pe.wait_ge(s["film_read"], n + 1)
                    for half in range(2):
                        for c in range(VC):
                            last = nc.tensor.matmul(fp[b][:, half, :], lhsT=uT[:, b, c, :], rhs=wf[:, c, half * D:(half + 1) * D],
                                                    start=(c == 0), stop=(c == VC - 1))
                    last.then_inc(s["film_done"], 1)

                def reverse(m, b):
                    n = 2 * m + b
                    pe.wait_ge(s["xm_ready"], n + 1)
                    pe.wait_ge(s["X_ready"], n + 1)
                    nc.tensor.matmul(rp[b][:], lhsT=const["anti"][:], rhs=xm[:, b], start=True, stop=True).then_inc(s["reversed"], 1)

                pe.sem_inc(s["film_read"], 2)
                turn_u(0, 0)
                turn_u(0, 1)
                film(0, 0)
                with pe.Fori(0, TILES // 2 - 1) as i:
                    for b in range(2):
                        turn_u(i + 1, b)
                        film(*after(i, b))
                        reverse(i, b)
                film(TILES // 2 - 1, 1)
                reverse(TILES // 2 - 1, 0)
                reverse(TILES // 2 - 1, 1)


LOG2E = 1.0 / math.log(2.0)
LN2_HIGH = 0.693359375
LN2_LOW = math.log(2.0) - LN2_HIGH
HALF_PI = [1.5703125, 4.837512969970703125e-4, 7.54978995489188216e-8]
EXP_TERMS = [1.0 / math.factorial(k) for k in range(7, 0, -1)]
SIN_TERMS = [1.0 / 362880, -1.0 / 5040, 1.0 / 120, -1.0 / 6]
COS_TERMS = [-1.0 / 3628800, 1.0 / 40320, -1.0 / 720, 1.0 / 24, -0.5]
LEVELS = 7
PAIRS = D // 2
CHUNKS = TILES
GROUP = 64
KROW = 2 * P


def s4d_scalars(nc, sem, const, a, W, root, kcoef, K0):
    scope, sb, ps = phase_scope(nc)
    with scope:
        raw = sb("ss_raw", [P, 4, DC, NS])
        ldt = sb("ss_ldt", [1, D])
        skip = sb("ss_skip", [GROUP, D // GROUP])
        sc = sb("ss_sc", [P, 5, PAIRS])
        wide = {n: sb("ss_" + n, [P, 2, PAIRS]) for n in ("x", "t", "r", "p", "z", "sin", "cos", "m", "o", "b1", "b2", "mag")}
        whole = sb("ss_whole", [P, 2, PAIRS], I32)
        t = [sb(f"ss_t{k}", [P, PAIRS]) for k in range(8)]
        pin = ps("ss_pin", [P, 3, 2, PAIRS])
        kp = ps("ss_kp", [GROUP, D // GROUP])
        s = {n: sem("ss_" + n) for n in ("in", "spread", "sc_ready", "root_wanted", "root_ready", "done", "k0_done", "k0_ready")}
        names = ("A_re", "A_im", "C_re", "C_im")

        with nc.Block() as block:
            @block.sync
            def _(sp):
                for j, name in enumerate(names):
                    sp.dma_start(raw[:, j], a[name].rearrange("(c p) n -> p c n", p=P)).then_inc(s["in"], 16)
                sp.dma_start(ldt[:], a["log_dt"].unsqueeze(0)).then_inc(s["in"], 16)
                sp.dma_start(skip[:], a["D_skip"].rearrange("(g p) -> p g", p=GROUP), allow_slow_non_contiguous=True).then_inc(s["in"], 16)

            @block.tensor
            def _(pe):
                pe.wait_ge(s["in"], 16 * 6)
                for e in range(2):
                    at = slice(NS * e, NS * (e + 1))
                    for j in range(4):
                        for c in range(DC):
                            nc.tensor.matmul(pin[at, j // 2, j % 2, NS * c:NS * (c + 1)], lhsT=raw[:, j, c, :],
                                             rhs=const["ident"][:, e::2], start=True, stop=True)
                    last = nc.tensor.matmul(pin[at, 2, 0, :], lhsT=const["one_row"][0:1, 0:NS], rhs=ldt[0:1, e::2],
                                            start=True, stop=True)
                last.then_inc(s["spread"], 1)
                pe.wait_ge(s["done"], 1)
                for g in range(D // GROUP):
                    last = nc.tensor.matmul(kp[:, g:g + 1], lhsT=kcoef[:, 0, g * GROUP // 2:(g + 1) * GROUP // 2, :].rearrange("p k e -> p (k e)"),
                                            rhs=const["ones"][:, 0:1], start=True, stop=True)
                last.then_inc(s["k0_done"], 1)

            @block.scalar
            def _(act):
                act.wait_ge(s["spread"], 1)
                for j in range(5):
                    last = nc.scalar.activation(sc[:, j], pin[:, j // 2, j % 2, :], ACT.Copy)
                last.then_inc(s["sc_ready"], 1)
                for k in range(2):
                    act.wait_ge(s["root_wanted"], k + 1)
                    nc.scalar.activation(t[1][:], t[0][:], ACT.Sqrt).then_inc(s["root_ready"], 1)

            @block.vector
            def _(dve):
                v = nc.vector

                def then(*_):
                    dve.drain()

                def exp(out, x):
                    tt, r, p = wide["t"][:, 0:1], wide["r"][:, 0:1], wide["p"][:, 0:1]
                    n = whole[:, 0:1]
                    then(v.tensor_scalar(x, x, -87.0, 88.0, ALU.max, ALU.min))
                    then(v.tensor_scalar(tt, x, LOG2E, ROUND, ALU.mult, ALU.add))
                    then(v.tensor_scalar(tt, tt, ROUND, None, ALU.subtract))
                    then(v.scalar_tensor_tensor(r, tt, -LN2_HIGH, x, ALU.mult, ALU.add))
                    then(v.scalar_tensor_tensor(r, tt, -LN2_LOW, r, ALU.mult, ALU.add),
                         v.tensor_scalar(x, tt, 127.0, 2.0 ** 23, ALU.add, ALU.mult))
                    then(v.tensor_scalar(p, r, EXP_TERMS[0], None, ALU.mult),
                         v.tensor_copy(n, x))
                    for c in EXP_TERMS[1:]:
                        then(v.scalar_tensor_tensor(p, p, c, r, ALU.add, ALU.mult))
                    then(v.scalar_tensor_tensor(out, p, 1.0, n.bitcast(F32), ALU.add, ALU.mult))

                def sin_cos():
                    x, tt, r, p, z, m, o = (wide[n][:] for n in ("x", "t", "r", "p", "z", "m", "o"))
                    sin, cos, b1, b2 = (wide[n][:] for n in ("sin", "cos", "b1", "b2"))
                    then(v.tensor_scalar(tt, x, 2.0 / math.pi, ROUND, ALU.mult, ALU.add))
                    then(v.tensor_scalar(tt, tt, ROUND, None, ALU.subtract))
                    then(v.scalar_tensor_tensor(r, tt, -HALF_PI[0], x, ALU.mult, ALU.add),
                         v.tensor_scalar(m, tt, 0.25, -0.375, ALU.mult, ALU.add))
                    then(v.scalar_tensor_tensor(r, tt, -HALF_PI[1], r, ALU.mult, ALU.add),
                         v.tensor_scalar(o, m, ROUND, ROUND, ALU.add, ALU.subtract))
                    then(v.scalar_tensor_tensor(r, tt, -HALF_PI[2], r, ALU.mult, ALU.add),
                         v.scalar_tensor_tensor(m, o, -4.0, tt, ALU.mult, ALU.add))
                    then(v.tensor_tensor(z, r, r, ALU.mult), v.tensor_scalar(o, m, 0.5, -0.25, ALU.mult, ALU.add))
                    then(v.tensor_scalar(p, z, SIN_TERMS[0], None, ALU.mult), v.tensor_scalar(cos, z, COS_TERMS[0], None, ALU.mult),
                         v.tensor_scalar(b1, o, ROUND, ROUND, ALU.add, ALU.subtract))
                    for k in range(1, 5):
                        if k < 4:
                            v.scalar_tensor_tensor(p, p, SIN_TERMS[k], z, ALU.add, ALU.mult)
                        then(v.scalar_tensor_tensor(cos, cos, COS_TERMS[k], z, ALU.add, ALU.mult))
                    then(v.scalar_tensor_tensor(sin, p, 1.0, r, ALU.add, ALU.mult),
                         v.tensor_scalar(cos, cos, 1.0, None, ALU.add),
                         v.scalar_tensor_tensor(o, b1, -2.0, m, ALU.mult, ALU.add))
                    then(v.scalar_tensor_tensor(b1, o, 1.0, sin, ALU.subtract, ALU.mult), v.tensor_tensor(b2, o, cos, ALU.mult),
                         v.scalar_tensor_tensor(p, o, 1.0, cos, ALU.subtract, ALU.mult), v.tensor_tensor(z, o, sin, ALU.mult),
                         v.tensor_scalar(x, m, 1.5, -2.0, ALU.is_ge, ALU.mult),
                         v.tensor_scalar(tt, m, 1.5, None, ALU.subtract))
                    then(v.tensor_tensor(b2, b2, b1, ALU.subtract), v.tensor_tensor(z, z, p, ALU.subtract),
                         v.scalar_tensor_tensor(tt, tt, -1.0, tt, ALU.mult, ALU.max))
                    then(v.tensor_scalar(tt, tt, 1.0, 2.0, ALU.is_ge, ALU.mult))
                    then(v.scalar_tensor_tensor(sin, x, 1.0, b2, ALU.add, ALU.mult),
                         v.scalar_tensor_tensor(cos, tt, 1.0, z, ALU.subtract, ALU.mult))

                def square_root(out, k):
                    dve.sem_inc(s["root_wanted"], 1)
                    dve.wait_ge(s["root_ready"], k + 1)
                    then(v.tensor_scalar(t[2][:], t[1][:], 1e-30, None, ALU.max))
                    then(v.reciprocal(t[2][:], t[2][:]))
                    then(v.tensor_tensor(t[2][:], t[2][:], t[0][:], ALU.mult))
                    then(v.tensor_tensor(t[2][:], t[2][:], t[1][:], ALU.add))
                    then(v.tensor_scalar(out, t[2][:], 0.5, None, ALU.mult))

                dve.wait_ge(s["sc_ready"], 1)
                are, aim, cre, cim = (sc[:, j] for j in range(4))
                x = wide["x"]
                dt = sc[:, 4]
                exp(dt.unsqueeze(1), dt.unsqueeze(1))
                then(v.tensor_tensor(x[:, 0], dt, are, ALU.mult))
                then(v.tensor_scalar(x[:, 1], x[:, 0], float(P), None, ALU.mult))
                exp(wide["mag"][:, 0:1], x[:, 0:1])
                exp(wide["mag"][:, 1:2], x[:, 1:2])
                then(v.tensor_tensor(x[:, 0], dt, aim, ALU.mult))
                then(v.tensor_scalar(x[:, 1], x[:, 0], float(P), None, ALU.mult))
                sin_cos()
                for k, level in ((0, 0), (1, LEVELS)):
                    v.tensor_tensor(W[:, level, 0], wide["mag"][:, k], wide["cos"][:, k], ALU.mult)
                    v.tensor_tensor(W[:, level, 1], wide["mag"][:, k], wide["sin"][:, k], ALU.mult)
                dve.drain()
                for level in range(1, LEVELS):
                    re, im = W[:, level - 1, 0], W[:, level - 1, 1]
                    then(v.tensor_tensor(t[0][:], re, im, ALU.subtract), v.tensor_tensor(t[1][:], re, im, ALU.add))
                    then(v.tensor_tensor(W[:, level, 0], t[0][:], t[1][:], ALU.mult),
                         v.scalar_tensor_tensor(W[:, level, 1], re, 2.0, im, ALU.mult, ALU.mult))
                wr, wi = W[:, 0, 0], W[:, 0, 1]
                then(v.tensor_scalar(t[0][:], wr, 1.0, None, ALU.subtract))
                then(v.tensor_tensor(t[1][:], cre, t[0][:], ALU.mult), v.tensor_tensor(t[2][:], cim, wi, ALU.mult),
                     v.tensor_tensor(t[3][:], cre, wi, ALU.mult), v.tensor_tensor(t[4][:], cim, t[0][:], ALU.mult),
                     v.tensor_tensor(t[5][:], are, are, ALU.mult), v.tensor_tensor(t[6][:], aim, aim, ALU.mult))
                then(v.tensor_tensor(t[1][:], t[1][:], t[2][:], ALU.subtract), v.tensor_tensor(t[3][:], t[3][:], t[4][:], ALU.add),
                     v.tensor_tensor(t[5][:], t[5][:], t[6][:], ALU.add))
                then(v.reciprocal(t[5][:], t[5][:]), v.tensor_tensor(t[0][:], t[1][:], are, ALU.mult),
                     v.tensor_tensor(t[2][:], t[3][:], aim, ALU.mult), v.tensor_tensor(t[4][:], t[3][:], are, ALU.mult),
                     v.tensor_tensor(t[6][:], t[1][:], aim, ALU.mult))
                then(v.tensor_tensor(t[0][:], t[0][:], t[2][:], ALU.add), v.tensor_tensor(t[4][:], t[4][:], t[6][:], ALU.subtract))
                dr, di = t[6], t[7]
                then(v.scalar_tensor_tensor(dr[:], t[0][:], 2.0, t[5][:], ALU.mult, ALU.mult),
                     v.scalar_tensor_tensor(di[:], t[4][:], 2.0, t[5][:], ALU.mult, ALU.mult))
                v.memset(kcoef[:], 0.0)
                dve.drain()
                for e in range(2):
                    at = slice(NS * e, NS * (e + 1))
                    last = v.tensor_copy(kcoef[at, 0, :, e], dr[at, :])
                last.then_inc(s["done"], 1)
                kr, ki, big = sc[:, 0], sc[:, 1], sc[:, 2]
                then(v.tensor_tensor(t[0][:], dr[:], wr, ALU.mult), v.tensor_tensor(t[1][:], di[:], wi, ALU.mult),
                     v.tensor_tensor(t[2][:], dr[:], wi, ALU.mult), v.tensor_tensor(t[3][:], di[:], wr, ALU.mult))
                then(v.tensor_tensor(kr, t[0][:], t[1][:], ALU.subtract), v.tensor_tensor(ki, t[2][:], t[3][:], ALU.add))
                then(v.tensor_tensor(t[0][:], kr, kr, ALU.mult), v.tensor_tensor(t[1][:], ki, ki, ALU.mult))
                then(v.tensor_tensor(t[0][:], t[0][:], t[1][:], ALU.add))
                square_root(big, 0)
                then(v.scalar_tensor_tensor(t[3][:], kr, -1.0, kr, ALU.mult, ALU.max))
                then(v.tensor_tensor(t[0][:], big, t[3][:], ALU.add))
                then(v.tensor_scalar(t[0][:], t[0][:], 0.5, None, ALU.mult))
                square_root(big, 1)
                then(v.tensor_scalar(t[0][:], big, 1e-30, 2.0, ALU.max, ALU.mult))
                then(v.reciprocal(t[0][:], t[0][:]), v.tensor_scalar(t[3][:], ki, 0.0, 2.0, ALU.is_ge, ALU.mult),
                     v.tensor_scalar(t[4][:], kr, 0.0, None, ALU.is_ge))
                then(v.tensor_tensor(t[0][:], t[0][:], ki, ALU.mult), v.scalar_tensor_tensor(t[3][:], t[3][:], 1.0, big, ALU.subtract, ALU.mult))
                then(v.scalar_tensor_tensor(t[1][:], t[0][:], -1.0, t[0][:], ALU.mult, ALU.max), v.tensor_tensor(t[2][:], t[4][:], big, ALU.mult),
                     v.tensor_tensor(t[5][:], t[4][:], t[0][:], ALU.mult), v.scalar_tensor_tensor(t[3][:], t[4][:], 1.0, t[3][:], ALU.subtract, ALU.mult))
                then(v.scalar_tensor_tensor(t[1][:], t[4][:], 1.0, t[1][:], ALU.subtract, ALU.mult))
                dve.wait_ge(s["k0_done"], 1)
                then(v.tensor_tensor(root[:, 0], t[2][:], t[1][:], ALU.subtract), v.tensor_tensor(root[:, 1], t[5][:], t[3][:], ALU.subtract),
                     v.tensor_tensor(K0[:], kp[:], skip[:], ALU.add))
                for e in range(2):
                    at = slice(NS * e, NS * (e + 1))
                    v.tensor_copy(kcoef[at, 0, :, e], root[at, 0])
                    v.tensor_scalar(kcoef[at, 1, :, e], root[at, 1], -1.0, None, ALU.mult)
                dve.drain()


def s4d(nc, sem, const, W, root, kcoef, K0, X, dram):
    scope, sb, ps = phase_scope(nc)
    GP = GROUP // 2
    GROUPS = PAIRS // GP
    HALF = GP // 2
    PIECE = 16
    OUT = 32
    BLOCK = 8
    with scope:
        Q = sb("s4_Q", [P, 2, 2, GP, P])
        S = sb("s4_S", [P, 2, 2, CHUNKS, GP])
        Xg = sb("s4_Xg", [P, 2, 2 * GP, CHUNKS])
        QT = sb("s4_QT", [P, 2, 4, P])
        M = {e: sb(f"s4_M_{e}", [P, 2, 2, HALF, PIECE]) for e in ("dve", "pool")}
        R = sb("s4_R", [P, 2, 2, GP])
        hankel = sb("s4_hankel", [P, 2, BLOCK, P])
        Ksum = sb("s4_Ksum", [P, 2 * GP])
        Krow = sb("s4_Krow", [2 * GP, KROW])
        tp = [ps(f"s4_tp{k}", [P, 4, P]) for k in range(2)]
        up = ps("s4_up", [P, 2, 8, CHUNKS])
        yp = [ps(f"s4_yp{k}", [P, 2, OUT // 2, CHUNKS]) for k in range(2)]
        kbank = ps("s4_kp", [P, BANK])
        ksp, ktp = kbank[:, 0:2 * GP], kbank[0:2 * GP, P:2 * P]
        s = {n: sem("s4_" + n) for n in (
            "Q_dve", "Q_pool", "turned", "QT_ready", "U_done", "U_copied", "K_done", "K_copied", "K_turned", "K_row",
            "K_stored", "h_in0", "h_in1", "h_used", "passed", "Xg_ready", "S_ready", "y_done", "y_copied", "row_set")}
        YG = 2 * GP // OUT
        HG = 2 * GP // BLOCK
        TG = GP // 2
        UG = GP // 8

        def table(eng, dve_like, m, b, half, temp, done):
            g = 2 * m + b
            pairs = slice(half * HALF, (half + 1) * HALF)
            eng.wait_ge(s["y_done"], YG * g + half + 1)
            for part in range(2):
                last = dve_like.tensor_copy(Q[:, b, part, pairs, 0], root[:, part, bass.ds(GP * g + half * HALF, HALF)])
            eng.drain()
            for level in range(LEVELS):
                n = 1 << level
                pieces = [(lo, min(lo + PIECE, n)) for lo in range(0, n, PIECE)]
                for lo, hi in pieces:
                    w = hi - lo
                    old = Q[:, b, :, pairs, lo:hi]
                    for part in range(2):
                        factor = W[:, level, part, bass.ds(GP * g + half * HALF, HALF)]
                        dve_like.tensor_tensor(temp[:, part, :, :, 0:w], old,
                                               factor.unsqueeze(1).unsqueeze(3).broadcast_to([P, 2, HALF, w]), ALU.mult)
                    eng.drain()
                    dve_like.tensor_tensor(Q[:, b, 0, pairs, n + lo:n + hi], temp[:, 0, 0, :, 0:w], temp[:, 1, 1, :, 0:w], ALU.subtract)
                    last = dve_like.tensor_tensor(Q[:, b, 1, pairs, n + lo:n + hi], temp[:, 0, 1, :, 0:w], temp[:, 1, 0, :, 0:w], ALU.add)
                    if level < LEVELS - 1 or hi < n:
                        eng.drain()
            last.then_inc(done, 1)

        with nc.Block() as block:
            @block.sync
            def _(sp):
                with sp.Fori(0, GROUPS // 2) as i:
                    for b in range(2):
                        g = 2 * i + b
                        sp.wait_ge(s["K_row"], g + 2)
                        sp.dma_start(dram["K"][bass.ts(g, 2 * GP), :], Krow[:]).then_inc(s["K_stored"], 16)
                        sp.wait_ge(s["K_stored"], 16 * (g + 1))
                        for j in range(HG):
                            sp.wait_ge(s["h_used"], HG * g + j + 1)
                            rows = dram["K"][bass.ds(2 * GP * g + j * BLOCK, BLOCK), :]
                            skewed = bass.AP(tensor=rows.tensor, offset=rows.offset, ap=[[1, P], [KROW, BLOCK], [1, P]])
                            sp.dma_start(hankel[:, j % 2], skewed).then_inc(s[f"h_in{j % 2}"], 16)

            @block.gpsimd
            def _(pool):
                nc.gpsimd.memset(Krow[:], 0.0).then_inc(s["row_set"], 1)
                with pool.Fori(0, GROUPS // 2) as i:
                    for b in range(2):
                        table(pool, nc.gpsimd, i, b, 1, M["pool"], s["Q_pool"])

            @block.vector
            def _(dve):
                def carry(m, b):
                    g = 2 * m + b
                    dve.wait_ge(s["U_copied"], UG * (g + 1) + 1)
                    factor = [W[:, LEVELS, part, bass.ds(GP * g, GP)].unsqueeze(1).broadcast_to([P, 2, GP]) for part in range(2)]
                    nc.vector.tensor_scalar(S[:, b, 1, 0, :], S[:, b, 1, 0, :], -1.0, None, ALU.mult)
                    dve.drain()
                    for c in range(1, CHUNKS - 1):
                        nc.vector.tensor_tensor(R[:, 0], S[:, b, :, c - 1, :], factor[0], ALU.mult)
                        nc.vector.tensor_tensor(R[:, 1], S[:, b, :, c - 1, :], factor[1], ALU.mult)
                        dve.drain()
                        nc.vector.tensor_tensor(R[:, 0, 0], R[:, 0, 0], R[:, 1, 1], ALU.add)
                        nc.vector.tensor_tensor(R[:, 0, 1], R[:, 0, 1], R[:, 1, 0], ALU.subtract)
                        dve.drain()
                        nc.vector.tensor_tensor(S[:, b, 0, c, :], S[:, b, 0, c, :], R[:, 0, 0], ALU.add)
                        last = nc.vector.tensor_tensor(S[:, b, 1, c, :], R[:, 0, 1], S[:, b, 1, c, :], ALU.subtract)
                        if c < CHUNKS - 2:
                            dve.drain()
                    last.then_inc(s["S_ready"], 1)

                dve.sem_inc(s["y_done"], 2 * YG)
                table(dve, nc.vector, 0, 0, 0, M["dve"], s["Q_dve"])
                with dve.Fori(0, GROUPS // 2 - 1) as i:
                    for b in range(2):
                        table(dve, nc.vector, *after(i, b), 0, M["dve"], s["Q_dve"])
                        carry(i, b)
                table(dve, nc.vector, GROUPS // 2 - 1, 1, 0, M["dve"], s["Q_dve"])
                carry(GROUPS // 2 - 1, 0)
                carry(GROUPS // 2 - 1, 1)

            @block.scalar
            def _(act):
                act.sem_inc(s["QT_ready"], 2)
                act.sem_inc(s["U_copied"], 1)
                act.sem_inc(s["y_copied"], 2)
                act.wait_ge(s["row_set"], 1)

                def gather(m, b, first=False):
                    g = 2 * m + b
                    act.wait_ge(s["y_done"], YG * (g + 1))
                    act.sem_inc(s["passed"], 1)
                    nc.scalar.activation(Xg[:, b].rearrange("p d c -> p c d"), X[:, :, bass.ds(2 * GP * g, 2 * GP)],
                                         ACT.Copy).then_inc(s["Xg_ready"], 1)
                    for j in range(TG):
                        act.wait_ge(s["turned"], TG * g + j + 1)
                        nc.scalar.activation(QT[:, j % 2], tp[j % 2][:], ACT.Copy).then_inc(s["QT_ready"], 1)
                        if j % 4 == 1 and j > 4:
                            copy_states(g, b, j // 4 - 1)
                    copy_states(g, b, UG - 1)
                    act.wait_ge(s["K_done"], g + 1)
                    nc.scalar.activation(Ksum[:], ksp, ACT.Copy).then_inc(s["K_copied"], 1)
                    act.wait_ge(s["K_turned"], g + 1)
                    if not first:
                        act.wait_ge(s["K_stored"], 16 * g)
                        act.sem_inc(s["passed"], 1)
                    nc.scalar.activation(Krow[:, P - 1:P], K0[:, bass.ds(g, 1)], ACT.Copy)
                    nc.scalar.activation(Krow[:, P:KROW - 1], ktp[:, 0:P - 1], ACT.Copy).then_inc(s["K_row"], 1)

                def copy_states(g, b, k):
                    act.wait_ge(s["U_done"], UG * g + k + 1)
                    nc.scalar.activation(S[:, b, :, :, 8 * k:8 * k + 8].rearrange("p r c k -> p r k c"), up[:], ACT.Copy).then_inc(s["U_copied"], 1)

                def spread(m, b):
                    g = 2 * m + b
                    for j in range(YG):
                        act.wait_ge(s["y_done"], YG * g + j + 1 + 2 * YG)
                        act.sem_inc(s["passed"], 1)
                        for e in range(2):
                            last = nc.scalar.activation(X[:].rearrange("p c (k e) -> p e c k", e=2)[:, e, :, bass.ds(GP * g + j * OUT // 2, OUT // 2)],
                                                        yp[j % 2][:, e].rearrange("p k c -> p c k"), ACT.Copy)
                        last.then_inc(s["y_copied"], 1)

                gather(0, 0, first=True)
                with act.Fori(0, GROUPS // 2 - 1) as i:
                    for b in range(2):
                        gather(*after(i, b))
                        spread(i, b)
                gather(GROUPS // 2 - 1, 1)
                spread(GROUPS // 2 - 1, 0)
                spread(GROUPS // 2 - 1, 1)
                act.wait_ge(s["y_copied"], YG * GROUPS + 2)

            @block.tensor
            def _(pe):
                pe.sem_inc(s["h_used"], 2)

                def gather(m, b):
                    g = 2 * m + b

                    def turn_tables(j):
                        if j == 0:
                            pe.wait_ge(s["Q_dve"], g + 1)
                        if j == TG // 2:
                            pe.wait_ge(s["Q_pool"], g + 1)
                        pe.wait_ge(s["QT_ready"], TG * g + j + 1)
                        for k in range(2):
                            for part in range(2):
                                last = nc.tensor.transpose(tp[j % 2][:, 2 * k + part, :], Q[:, b, part, 2 * j + k, :], const["ident"][:])
                        last.then_inc(s["turned"], 1)
                        for k in range(2):
                            pair = 2 * j + k
                            for part in range(2):
                                last = nc.tensor.matmul(ksp[:, 2 * pair:2 * pair + 2], lhsT=Q[:, b, part, pair, :],
                                                        rhs=kcoef[:, part, bass.ds(GP * g + pair, 1), :].rearrange("p k e -> p (k e)"),
                                                        start=(part == 0), stop=(part == 1))
                        if j == TG - 1:
                            last.then_inc(s["K_done"], 1)

                    pe.wait_ge(s["K_row"], g + 1)
                    turn_tables(0)
                    for j in range(TG):
                        if j < TG - 1:
                            turn_tables(j + 1)
                        pe.wait_ge(s["QT_ready"], TG * g + j + 3)
                        if j == 0:
                            pe.wait_ge(s["Xg_ready"], g + 1)
                        if j % 4 == 0:
                            pe.wait_ge(s["U_copied"], UG * g + j // 4 + 1)
                        for k in range(2):
                            pair = 2 * j + k
                            for part in range(2):
                                for e in range(2):
                                    last = nc.tensor.matmul(up[NS * e:NS * (e + 1), part, pair % 8, :],
                                                            lhsT=QT[:, j % 2, 2 * k + part, NS * e:NS * (e + 1)],
                                                            rhs=Xg[:, b, 2 * pair + e, :],
                                                            start=True, stop=True)
                        if j % 4 == 3:
                            last.then_inc(s["U_done"], 1)
                    pe.wait_ge(s["K_copied"], g + 1)
                    pe.sem_inc(s["passed"], 1)
                    nc.tensor.transpose(ktp, Ksum[:], const["ident"][:]).then_inc(s["K_turned"], 1)

                def spread(m, b):
                    g = 2 * m + b
                    pe.wait_ge(s["S_ready"], g + 1)
                    for j in range(YG):
                        pe.wait_ge(s["y_copied"], YG * g + j + 1)
                        for d in range(OUT):
                            pair, e = (j * OUT + d) // 2, d % 2
                            load = (j * OUT + d) // BLOCK
                            if d % BLOCK == 0:
                                pe.wait_ge(s[f"h_in{load % 2}"], 16 * (HG // 2 * g + load // 2 + 1))
                            last = nc.tensor.matmul(yp[j % 2][:, e, d // 2, :], lhsT=hankel[:, load % 2, d % BLOCK, :],
                                                    rhs=Xg[:, b, j * OUT + d, :],
                                                    start=True, stop=False)
                            if d % BLOCK == BLOCK - 1:
                                last.then_inc(s["h_used"], 1)
                            for part in range(2):
                                last = nc.tensor.matmul(yp[j % 2][:, e, d // 2, 1:CHUNKS], lhsT=Q[NS * e:NS * (e + 1), b, part, pair, :],
                                                        rhs=S[NS * e:NS * (e + 1), b, part, 0:CHUNKS - 1, pair], start=False, stop=(part == 1))
                        last.then_inc(s["y_done"], 1)

                pe.sem_inc(s["K_row"], 1)
                gather(0, 0)
                with pe.Fori(0, GROUPS // 2 - 1) as i:
                    for b in range(2):
                        gather(*after(i, b))
                        spread(i, b)
                gather(GROUPS // 2 - 1, 1)
                spread(GROUPS // 2 - 1, 0)
                spread(GROUPS // 2 - 1, 1)


LEAST = 1e-5
LEVEL = 127.0


def fold_ffn(nc, sem, const, a, W1, W2, b1):
    scope, sb, ps = phase_scope(nc)
    with scope:
        gain = sb("fold_gain", [P, DC])
        offset = sb("fold_offset", [P, DC])
        bp = ps("fold_bp", [P, HID // P])
        s = {n: sem("fold_" + n) for n in ("in", "offset_done", "gained")}

        with nc.Block() as block:
            @block.sync
            def _(sp):
                sp.dma_start(W1[:], a["W1"].rearrange("(c p) n -> p c n", p=P)).then_inc(s["in"], 16)
                sp.dma_start(gain[:], a["g_ffn"].rearrange("(c p) -> p c", p=P), allow_slow_non_contiguous=True).then_inc(s["in"], 16)
                sp.dma_start(offset[:], a["b_ffn"].rearrange("(c p) -> p c", p=P), allow_slow_non_contiguous=True).then_inc(s["in"], 16)
                sp.dma_start(b1[:], a["b1"].rearrange("(f p) -> p f", p=P), allow_slow_non_contiguous=True).then_inc(s["in"], 16)
                sp.dma_start(W2[:], a["W2"].rearrange("(f p) n -> p f n", p=P)).then_inc(s["in"], 16)

            @block.tensor
            def _(pe):
                pe.wait_ge(s["in"], 16 * 5)
                for f in range(HID // P):
                    for c in range(DC):
                        last = nc.tensor.matmul(bp[:, f:f + 1], lhsT=W1[:, c, f * P:(f + 1) * P], rhs=offset[:, c:c + 1],
                                                start=(c == 0), stop=(c == DC - 1))
                last.then_inc(s["offset_done"], 1)

            @block.vector
            def _(dve):
                dve.wait_ge(s["offset_done"], 1)
                nc.vector.tensor_tensor(b1[:], bp[:], b1[:], ALU.add).then_inc(s["gained"], 1)
                for c in range(DC):
                    nc.vector.tensor_scalar(W1[:, c, :], W1[:, c, :], gain[:, c:c + 1], None, ALU.mult).then_inc(s["gained"], 1)
                dve.wait_ge(s["gained"], DC + 1)


def feed_forward(nc, sem, const, a, wf, fb, W1, W2, b1, Y, qstep, dram):
    scope, sb, ps = phase_scope(nc)
    QUADS = TILES // QUAD
    FC = HID // P
    TURN_U, FILM, TURN_Q = (2, 5, 8, 11), (3, 6, 9, 12), (7, 10, 13, 14)
    with scope:
        rows = {n: sb("ff_" + n, [P, D]) for n in ("b2", "g_norm_out", "b_norm_out")}
        u = sb("ff_u", [P, DV])
        uT = sb("ff_uT", [P, VC, P])
        xt = sb("ff_xt", [P, 2, QUAD, D])
        x = sb("ff_x", [P, QUAD, D])
        h = sb("ff_h", [P, 2, D])
        hT = sb("ff_hT", [P, DC, QUAD * P])
        act_out = sb("ff_gelu", [P, 2, QUAD * P])
        sc = sb("ff_scale", [P, D])
        q = sb("ff_q", [P, QUAD, D], BF16)
        qT = sb("ff_qT", [P, DC, QUAD * P], BF16)
        stats = {n: sb("ff_stats_" + n, [P, QUAD, 6]) for n in ("sum", "out", "x")}
        mv = {n: sb("ff_mv_" + n, [P, QUAD, 2]) for n in ("sum", "out", "x")}
        rstd = {n: sb("ff_rstd_" + n, [P, QUAD]) for n in ("sum", "out", "x")}
        most = sb("ff_most", [P, QUAD])
        steps = sb("ff_steps", [P, QUAD])
        zero = sb("ff_zero", [P, DC], BF16)
        fl = [ps(f"ff_fl{k}", [P, BANK]) for k in range(2)]
        fp = [ps(f"ff_fp{k}", [P, BANK]) for k in range(2)]
        acc = ps("ff_acc", [P, QUAD, BANK])
        s = {n: sem("ff_" + n) for n in (
            "rows_in", "u_in", "xt_in0", "xt_in1", "x_in", "u_turned", "uT_ready", "film_done", "film_read", "factors", "modulated",
            "sum_wanted", "sum_ready", "h_ready", "h_turned", "hT_ready", "hidden", "gelu_done", "acc_done", "acc_read",
            "out_wanted", "out_ready", "out_normed", "x_ready", "xb_ready", "x_wanted", "x_root", "x_read", "q_ready", "q_turned", "qT_ready",
            "xt_free", "qT_stored", "x_stored", "biased", "edges", "passed")}

        with nc.Block() as block:
            @block.sync
            def _(sp):
                for n in rows:
                    sp.dma_start(rows[n][:], a[n].partition_broadcast(P)).then_inc(s["rows_in"], 16)
                xt_q = dram["xt"].rearrange("(q k p) d -> q p k d", k=QUAD, p=P)
                x_q = a["x"].rearrange("(q k p) d -> q p k d", k=QUAD, p=P)
                x2_q = dram["x2"].rearrange("(q k p) d -> q p k d", k=QUAD, p=P)

                def load_u(m, b, tiles):
                    for k in tiles:
                        n = QUAD * (2 * m + b) + k
                        sp.wait_ge(s["u_turned"], n + 1)
                        sp.sem_inc(s["passed"], 1)
                        sp.dma_start(u[:], dram["u"][bass.ts(n, P), :]).then_inc(s["u_in"], 16)

                def load_xt(m, b):
                    g = 2 * m + b
                    sp.wait_ge(s["xt_free"], g + 1)
                    sp.sem_inc(s["passed"], 1)
                    sp.dma_start(xt[:, b], xt_q[g, :, :, :]).then_inc(s[f"xt_in{b}"], 16)

                def load_back(m, b, first=False):
                    g = 2 * m + b
                    if not first:
                        sp.wait_ge(s["x_read"], g)
                        sp.sem_inc(s["passed"], 1)
                        sp.wait_ge(s["x_stored"], 16 * g)
                        sp.sem_inc(s["passed"], 1)
                    sp.dma_start(x[:], x_q[g, :, :, :]).then_inc(s["x_in"], 16)

                def store(m, b):
                    g = 2 * m + b
                    sp.wait_ge(s["x_ready"], QUAD * (g + 1))
                    sp.sem_inc(s["passed"], 1)
                    sp.dma_start(x2_q[g, :, :, :], x[:]).then_inc(s["x_stored"], 16)

                load_xt(0, 0)
                load_u(0, 0, range(QUAD))
                load_xt(0, 1)
                load_back(0, 0, first=True)
                load_u(0, 1, range(QUAD))
                with sp.Fori(0, QUADS // 2 - 1) as i:
                    for b in range(2):
                        load_u(i + 1, b, (0,))
                        store(i, b)
                        load_back(*after(i, b))
                        load_xt(i + 1, b)
                        load_u(i + 1, b, range(1, QUAD))
                store(QUADS // 2 - 1, 0)
                load_back(QUADS // 2 - 1, 1)
                store(QUADS // 2 - 1, 1)
                sp.wait_ge(s["x_stored"], 16 * QUADS)

            @block.gpsimd
            def _(pool):
                nc.gpsimd.memset(zero[:], 0.0).then_inc(s["edges"], 1)
                pool.wait_ge(s["rows_in"], 16 * 3)

                def front(m, b):
                    g = 2 * m + b
                    for k in range(QUAD):
                        n = QUAD * g + k
                        pool.wait_ge(s["factors"], n + 1)
                        pool.sem_inc(s["passed"], 1)
                        nc.gpsimd.tensor_tensor(sc[:].unsqueeze(1), Y[:, bass.ds(n, 1), :], sc[:].unsqueeze(1), ALU.mult)
                        nc.gpsimd.tensor_tensor(xt[:, b, k], xt[:, b, k], fb[:, D:2 * D], ALU.add)
                        pool.drain()
                        nc.gpsimd.tensor_tensor(xt[:, b, k], xt[:, b, k], sc[:], ALU.add).then_inc(s["modulated"], 1)

                def bias(m, b):
                    g = 2 * m + b
                    for k in range(QUAD):
                        pool.wait_ge(s["h_ready"], QUAD * g + k + 1)
                        pool.sem_inc(s["passed"], 1)
                        last = nc.gpsimd.tensor_tensor(xt[:, b, k], xt[:, b, k], rows["b2"][:], ALU.add)
                    last.then_inc(s["biased"], 1)

                def back(m, b):
                    g = 2 * m + b
                    pool.wait_ge(s["x_in"], 16 * (g + 1))
                    pool.sem_inc(s["passed"], 1)
                    nc.gpsimd.tensor_tensor(x[:], x[:], rows["b_norm_out"][:].unsqueeze(1).broadcast_to([P, QUAD, D]), ALU.add)
                    for k in range(QUAD):
                        pool.wait_ge(s["out_normed"], QUAD * g + k + 1)
                        pool.sem_inc(s["passed"], 1)
                        nc.gpsimd.tensor_tensor(xt[:, b, k], xt[:, b, k], rows["g_norm_out"][:], ALU.mult)
                        pool.drain()
                        nc.gpsimd.tensor_tensor(x[:, k], x[:, k], xt[:, b, k], ALU.add).then_inc(s["x_ready"], 1)

                front(0, 0)
                bias(0, 0)
                front(0, 1)
                bias(0, 1)
                with pool.Fori(0, QUADS // 2 - 1) as i:
                    for b in range(2):
                        back(i, b)
                        front(i + 1, b)
                        bias(i + 1, b)
                back(QUADS // 2 - 1, 0)
                back(QUADS // 2 - 1, 1)

            @block.vector
            def _(dve):
                def front(m, b):
                    g = 2 * m + b
                    for k in range(QUAD):
                        n = QUAD * g + k
                        dve.wait_ge(s["film_done"], n + 1)
                        dve.sem_inc(s["passed"], 1)
                        if k:
                            dve.wait_ge(s["modulated"], n)
                        else:
                            dve.wait_ge(s[f"xt_in{b}"], 16 * (m + 1))
                        nc.vector.tensor_tensor(sc[:], fl[0][:], fb[:, 0:D], ALU.add)
                        nc.vector.tensor_tensor(xt[:, b, k], fl[1][:], xt[:, b, k], ALU.add)
                        dve.drain()
                        dve.sem_inc(s["film_read"], 1)
                        dve.sem_inc(s["factors"], 1)
                    for k in range(QUAD):
                        dve.wait_ge(s["modulated"], QUAD * g + k + 1)
                        dve.sem_inc(s["passed"], 1)
                        nc.vector.bn_stats(stats["sum"][:, k, :], xt[:, b, k, :])
                    norm_factors("sum", g)
                    for k in range(QUAD):
                        dve.wait_ge(s["h_turned"], QUAD * g + k + 1)
                        nc.vector.tensor_scalar(h[:, k % 2], xt[:, b, k], mv["sum"][:, k, 0:1], rstd["sum"][:, k:k + 1],
                                                ALU.subtract, ALU.mult).then_inc(s["h_ready"], 1)

                def norm_factors(name, g):
                    dve.drain()
                    for k in range(QUAD):
                        last = nc.vector.bn_aggr(mv[name][:, k, :], stats[name][:, k, :])
                    last.then_inc(s[name + "_wanted"], 1)
                    dve.wait_ge(s[{"sum": "sum_ready", "out": "out_ready", "x": "x_root"}[name]], g + 1)
                    nc.vector.reciprocal(rstd[name][:], rstd[name][:])
                    dve.drain()

                def back(m, b):
                    g = 2 * m + b
                    dve.wait_ge(s["acc_done"], g + 1)
                    dve.sem_inc(s["passed"], 1)
                    dve.wait_ge(s["biased"], g + 1)
                    for k in range(QUAD):
                        last = nc.vector.tensor_tensor(xt[:, b, k], acc[:, k, :], xt[:, b, k], ALU.add)
                    last.then_inc(s["acc_read"], 1)
                    dve.drain()
                    for k in range(QUAD):
                        nc.vector.bn_stats(stats["out"][:, k, :], xt[:, b, k, :])
                    norm_factors("out", g)
                    for k in range(QUAD):
                        nc.vector.tensor_scalar(xt[:, b, k], xt[:, b, k], mv["out"][:, k, 0:1], rstd["out"][:, k:k + 1],
                                                ALU.subtract, ALU.mult).then_inc(s["out_normed"], 1)
                    for k in range(QUAD):
                        dve.wait_ge(s["x_ready"], QUAD * g + k + 1)
                        dve.sem_inc(s["passed"], 1)
                        nc.vector.bn_stats(stats["x"][:, k, :], x[:, k, :])
                    norm_factors("x", g)
                    for k in range(QUAD):
                        nc.vector.tensor_scalar(xt[:, b, k], x[:, k], mv["x"][:, k, 0:1], rstd["x"][:, k:k + 1], ALU.subtract, ALU.mult)
                    dve.drain()
                    dve.sem_inc(s["x_read"], 1)
                    nc.vector.tensor_reduce(most[:], xt[:, b], AX.X, ALU.max, apply_absolute_value=True)
                    dve.drain()
                    nc.vector.tensor_scalar(most[:], most[:], LEAST, None, ALU.max)
                    dve.drain()
                    nc.vector.tensor_scalar(qstep[:, bass.ds(QUAD * g, QUAD)], most[:], 1.0 / LEVEL, None, ALU.mult)
                    nc.vector.reciprocal(steps[:], most[:])
                    dve.drain()
                    nc.vector.tensor_scalar(steps[:], steps[:], LEVEL, None, ALU.mult)
                    dve.drain()
                    for k in range(QUAD):
                        nc.vector.tensor_scalar(xt[:, b, k], xt[:, b, k], steps[:, k:k + 1], ROUND, ALU.mult, ALU.add)
                    dve.drain()
                    for k in range(QUAD):
                        dve.wait_ge(s["q_turned"], QUAD * g + k + 1)
                        nc.vector.tensor_scalar(q[:, k], xt[:, b, k], ROUND, None, ALU.subtract).then_inc(s["q_ready"], 1)
                    dve.drain()
                    dve.sem_inc(s["xt_free"], 1)

                dve.sem_inc(s["xt_free"], 2)
                front(0, 0)
                front(0, 1)
                with dve.Fori(0, QUADS // 2 - 1) as i:
                    for b in range(2):
                        back(i, b)
                        front(i + 1, b)
                back(QUADS // 2 - 1, 0)
                back(QUADS // 2 - 1, 1)

            @block.scalar
            def _(act):
                act.sem_inc(s["qT_ready"], 1)
                act.sem_inc(s["hT_ready"], 2)
                act.wait_ge(s["edges"], 1)
                act.dma_start(dram["qT"][:, :, 0], zero[:], allow_slow_non_contiguous=True).then_inc(s["qT_stored"], 16)
                act.dma_start(dram["qT"][:, :, T + 1], zero[:], allow_slow_non_contiguous=True).then_inc(s["qT_stored"], 16)

                def root(name, ready, g):
                    act.wait_ge(s[name + "_wanted"], g + 1)
                    nc.scalar.activation(rstd[name][:], mv[name][:, :, 1], ACT.Sqrt, bias=const["eps"][:, 0:1]).then_inc(s[ready], 1)

                def copy_u(g, k):
                    act.wait_ge(s["u_turned"], QUAD * g + k + 1 + 1)
                    nc.scalar.activation(uT[:], fl[0][:, 0:DV].rearrange("p (c t) -> p c t", t=P), ACT.Copy).then_inc(s["uT_ready"], 1)

                def copy_h(g, k):
                    act.wait_ge(s["h_turned"], QUAD * g + k + 1 + 2)
                    nc.scalar.activation(hT[:, :, k * P:(k + 1) * P], fl[k % 2][:].rearrange("p (c t) -> p c t", t=P), ACT.Copy).then_inc(s["hT_ready"], 1)

                def copy_q(g, k):
                    if k == 0:
                        act.wait_ge(s["qT_stored"], 16 * (g + 2))
                        act.sem_inc(s["passed"], 1)
                    act.wait_ge(s["q_turned"], QUAD * (g + 1) + k + 1)
                    nc.scalar.activation(qT[:, :, k * P:(k + 1) * P], fl[1][:].bitcast(BF16)[:, 0:D].rearrange("p (c t) -> p c t", t=P),
                                         ACT.Copy).then_inc(s["qT_ready"], 1)
                    if k == QUAD - 1:
                        act.wait_ge(s["qT_ready"], QUAD * (g + 1) + 1)
                        act.sem_inc(s["passed"], 1)
                        act.dma_start(dram["qT"][:, :, bass.ds(QUAD * P * g + 1, QUAD * P)], qT[:]).then_inc(s["qT_stored"], 16)

                def turn(m, b, front=True, back=True):
                    g = 2 * m + b
                    old, new = 2 * before(m, b)[0] + before(m, b)[1], 2 * after(m, b)[0] + after(m, b)[1]
                    for k in range(QUAD):
                        copy_h(g, k)
                    for f in range(FC):
                        if front and f in TURN_U:
                            copy_u(new, TURN_U.index(f))
                        if back and f in TURN_Q:
                            copy_q(old, TURN_Q.index(f))
                        act.wait_ge(s["hidden"], FC * g + f + 1)
                        nc.scalar.activation(act_out[:, f % 2], fp[f % 2][:], ACT.Gelu, bias=b1[:, f:f + 1]).then_inc(s["gelu_done"], 1)
                        if back and f == 1:
                            root("out", "out_ready", old)
                        if back and f == 4:
                            root("x", "x_root", old)
                        if front and f == FC - 2:
                            root("sum", "sum_ready", new)

                for k in range(QUAD):
                    copy_u(0, k)
                root("sum", "sum_ready", 0)
                turn(0, 0, back=False)
                with act.Fori(0, QUADS // 2 - 1) as i:
                    turn(i, 1)
                    turn(i + 1, 0)
                turn(QUADS // 2 - 1, 1, front=False)
                root("out", "out_ready", QUADS - 1)
                root("x", "x_root", QUADS - 1)
                for k in range(QUAD):
                    copy_q(QUADS - 1, k)
                act.wait_ge(s["qT_stored"], 16 * (QUADS + 2))

            @block.tensor
            def _(pe):
                pe.sem_inc(s["u_turned"], 1)
                pe.sem_inc(s["h_turned"], 2)
                pe.sem_inc(s["q_turned"], QUAD)
                pe.sem_inc(s["gelu_done"], 2)

                def turn_u(m, b, k):
                    n = QUAD * (2 * m + b) + k
                    pe.wait_ge(s["u_in"], 16 * (n + 1))
                    if k:
                        pe.wait_ge(s["film_read"], n)
                    for c in range(VC):
                        last = nc.tensor.transpose(fl[0][:, c * P:(c + 1) * P], u[:, c * P:(c + 1) * P], const["ident"][:])
                    last.then_inc(s["u_turned"], 1)

                def film(m, b, k):
                    n = QUAD * (2 * m + b) + k
                    pe.wait_ge(s["uT_ready"], n + 1)
                    for half in range(2):
                        for c in range(VC):
                            last = nc.tensor.matmul(fl[half][:], lhsT=uT[:, c, :], rhs=wf[:, c, half * D:(half + 1) * D],
                                                    start=(c == 0), stop=(c == VC - 1))
                    last.then_inc(s["film_done"], 1)

                def turn_h(m, b, k):
                    n = QUAD * (2 * m + b) + k
                    pe.wait_ge(s["h_ready"], n + 1)
                    if k >= 2:
                        pe.wait_ge(s["hT_ready"], n + 1)
                    for c in range(DC):
                        last = nc.tensor.transpose(fl[k % 2][:, c * P:(c + 1) * P], h[:, k % 2, c * P:(c + 1) * P], const["ident"][:])
                    last.then_inc(s["h_turned"], 1)

                def turn_q(m, b, k):
                    n = QUAD * (2 * m + b) + k
                    pe.wait_ge(s["q_ready"], n + 1)
                    for c in range(DC):
                        last = nc.tensor.transpose(fl[1][:].bitcast(BF16)[:, c * P:(c + 1) * P], q[:, k, c * P:(c + 1) * P],
                                                   const["ident_bf"][:])
                    last.then_inc(s["q_turned"], 1)

                def second(m, b, f):
                    g = 2 * m + b
                    pe.wait_ge(s["gelu_done"], FC * g + f + 1 + 2)
                    if f == 0:
                        pe.wait_ge(s["acc_read"], g + 1)
                    for k in range(QUAD):
                        last = nc.tensor.matmul(acc[:, k, :], lhsT=act_out[:, f % 2, k * P:(k + 1) * P], rhs=W2[:, f, :],
                                                start=(f == 0), stop=(f == FC - 1))
                    if f == FC - 1:
                        last.then_inc(s["acc_done"], 1)

                def turn(m, b, front=True, back=True):
                    g = 2 * m + b
                    for k in range(QUAD):
                        if k == 1 and back:
                            pe.wait_ge(s["qT_ready"], QUAD * (g - 1) + 1)
                        turn_h(m, b, k)
                    pe.wait_ge(s["hT_ready"], QUAD * (g + 1) + 2)
                    for f in range(FC):
                        pe.wait_ge(s["gelu_done"], FC * g + f + 1)
                        for c in range(DC):
                            last = nc.tensor.matmul(fp[f % 2][:], lhsT=W1[:, c, f * P:(f + 1) * P], rhs=hT[:, c, :],
                                                    start=(c == 0), stop=(c == DC - 1))
                        last.then_inc(s["hidden"], 1)
                        if f:
                            second(m, b, f - 1)
                        if front and f in TURN_U:
                            turn_u(*after(m, b), TURN_U.index(f))
                        if front and f in FILM:
                            k = FILM.index(f)
                            if back and f > TURN_Q[0]:
                                done = sum(t < f for t in TURN_Q)
                                pe.wait_ge(s["qT_ready"], QUAD * (2 * before(m, b)[0] + before(m, b)[1]) + done + 1)
                            film(*after(m, b), k)
                        if back and f in TURN_Q:
                            k = TURN_Q.index(f)
                            done = sum(t < f for t in FILM)
                            if front:
                                pe.wait_ge(s["film_read"], QUAD * (2 * after(m, b)[0] + after(m, b)[1]) + done)
                            if k:
                                pe.wait_ge(s["qT_ready"], QUAD * (2 * before(m, b)[0] + before(m, b)[1]) + k + 1)
                            turn_q(*before(m, b), k)
                    second(m, b, FC - 1)

                pe.sem_inc(s["acc_read"], 1)
                pe.wait_ge(s["rows_in"], 16)
                for k in range(QUAD):
                    turn_u(0, 0, k)
                    film(0, 0, k)
                pe.wait_ge(s["film_read"], QUAD)
                turn(0, 0, back=False)
                with pe.Fori(0, QUADS // 2 - 1) as i:
                    turn(i, 1)
                    turn(i + 1, 0)
                turn(QUADS // 2 - 1, 1, front=False)
                for k in range(QUAD):
                    if k:
                        pe.wait_ge(s["qT_ready"], QUAD * (QUADS - 1) + k + 1)
                    turn_q(QUADS // 2 - 1, 1, k)


def quantise_weights(nc, sem, const, a, W1q, W2q, mean, qstep, rowstep):
    scope, sb, ps = phase_scope(nc)
    FC = HID // P
    with scope:
        w1 = sb("qw_w1", [P, FC, D])
        w2 = sb("qw_w2", [P, DC, HID])
        w1b = sb("qw_w1b", [P, FC, D], BF16)
        w2b = sb("qw_w2b", [P, DC, HID], BF16)
        part = sb("qw_part", [P, FC + DC])
        sums = sb("qw_sums", [P, 2])
        inverse = sb("qw_inverse", [P, 2])
        every = sb("qw_every", [P, P])
        diag = sb("qw_diag", [P, 2, QUAD, P])
        total = ps("qw_total", [P, 2])
        tp = [ps(f"qw_tp{k}", [P, 2 * BANK], BF16) for k in range(2)]
        rp = [ps(f"qw_rp{k}", [P, BANK]) for k in range(2)]
        s = {n: sem("qw_" + n) for n in ("in0", "in1", "summed", "totalled", "quantised", "turned", "copied", "diag_ready", "spread", "rows_copied",
                                         "mean_ready")}

        with nc.Block() as block:
            @block.sync
            def _(sp):
                sp.dma_start(w1[:], a["ffn_w1"].rearrange("(f p) d -> p f d", p=P)).then_inc(s["in0"], 16)
                sp.dma_start(w2[:], a["ffn_w2"].rearrange("(c p) f -> p c f", p=P)).then_inc(s["in1"], 16)

            @block.vector
            def _(dve):
                nc.vector.memset(every[:], 1.0)
                nc.vector.memset(rowstep[:, 0:1], 0.0)
                nc.vector.memset(rowstep[:, T + 1:T + 2], 0.0)
                dve.wait_ge(s["in0"], 16)
                nc.vector.tensor_reduce(part[:, 0:FC], w1[:], AX.X, ALU.add, apply_absolute_value=True)
                dve.wait_ge(s["in1"], 16)
                nc.vector.tensor_reduce(part[:, FC:FC + DC], w2[:], AX.X, ALU.add, apply_absolute_value=True)
                dve.drain()
                nc.vector.tensor_reduce(sums[:, 0:1], part[:, 0:FC], AX.X, ALU.add)
                nc.vector.tensor_reduce(sums[:, 1:2], part[:, FC:FC + DC], AX.X, ALU.add).then_inc(s["summed"], 1)
                dve.wait_ge(s["totalled"], 1)
                nc.vector.tensor_scalar(mean[:], total[:], 1.0 / (HID * D), LEAST, ALU.mult, ALU.max)
                dve.drain()
                nc.vector.reciprocal(inverse[:], mean[:]).then_inc(s["mean_ready"], 1)
                for q in range(TILES // QUAD):
                    if q >= 2:
                        dve.wait_ge(s["spread"], q - 1)
                    for k in range(QUAD):
                        n = QUAD * q + k
                        last = nc.vector.tensor_scalar(diag[:, q % 2, k, :], const["ident"][:], qstep[:, n:n + 1], None, ALU.mult)
                    last.then_inc(s["diag_ready"], 1)
                dve.drain()
                for j, (w, wb) in enumerate(((w1, w1b), (w2, w2b))):
                    nc.vector.tensor_scalar(w[:], w[:], inverse[:, j:j + 1], 1.0, ALU.mult, ALU.min)
                    dve.drain()
                    nc.vector.tensor_scalar(w[:], w[:], -1.0, ROUND, ALU.max, ALU.add)
                    dve.drain()
                    nc.vector.tensor_scalar(wb[:], w[:], ROUND, None, ALU.subtract).then_inc(s["quantised"], 1)

            @block.tensor
            def _(pe):
                pe.wait_ge(s["summed"], 1)
                nc.tensor.matmul(total[:], lhsT=every[:], rhs=sums[:], start=True, stop=True).then_inc(s["totalled"], 1)
                for q in range(TILES // QUAD):
                    pe.wait_ge(s["diag_ready"], q + 1)
                    if q >= 2:
                        pe.wait_ge(s["rows_copied"], q - 1)
                    nc.tensor.matmul(rp[q % 2][:], lhsT=every[:], rhs=diag[:, q % 2].rearrange("p k t -> p (k t)"),
                                     start=True, stop=True).then_inc(s["spread"], 1)
                for j in range(2):
                    pe.wait_ge(s["quantised"], j + 1)
                    for f in range(FC):
                        if FC * j + f >= 2:
                            pe.wait_ge(s["copied"], FC * j + f - 1)
                        for c in range(DC):
                            piece = w1b[:, f, c * P:(c + 1) * P] if j == 0 else w2b[:, c, f * P:(f + 1) * P]
                            last = nc.tensor.transpose(tp[f % 2][:, c * P:(c + 1) * P], piece, const["ident_bf"][:])
                        last.then_inc(s["turned"], 1)

            @block.scalar
            def _(act):
                act.wait_ge(s["mean_ready"], 1)
                for q in range(TILES // QUAD):
                    act.wait_ge(s["spread"], q + 1)
                    nc.scalar.activation(rowstep[:, 1 + q * BANK:1 + (q + 1) * BANK], rp[q % 2][:], ACT.Copy,
                                         scale=mean[:, 0:1]).then_inc(s["rows_copied"], 1)
                for j in range(2):
                    for f in range(FC):
                        act.wait_ge(s["turned"], FC * j + f + 1)
                        piece = tp[f % 2][:, 0:D]
                        if j == 0:
                            last = nc.scalar.activation(W1q[:, :, f * P:(f + 1) * P], piece.rearrange("p (c f) -> p c f", f=P), ACT.Copy)
                        else:
                            last = nc.scalar.activation(W2q[:, f, :], piece, ACT.Copy)
                        last.then_inc(s["copied"], 1)
                act.wait_ge(s["copied"], 2 * FC)


def bit_feed_forward(nc, sem, const, a, W1q, W2q, mean, rowstep, dram, out):
    scope, sb, ps = phase_scope(nc)
    FC = HID // P
    BT = 2 * P
    BLOCKS = T // BT
    HALO = BT + 2
    JC = FC // 2
    with scope:
        taps = sb("bf_taps", [P, FC, 3])
        tap_bias = sb("bf_tap_bias", [P, FC])
        qin = sb("bf_qin", [P, 2, DC, HALO], BF16)
        x2 = sb("bf_x2", [P, 2, 2, D])
        hidden = sb("bf_hidden", [P, 2, 2, HALO])
        conv = sb("bf_conv", [P, 2, 2, BT])
        g = sb("bf_silu", [P, 2, FC, BT])
        gq = sb("bf_gq", [P, FC, BT], BF16)
        top = sb("bf_top", [P, BT])
        most = sb("bf_most", [P, 2])
        step = sb("bf_step", [P, 2])
        undo = sb("bf_undo", [P, 2, 2])
        diag = sb("bf_diag", [P, 2, P])
        every = sb("bf_every", [P, P])
        scale = sb("bf_scale", [P, BT])
        y = sb("bf_y", [P, 2, 2, D])
        hp = [ps(f"bf_hp{k}", [P, 2, BANK]) for k in range(2)]
        op = ps("bf_op", [P, 2, BANK])
        mp = ps("bf_mp", [P, 2, P])
        sp_ = ps("bf_sp", [P, BANK])
        s = {n: sem("bf_" + n) for n in (
            "taps_in", "q_in0", "q_in1", "x_in0", "x_in1", "every_set", "first_done", "dequantised", "tapped0", "tapped", "silu_done", "top_done",
            "top_turned", "steps_ready", "steps_spread", "scale_ready", "scaled", "quantised", "second_done", "y_ready", "stored0", "stored1", "passed",
            "block_done")}
        x2_b = dram["x2"].rearrange("(n k p) d -> n p k d", k=2, p=P)
        out_b = out.rearrange("(n k p) d -> n p k d", k=2, p=P)

        with nc.Block() as block:
            @block.sync
            def _(sp):
                sp.dma_start(taps[:], a["conv_w"].rearrange("(f p) o k -> p f (o k)", p=P), allow_slow_non_contiguous=True).then_inc(s["taps_in"], 16)
                sp.dma_start(tap_bias[:], a["conv_b"].rearrange("(f p) -> p f", p=P), allow_slow_non_contiguous=True).then_inc(s["taps_in"], 16)

                def load(m, b):
                    n = 2 * m + b
                    sp.wait_ge(s["block_done"], n + 1)
                    sp.sem_inc(s["passed"], 1)
                    sp.dma_start(qin[:, b], dram["qT"][:, :, bass.ds(BT * n, HALO)]).then_inc(s[f"q_in{b}"], 16)

                def load_x(m, b):
                    n = 2 * m + b
                    sp.wait_ge(s["y_ready"], n + 1)
                    sp.sem_inc(s["passed"], 1)
                    sp.dma_start(x2[:, b], x2_b[n, :, :, :]).then_inc(s[f"x_in{b}"], 16)

                def store(m, b):
                    n = 2 * m + b
                    sp.wait_ge(s["y_ready"], n + 1 + 2)
                    sp.sem_inc(s["passed"], 1)
                    sp.dma_start(out_b[n, :, :, :], y[:, b]).then_inc(s[f"stored{b}"], 16)

                load(0, 0)
                load(0, 1)
                load_x(0, 0)
                load_x(0, 1)
                with sp.Fori(0, BLOCKS // 2 - 1) as i:
                    for b in range(2):
                        load(i + 1, b)
                        store(i, b)
                        load_x(i + 1, b)
                store(BLOCKS // 2 - 1, 0)
                store(BLOCKS // 2 - 1, 1)
                for b in range(2):
                    sp.wait_ge(s[f"stored{b}"], 16 * (BLOCKS // 2 + 1))

            @block.gpsimd
            def _(pool):
                nc.gpsimd.memset(every[:], 1.0).then_inc(s["every_set"], 1)

                def scaling(m, b):
                    n = 2 * m + b
                    pool.wait_ge(s["scale_ready"], n + 1)
                    pool.sem_inc(s["passed"], 1)
                    for k in range(2):
                        part = g[:, b, k * JC:(k + 1) * JC, :]
                        nc.gpsimd.tensor_tensor(part, part, scale[:].unsqueeze(1).broadcast_to([P, JC, BT]),
                                                ALU.mult).then_inc(s["scaled"], 1)

                with pool.Fori(0, BLOCKS // 2) as i:
                    for b in range(2):
                        scaling(i, b)

            @block.vector
            def _(dve):
                dve.sem_inc(s["y_ready"], 2)
                dve.sem_inc(s["dequantised"], 2)

                def dequantise(m, b, j):
                    n = 2 * m + b
                    dve.drain()
                    dve.wait_ge(s["first_done"], JC * n + j + 1)
                    nc.vector.tensor_tensor(hidden[:, j % 2], hp[j % 2][:, :, 0:HALO],
                                            rowstep[:, bass.ds(BT * n, HALO)].unsqueeze(1).broadcast_to([P, 2, HALO]),
                                            ALU.mult).then_inc(s["dequantised"], 1)

                def add_taps(m, b, j):
                    n = 2 * m + b
                    dve.wait_ge(s["tapped0"], JC * n + j + 1)
                    for k in range(1, 3):
                        for e in range(2):
                            last = nc.vector.scalar_tensor_tensor(conv[:, j % 2, e], hidden[:, j % 2, e, k:k + BT], taps[:, 2 * j + e, k:k + 1],
                                                                  conv[:, j % 2, e], ALU.mult, ALU.add)
                        if k == 1:
                            dve.drain()
                    last.then_inc(s["tapped"], 1)

                def largest(m, b):
                    dve.drain()
                    dve.wait_ge(s["silu_done"], JC * (2 * m + b + 1) + 2)
                    nc.vector.tensor_reduce(top[:], g[:, b].rearrange("p f t -> p t f"), AX.X, ALU.max,
                                            apply_absolute_value=True).then_inc(s["top_done"], 1)

                def steps(m, b):
                    n = 2 * m + b
                    dve.wait_ge(s["top_turned"], n + 1)
                    nc.vector.tensor_reduce(most[:], mp[:], AX.X, ALU.max)
                    dve.drain()
                    nc.vector.tensor_scalar(most[:], most[:], LEAST, None, ALU.max)
                    dve.drain()
                    nc.vector.reciprocal(step[:], most[:])
                    nc.vector.tensor_scalar(undo[:, b], most[:], mean[:, 1:2], 1.0 / LEVEL, ALU.mult, ALU.mult)
                    dve.drain()
                    nc.vector.tensor_scalar(step[:], step[:], LEVEL, None, ALU.mult)
                    dve.drain()
                    for k in range(2):
                        last = nc.vector.tensor_scalar(diag[:, k], const["ident"][:], step[:, k:k + 1], None, ALU.mult)
                    last.then_inc(s["steps_ready"], 1)

                def quantise(m, b):
                    n = 2 * m + b
                    dve.wait_ge(s["second_done"], n + 1)
                    dve.sem_inc(s["passed"], 1)
                    for k in range(2):
                        dve.wait_ge(s["scaled"], 2 * n + k + 1)
                        last = nc.vector.tensor_scalar(gq[:, k * JC:(k + 1) * JC, :], g[:, b, k * JC:(k + 1) * JC, :], ROUND, ROUND,
                                                       ALU.add, ALU.subtract)
                    last.then_inc(s["quantised"], 1)

                def finish(m, b):
                    n = 2 * m + b
                    dve.wait_ge(s["second_done"], n + 2)
                    dve.sem_inc(s["passed"], 1)
                    dve.wait_ge(s[f"stored{b}"], 16 * (m + 1))
                    dve.sem_inc(s["passed"], 1)
                    dve.wait_ge(s[f"x_in{b}"], 16 * (m + 1))
                    for k in range(2):
                        last = nc.vector.scalar_tensor_tensor(y[:, b, k], op[:, k, :], undo[:, b, k:k + 1], x2[:, b, k], ALU.mult, ALU.add)
                    last.then_inc(s["y_ready"], 1)

                def turn(m, b, first=False):
                    dequantise(m, b, 0)
                    dequantise(m, b, 1)
                    if not first:
                        largest(*before(m, b))
                    for j in range(JC):
                        add_taps(m, b, j)
                        if j + 2 < JC:
                            dequantise(m, b, j + 2)
                        if not first and j == 2:
                            steps(*before(m, b))
                        if not first and j == 6:
                            quantise(*before(m, b))
                    if not first:
                        finish(*before(m, b))

                turn(0, 0, first=True)
                with dve.Fori(0, BLOCKS // 2 - 1) as i:
                    turn(i, 1)
                    turn(i + 1, 0)
                turn(BLOCKS // 2 - 1, 1)
                largest(BLOCKS // 2 - 1, 1)
                steps(BLOCKS // 2 - 1, 1)
                quantise(BLOCKS // 2 - 1, 1)
                finish(BLOCKS // 2 - 1, 1)

            @block.scalar
            def _(act):
                act.sem_inc(s["silu_done"], 2)
                act.sem_inc(s["stored0"], 16)
                act.sem_inc(s["stored1"], 16)
                act.wait_ge(s["taps_in"], 32)

                def first_tap(m, b, j):
                    n = 2 * m + b
                    act.wait_ge(s["silu_done"], JC * n + j + 1)
                    act.sem_inc(s["passed"], 1)
                    act.wait_ge(s["dequantised"], JC * n + j + 1 + 2)
                    for e in range(2):
                        f = 2 * j + e
                        last = nc.scalar.activation(conv[:, j % 2, e], hidden[:, j % 2, e, 0:BT], ACT.Identity, bias=tap_bias[:, f:f + 1],
                                                    scale=taps[:, f, 0:1])
                    last.then_inc(s["tapped0"], 1)

                def silu(m, b, j):
                    n = 2 * m + b
                    act.wait_ge(s["tapped"], JC * n + j + 1)
                    if j == 0:
                        act.sem_inc(s["passed"], 1)
                        act.wait_ge(s["quantised"], n + 1)
                    nc.scalar.activation(g[:, b, 2 * j:2 * j + 2, :], conv[:, j % 2], ACT.Silu).then_inc(s["silu_done"], 1)

                def copy_scale(m, b):
                    act.wait_ge(s["steps_spread"], 2 * m + b + 1)
                    nc.scalar.activation(scale[:], sp_[:, 0:BT], ACT.Copy).then_inc(s["scale_ready"], 1)

                def turn(m, b, first=False):
                    first_tap(m, b, 0)
                    for j in range(JC):
                        if j + 1 < JC:
                            first_tap(m, b, j + 1)
                        silu(m, b, j)
                        if not first and j == 3:
                            copy_scale(*before(m, b))

                act.sem_inc(s["quantised"], 2)
                turn(0, 0, first=True)
                with act.Fori(0, BLOCKS // 2 - 1) as i:
                    turn(i, 1)
                    turn(i + 1, 0)
                turn(BLOCKS // 2 - 1, 1)
                copy_scale(BLOCKS // 2 - 1, 1)

            @block.tensor
            def _(pe):
                pe.sem_inc(s["block_done"], 2)
                pe.sem_inc(s["second_done"], 1)
                pe.wait_ge(s["every_set"], 1)

                def first(m, b, pairs):
                    n = 2 * m + b
                    for j in pairs:
                        if j == 0:
                            pe.wait_ge(s[f"q_in{b}"], 16 * (m + 1))
                        pe.wait_ge(s["dequantised"], JC * n + j + 1)
                        for e in range(2):
                            f = 2 * j + e
                            for c in range(DC):
                                last = nc.tensor.matmul(hp[j % 2][:, e, 0:HALO], lhsT=W1q[:, c, f * P:(f + 1) * P], rhs=qin[:, b, c, :],
                                                        start=(c == 0), stop=(c == DC - 1))
                        last.then_inc(s["first_done"], 1)

                def turn_top(m, b):
                    pe.wait_ge(s["top_done"], 2 * m + b + 1)
                    for t in range(2):
                        last = nc.tensor.transpose(mp[:, t, :], top[:, t * P:(t + 1) * P], const["ident"][:])
                    last.then_inc(s["top_turned"], 1)

                def spread_steps(m, b):
                    pe.wait_ge(s["steps_ready"], 2 * m + b + 1)
                    nc.tensor.matmul(sp_[:, 0:BT], lhsT=every[:], rhs=diag[:].rearrange("p k t -> p (k t)"), start=True,
                                     stop=True).then_inc(s["steps_spread"], 1)

                def second(m, b):
                    n = 2 * m + b
                    pe.wait_ge(s["quantised"], n + 3)
                    pe.sem_inc(s["passed"], 1)
                    pe.wait_ge(s["y_ready"], n + 2)
                    for k in range(2):
                        for f in range(FC):
                            last = nc.tensor.matmul(op[:, k, :], lhsT=gq[:, f, k * P:(k + 1) * P], rhs=W2q[:, f, :],
                                                    start=(f == 0), stop=(f == FC - 1))
                    last.then_inc(s["second_done"], 1)

                def turn(m, b, start=False):
                    first(m, b, range(0, 4))
                    if not start:
                        turn_top(*before(m, b))
                    first(m, b, range(4, 6))
                    if not start:
                        spread_steps(*before(m, b))
                    first(m, b, range(6, JC))
                    pe.drain()
                    pe.sem_inc(s["block_done"], 1)
                    if not start:
                        second(*before(m, b))

                turn(0, 0, start=True)
                with pe.Fori(0, BLOCKS // 2 - 1) as i:
                    turn(i, 1)
                    turn(i + 1, 0)
                turn(BLOCKS // 2 - 1, 1)
                turn_top(BLOCKS // 2 - 1, 1)
                spread_steps(BLOCKS // 2 - 1, 1)
                second(BLOCKS // 2 - 1, 1)


def xattn_ffn(nc, a, out):
    whole = ExitStack()
    with whole:
        held = []

        def sem(name):
            held.append(nc.alloc_semaphore(name=name))
            return held[-1]

        def end_phase():
            nc.clear_and_free_semaphores(held)
            nc.all_engine_barrier()
            held.clear()

        def sb(name, shape, dt=F32):
            return whole.enter_context(nc.sbuf_tensor(name, shape, dt))

        dram = {
            "xt": nc.dram_tensor("scratch_xt", (T, D), F32).ap(),
            "qt": nc.dram_tensor("scratch_qt", (2, P, T), F32).ap(),
            "u": nc.dram_tensor("scratch_u", (T, DV), F32).ap(),
            "x2": nc.dram_tensor("scratch_x2", (T, D), F32).ap(),
            "qT": nc.dram_tensor("scratch_qT", (P, DC, T + 2), BF16).ap(),
            "K": nc.dram_tensor("scratch_K", (D, KROW), F32).ap(),
        }
        const = {"ident": sb("ident", [P, P]), "anti": sb("anti", [P, P]), "ones": sb("ones", [P, 1]),
                 "one_row": sb("one_row", [1, P]), "eps": sb("eps", [P, 1]),
                 "ident_bf": sb("ident_bf", [P, P], BF16)}
        ident_made = sem("ident_made")
        with nc.Block() as block:
            @block.gpsimd
            def _(pool):
                nc.gpsimd.memset(const["ident"][:], 0.0)
                nc.gpsimd.memset(const["anti"][:], 0.0)
                nc.gpsimd.memset(const["ones"][:], 1.0)
                nc.gpsimd.memset(const["one_row"][:], 1.0)
                nc.gpsimd.memset(const["eps"][:], EPS)
                pool.drain()
                nc.gpsimd.affine_select(out=const["ident"][:], in_=const["ident"][:], compare_op=ALU.not_equal, fill=1.0,
                                        base=0, pattern=[[-1, P]], channel_multiplier=1).then_inc(ident_made, 1)
                nc.gpsimd.affine_select(out=const["anti"][:], in_=const["anti"][:], compare_op=ALU.not_equal, fill=1.0,
                                        base=1 - P, pattern=[[1, P]], channel_multiplier=1).then_inc(ident_made, 1)
                pool.wait_ge(ident_made, 2)
                nc.gpsimd.tensor_copy(const["ident_bf"][:], const["ident"][:]).then_inc(ident_made, 1)
                pool.wait_ge(ident_made, 3)
        qstep = sb("qstep", [P, TILES])
        keys = ExitStack()
        with keys:
            KT = keys.enter_context(nc.sbuf_tensor("KT", [P, H // 2, G], F32R))
            prepare_attention(nc, sem, const, a, KT, dram)
            end_phase()
            attention(nc, sem, const, a, KT, dram)
            end_phase()
        rows = ExitStack()
        with rows:
            X = rows.enter_context(nc.sbuf_tensor("X", [P, TILES, D], F32))
            film = ExitStack()
            with film:
                wf = film.enter_context(nc.sbuf_tensor("wf_in", [P, VC, 2 * D], F32))
                fb = film.enter_context(nc.sbuf_tensor("fb_in", [P, 2 * D], F32))
                film_weights(nc, sem, const, a, "in", wf, fb)
                end_phase()
                modulate(nc, sem, const, a, wf, fb, X, dram)
                end_phase()
            layer = ExitStack()
            with layer:
                W = layer.enter_context(nc.sbuf_tensor("W", [P, LEVELS + 1, 2, PAIRS], F32))
                root = layer.enter_context(nc.sbuf_tensor("root", [P, 2, PAIRS], F32))
                kcoef = layer.enter_context(nc.sbuf_tensor("kcoef", [P, 2, PAIRS, 2], F32))
                K0 = layer.enter_context(nc.sbuf_tensor("K0", [GROUP, D // GROUP], F32))
                s4d_scalars(nc, sem, const, a, W, root, kcoef, K0)
                end_phase()
                s4d(nc, sem, const, W, root, kcoef, K0, X, dram)
                end_phase()
            second = ExitStack()
            with second:
                W1 = second.enter_context(nc.sbuf_tensor("W1", [P, DC, HID], F32))
                W2 = second.enter_context(nc.sbuf_tensor("W2", [P, HID // P, D], F32))
                b1 = second.enter_context(nc.sbuf_tensor("b1", [P, HID // P], F32))
                wf = second.enter_context(nc.sbuf_tensor("wf_out", [P, VC, 2 * D], F32))
                fb = second.enter_context(nc.sbuf_tensor("fb_out", [P, 2 * D], F32))
                film_weights(nc, sem, const, a, "out", wf, fb)
                end_phase()
                fold_ffn(nc, sem, const, a, W1, W2, b1)
                end_phase()
                feed_forward(nc, sem, const, a, wf, fb, W1, W2, b1, X, qstep, dram)
                end_phase()
        third = ExitStack()
        with third:
            W1q = third.enter_context(nc.sbuf_tensor("W1q", [P, DC, HID], BF16))
            W2q = third.enter_context(nc.sbuf_tensor("W2q", [P, HID // P, D], BF16))
            mean = third.enter_context(nc.sbuf_tensor("mean", [P, 2], F32))
            rowstep = third.enter_context(nc.sbuf_tensor("rowstep", [P, T + 2], F32))
            quantise_weights(nc, sem, const, a, W1q, W2q, mean, qstep, rowstep)
            end_phase()
            bit_feed_forward(nc, sem, const, a, W1q, W2q, mean, rowstep, dram, out)


def kernel(**inputs):
    import concourse.bacc as bacc
    from concourse.bass_utils import run_bass_kernel_spmd

    nc = bacc.Bacc("TRN2", target_bir_lowering=False, num_devices=1)
    arrays, a = {}, {}
    for name, v in inputs.items():
        v = np.ascontiguousarray(v)
        if v.dtype == np.bool_:
            v = v.view(np.uint8)
        if v.ndim == 0:
            v = v.reshape(1)
        elif v.ndim > 1 and v.shape[0] == 1:
            v = v.reshape(v.shape[1:])
        arrays["in_" + name] = v
        short = {"ctx_768": "ctx", "mask_BxS_bf1": "mask1", "mask_BxS2_bf1": "mask2", "L0_ffn_w1": "ffn_w1", "L0_ffn_w2": "ffn_w2"}
        a[short.get(name, name.replace("L0_xattn_", "").replace("L0_ffn_", ""))] = nc.dram_tensor(
            "in_" + name, v.shape, mybir.dt.from_np(v.dtype), kind="ExternalInput").ap()
    out = nc.dram_tensor("out", (T, D), F32, kind="ExternalOutput").ap()
    xattn_ffn(nc, a, out)
    r = run_bass_kernel_spmd(nc, [arrays], core_ids=[0])
    return r.results[0]["out"].reshape(1, T, D)
```

```python
import math
from contextlib import ExitStack

import numpy as np

import concourse.bass as bass
from concourse import mybir

F32 = mybir.dt.float32
BF16 = mybir.dt.bfloat16
F32R = mybir.dt.float32r
I32 = mybir.dt.int32
U8 = mybir.dt.uint8
ALU = mybir.AluOpType
ACT = mybir.ActivationFunctionType
AX = mybir.AxisListType

P = 128
T, D = 4096, 512
G, DV = 3202, 384
H, DH = 4, 32
INNER = H * DH
TOP = 32
HID = 2048
NS = 64
TILES = T // P
GC = -(-G // P)
GLAST = G - (GC - 1) * P
DC = D // P
VC = DV // P
QUAD = 4
EPS = 1e-5
SCALE = 1.0 / math.sqrt(DH)
SEGS = 32
SEG = G // SEGS
CAND = SEGS * 8
LOWEST = -3.0e38
MASKED = 1.0e30
BANK = 512
SCORE_CHUNKS = -(-G // BANK)
ROUND = 1.5 * 2 ** 23


def phase_scope(nc):
    scope = ExitStack()

    def sb(name, shape, dt=F32):
        return scope.enter_context(nc.sbuf_tensor(name, shape, dt))

    def ps(name, shape, dt=F32):
        return scope.enter_context(nc.psum_tensor(name, shape, dt))

    return scope, sb, ps


I8 = mybir.dt.int8


def before(m, b):
    return (m, 0) if b else (m - 1, 1)


def after(m, b):
    return (m + 1, 0) if b else (m, 1)


def normalise_quad(nc, x, out, stats, mv, rstd, std_wanted, std_ready, turn):
    for k in range(QUAD):
        nc.vector.bn_stats(stats[:, k, :], x[:, k, :])
    nc.vector.drain()
    for k in range(QUAD):
        last = nc.vector.bn_aggr(mv[:, k, :], stats[:, k, :])
    last.then_inc(std_wanted, 1)
    nc.vector.wait_ge(std_ready, turn + 1)
    nc.vector.reciprocal(rstd[:], rstd[:])
    nc.vector.drain()
    for k in range(QUAD):
        last = nc.vector.tensor_scalar(out[:, k, :], x[:, k, :], mv[:, k, 0:1], rstd[:, k:k + 1],
                                       ALU.subtract, ALU.mult)
    return last


def key_rows(h):
    at = h % 2 * 2 * DH
    return slice(at, at + DH), slice(at + DH, at + 2 * DH), slice(h * DH, (h + 1) * DH)


def prepare_attention(nc, sem, const, a, KT, dram):
    scope, sb, ps = phase_scope(nc)
    ident, eps = const["ident"], const["eps"]
    x_q = a["x"].rearrange("(q k p) d -> q p k d", k=QUAD, p=P)
    xt_q = dram["xt"].rearrange("(q k p) d -> q p k d", k=QUAD, p=P)
    ctx_q = a["ctx"][0:24 * P, :].rearrange("(q k p) c -> q p k c", k=QUAD, p=P)
    with scope:
        wq = sb("wq", [P, DC, INNER])
        wk = sb("wk", [P, VC, INNER])
        x_in = sb("x_in", [P, 2, QUAD, D])
        xt = sb("xt_prep", [P, 2, QUAD, D])
        xtT = sb("xtT_prep", [P, DC, QUAD * P])
        qt = sb("qt_prep", [P, 2, 2, QUAD * P], F32R)
        stats = sb("stats_prep", [P, QUAD, 6])
        mv = sb("mv_prep", [P, QUAD, 2])
        rstd = sb("rstd_prep", [P, QUAD])
        cx = sb("cx_prep", [P, 2, QUAD, DV])
        cxT = sb("cxT_prep", [P, VC, QUAD * P])
        tp = ps("tp_prep", [P, DC, BANK])
        qp = ps("qp_prep", [P, BANK])
        kp = ps("kp_prep", [P, BANK])
        quads = T // (QUAD * P)
        cquads = 24 // QUAD
        s = {n: sem("prep_" + n) for n in (
            "weights_in", "x_loaded0", "x_loaded1", "x_read", "std_wanted", "std_ready", "xt_ready", "xt_turned", "xtT_ready",
            "q_done", "q_copied", "q_stored", "xt_stored", "stored", "cx_loaded0", "cx_loaded1", "cx_turned", "cxT_ready", "k_done",
            "k_high", "k_copied", "xt_transposed")}

        with nc.Block() as block:
            @block.sync
            def _(sp):
                sp.dma_start(wq[:], a["Wq"].rearrange("(c p) n -> p c n", p=P)).then_inc(s["weights_in"], 16)
                sp.dma_start(wk[:], a["Wk"].rearrange("(c p) n -> p c n", p=P)).then_inc(s["weights_in"], 16)

                with sp.Fori(0, quads // 2) as i:
                    for b in range(2):
                        q = 2 * i + b
                        sp.wait_ge(s["x_read"], q + 1)
                        sp.dma_start(x_in[:, b], x_q[q, :, :, :]).then_inc(s[f"x_loaded{b}"], 16)
                with sp.Fori(0, cquads // 2) as i:
                    for b in range(2):
                        sp.wait_ge(s["cx_turned"], 2 * i + b + 1)
                        sp.dma_start(cx[:, b], ctx_q[2 * i + b, :, :, :]).then_inc(s[f"cx_loaded{b}"], 16)
                sp.wait_ge(s["cx_turned"], cquads + 1)
                sp.dma_start(cx[:, 0, 0, :], a["ctx"][24 * P:25 * P, :]).then_inc(s["cx_loaded0"], 16)
                sp.dma_start(cx[0:GLAST, 0, 1, :], a["ctx"][25 * P:G, :]).then_inc(s["cx_loaded0"], 16)

            @block.gpsimd
            def _(pool):
                with pool.Fori(0, quads // 2) as i:
                    for b in range(2):
                        q = 2 * i + b
                        pool.wait_ge(s["xt_ready"], q + 1)
                        pool.dma_start(xt_q[q, :, :, :], xt[:, b]).then_inc(s["xt_stored"], 16)
                        pool.wait_ge(s["q_copied"], q + 1)
                        pool.dma_start(dram["qt"][:, :, bass.ts(q, QUAD * P)].rearrange("c p t -> p c t"), qt[:, b].bitcast(F32)).then_inc(s["q_stored"], 16)
                        pool.wait_ge(s["xt_stored"], 16 * (q + 1))
                        pool.wait_ge(s["q_stored"], 16 * (q + 1))
                        pool.sem_inc(s["stored"], 1)

            @block.vector
            def _(dve):
                dve.sem_inc(s["x_read"], 2)
                dve.sem_inc(s["stored"], 2)
                with dve.Fori(0, quads // 2) as i:
                    for b in range(2):
                        q = 2 * i + b
                        dve.wait_ge(s[f"x_loaded{b}"], 16 * (i + 1))
                        dve.wait_ge(s["stored"], q + 1)
                        normalise_quad(nc, x_in[:, b], xt[:, b], stats, mv, rstd, s["std_wanted"], s["std_ready"],
                                       q).then_inc(s["xt_ready"], 1)
                        dve.drain()
                        dve.sem_inc(s["x_read"], 1)
                        dve.wait_ge(s["q_done"], q + 1)
                        nc.vector.tensor_copy(qt[:, b, 0], qp[:])
                        dve.drain()
                        nc.vector.tensor_tensor(qt[:, b, 1], qp[:], qt[:, b, 0].bitcast(F32), ALU.subtract).then_inc(s["q_copied"], 1)
                for q in range(cquads + 1):
                    w = QUAD * P if q < cquads else P + GLAST
                    dve.wait_ge(s["k_high"], q + 1)
                    for h in range(H):
                        high, low, src = key_rows(h)
                        last = nc.vector.tensor_tensor(KT[low, h // 2, q * BANK:q * BANK + w], kp[src, 0:w],
                                                       KT[high, h // 2, q * BANK:q * BANK + w].bitcast(F32), ALU.subtract)
                    last.then_inc(s["k_copied"], 1)

            @block.scalar
            def _(act):
                with act.Fori(0, quads) as q:
                    act.wait_ge(s["std_wanted"], q + 1)
                    nc.scalar.activation(rstd[:], mv[:, :, 1], ACT.Sqrt, bias=eps[:, 0:1]).then_inc(s["std_ready"], 1)
                    act.wait_ge(s["xt_turned"], q + 1)
                    nc.scalar.activation(xtT[:], tp[:], ACT.Copy).then_inc(s["xtT_ready"], 1)
                for q in range(cquads + 1):
                    w = QUAD * P if q < cquads else P + GLAST
                    act.wait_ge(s["cx_turned"], q + 3)
                    nc.scalar.activation(cxT[:, :, 0:w], tp[:, 0:VC, 0:w], ACT.Copy).then_inc(s["cxT_ready"], 1)
                    act.wait_ge(s["k_done"], q + 1)
                    for h in range(H):
                        high, _, src = key_rows(h)
                        last = nc.scalar.activation(KT[high, h // 2, q * BANK:q * BANK + w], kp[src, 0:w], ACT.Copy)
                    last.then_inc(s["k_high"], 1)

            @block.tensor
            def _(pe):
                pe.sem_inc(s["cx_turned"], 2)
                pe.wait_ge(s["weights_in"], 32)
                with pe.Fori(0, quads // 2) as i:
                    for b in range(2):
                        q = 2 * i + b
                        pe.wait_ge(s["xt_ready"], q + 1)
                        for c in range(DC):
                            for k in range(QUAD):
                                last = nc.tensor.transpose(tp[:, c, k * P:(k + 1) * P], xt[:, b, k, c * P:(c + 1) * P],
                                                           ident[:])
                        last.then_inc(s["xt_turned"], 1)
                        pe.wait_ge(s["xtT_ready"], q + 1)
                        for c in range(DC):
                            last = nc.tensor.matmul(qp[:], lhsT=wq[:, c, :], rhs=xtT[:, c, :], start=(c == 0),
                                                    stop=(c == DC - 1))
                        last.then_inc(s["q_done"], 1)
                for q in range(cquads + 1):
                    parts = [(k, P) for k in range(QUAD)] if q < cquads else [(0, P), (1, GLAST)]
                    w = sum(n for _, n in parts)
                    pe.wait_ge(s[f"cx_loaded{q % 2}"], 16 * (q // 2 + 1) if q < cquads else 16 * (q // 2 + 2))
                    for c in range(VC):
                        for k, n in parts:
                            last = nc.tensor.transpose(tp[:, c, k * P:k * P + n], cx[0:n, q % 2, k, c * P:(c + 1) * P],
                                                       ident[0:n, 0:n])
                    last.then_inc(s["cx_turned"], 1)
                    pe.wait_ge(s["cxT_ready"], q + 1)
                    if q:
                        pe.wait_ge(s["k_copied"], q)
                    for c in range(VC):
                        last = nc.tensor.matmul(kp[:, 0:w], lhsT=wk[:, c, :], rhs=cxT[:, c, 0:w], start=(c == 0),
                                                stop=(c == VC - 1))
                    last.then_inc(s["k_done"], 1)


def attention(nc, sem, const, a, KT, dram):
    scope, sb, ps = phase_scope(nc)
    ident, ones = const["ident"], const["ones"]
    with scope:
        ctx = sb("ctx", [P, GC, DV])
        hidden = sb("hidden", [P, G], I8)
        S = sb("S", [P, 2, H, G])
        E = sb("E", [P, 2, G])
        attnT = sb("attnT", [P, 2, 4, P])
        q = sb("q", [P, 2, H // 2, P], F32R)
        cand = sb("cand", [P, H, CAND])
        tops = sb("tops", [P, 2, H, TOP])
        seg8 = sb("seg8", [P, H])
        left = sb("left", [P, H])
        bad = sb("bad", [P, H])
        badi = sb("badi", [1, H + 1], I32)
        masked = sb("masked", [1, 1], I32)
        mrow = sb("mrow", [1, 1])
        tmask8 = sb("tmask8", [P, TILES], U8)
        tmask = sb("tmask", [P, TILES])
        nmax = sb("nmax", [P, H])
        etop = sb("etop", [P, H, TOP], BF16)
        den = sb("den", [P, H])
        lden = sb("lden", [P, H])
        ebias = sb("ebias", [P, 2, H])
        u = sb("u", [P, DV])
        score = [ps(f"score{k}", [P, 2, BANK]) for k in range(2)]
        tp = [ps(f"turn{k}", [P, 4, P]) for k in range(2)]
        up = ps("up", [P, BANK])
        fp = ps("fp", [P, BANK])
        mask8 = E[:, 0, :].bitcast(U8)[:, 0:G]
        s = {n: sem("attn_" + n) for n in (
            "ctx_in", "mask_in", "tmask_ready", "q_in", "q_free", "score_done", "score_copied", "flags_wanted",
            "flags_done", "tops_final", "lden_ready", "ebias_ready", "e_ready", "e_used", "pair_summed", "summed", "turned",
            "turn_copied", "times_done", "u_copied", "u_stored", "passed")}
        ORDER = (1, 3, 2, 0)
        HALVES = -(-SCORE_CHUNKS // 2)
        GROUPS = H * HALVES
        TURNS = SCORE_CHUNKS

        def chunk(j):
            return slice(j * BANK, min((j + 1) * BANK, G))

        with nc.Block() as block:
            @block.sync
            def _(sp):
                sp.dma_start(mask8, a["mask2"].partition_broadcast(P)).then_inc(s["mask_in"], 16)
                sp.dma_start(tmask8[:], a["mask1"].rearrange("(n p) -> p n", p=P), allow_slow_non_contiguous=True).then_inc(s["mask_in"], 16)
                qd = dram["qt"].rearrange("c (p e d) t -> e d c p t", e=2, d=DH)
                with sp.Fori(0, TILES) as n:
                    sp.wait_ge(s["q_free"], n + 1)
                    for e in range(2):
                        for r in range(2):
                            at = (2 * e + r) * DH
                            sp.dma_start(q[at:at + DH].bitcast(F32), qd[e, :, :, :, bass.ts(n, P)]).then_inc(s["q_in"], 16)

            @block.gpsimd
            def _(pool):
                def bias(m, b):
                    pool.wait_ge(s["lden_ready"], 2 * m + b + 1)
                    nc.gpsimd.tensor_tensor(ebias[:, b, :], nmax[:], lden[:], ALU.subtract).then_inc(s["ebias_ready"], 1)

                def sums(m, b):
                    n = 2 * m + b
                    pool.wait_ge(s["e_used"], H * n + 4)
                    nc.gpsimd.tensor_tensor(S[:, b, 0, :], S[:, b, 0, :], S[:, b, 1, :], ALU.add).then_inc(s["pair_summed"], 1)
                    pool.wait_ge(s["e_used"], H * n + 6)
                    nc.gpsimd.tensor_tensor(S[:, b, 2, :], S[:, b, 2, :], S[:, b, 3, :], ALU.add).then_inc(s["pair_summed"], 1)
                    pool.drain()
                    for j in range(SCORE_CHUNKS):
                        nc.gpsimd.tensor_tensor(S[:, b, 0, chunk(j)], S[:, b, 0, chunk(j)], S[:, b, 2, chunk(j)],
                                                ALU.add).then_inc(s["summed"], 1)

                def turn(m, b):
                    bias(*before(m, b))
                    sums(*before(m, b))

                turn(0, 1)
                with pool.Fori(0, (TILES - 2) // 2) as i:
                    turn(i + 1, 0)
                    turn(i + 1, 1)
                turn(TILES // 2, 0)

            @block.vector
            def _(dve):
                dve.wait_ge(s["mask_in"], 32)
                nc.vector.tensor_scalar(hidden[:], mask8, 1.0, None, ALU.subtract)
                nc.vector.tensor_reduce(mrow[:], mask8[0:1, :], AX.X, ALU.min)
                nc.vector.tensor_copy(tmask[:], tmask8[:]).then_inc(s["tmask_ready"], 1)
                dve.drain()
                nc.vector.tensor_scalar(mrow[:], mrow[:], -1.0, 1.0, ALU.mult, ALU.add)
                dve.drain()
                nc.vector.tensor_copy(masked[:], mrow[:])
                dve.drain()
                any_masked = dve.value_load(masked[0:1, 0:1], min_val=0, max_val=1)

                def arrived(n, groups):
                    dve.wait_ge(s["score_copied"], GROUPS * n + groups + 2)
                    dve.sem_inc(s["passed"], 1)

                def segments(m, b, h):
                    n = 2 * m + b
                    arrived(n, HALVES * (ORDER.index(h) + 1))
                    with dve.If(any_masked > 0):
                        nc.vector.scalar_tensor_tensor(S[:, b, h, :], hidden[:], MASKED, S[:, b, h, :], ALU.mult, ALU.add)
                        dve.drain()
                    for k in range(SEGS):
                        end = (k + 1) * SEG if k < SEGS - 1 else G
                        nc.vector.max(cand[:, h, 8 * k:8 * k + 8], S[:, b, h, k * SEG:end])

                def keep_top(m, b, h):
                    dve.wait_ge(s["e_ready"], H * (2 * m + b) + h + 1)
                    nc.vector.scalar_tensor_tensor(S[:, b, h, :], S[:, b, h, :], tops[:, b, h, TOP - 1:TOP], E[:, h % 2, :],
                                                   ALU.is_ge, ALU.mult).then_inc(s["e_used"], 1)

                def exact(b, h):
                    src, rest = S[:, b, h, :], E[:, 0, :]
                    for r in range(TOP // 8):
                        nc.vector.max(tops[:, b, h, 8 * r:8 * r + 8], src)
                        dve.drain()
                        nc.vector.match_replace(rest, tops[:, b, h, 8 * r:8 * r + 8], src, LOWEST)
                        dve.drain()
                        src = rest
                    nc.vector.tensor_tensor(rest, rest, S[:, b, h, :], ALU.is_equal)
                    dve.drain()
                    nc.vector.scalar_tensor_tensor(S[:, b, h, :], rest, LOWEST, S[:, b, h, :], ALU.mult, ALU.add)
                    dve.drain()

                def thresholds(m, b):
                    dve.drain()
                    nc.vector.tensor_reduce(seg8[:], cand[:, :, 7::8], AX.X, ALU.max)
                    for r in range(TOP // 8):
                        for h in range(H):
                            nc.vector.max(tops[:, b, h, 8 * r:8 * r + 8], cand[:, h, :])
                        dve.drain()
                        if r < TOP // 8 - 1:
                            for h in range(H):
                                nc.vector.match_replace(cand[:, h, :], tops[:, b, h, 8 * r:8 * r + 8], cand[:, h, :], LOWEST)
                            dve.drain()
                    for h in range(H):
                        nc.vector.tensor_scalar(cand[:, h, :], cand[:, h, :], tops[:, b, h, TOP - 1:TOP], 0.0,
                                                ALU.is_ge, ALU.add, accum_out=left[:, h:h + 1])
                    nc.vector.tensor_tensor(bad[:], seg8[:], tops[:, b, :, TOP - 1], ALU.is_ge)
                    dve.drain()
                    nc.vector.scalar_tensor_tensor(bad[:], left[:], 8.0, bad[:], ALU.not_equal, ALU.add).then_inc(s["flags_wanted"], 1)

                def check(m, b):
                    dve.wait_ge(s["flags_done"], 2 * m + b + 1)
                    nc.vector.tensor_copy(badi[0:1, 0:H], fp[0:1, 0:H])
                    nc.vector.tensor_reduce(badi[0:1, H:H + 1], fp[0:1, 0:H], AX.X, ALU.max)
                    dve.drain()
                    some = dve.value_load(badi[0:1, H:H + 1], min_val=0, max_val=2 * P)
                    with dve.If(some > 0):
                        for h in range(H):
                            this = dve.value_load(badi[0:1, h:h + 1], min_val=0, max_val=2 * P)
                            with dve.If(this > 0):
                                exact(b, h)
                    dve.drain()
                    dve.sem_inc(s["tops_final"], 1)

                def turn(m, b, first=False):
                    segments(m, b, ORDER[0])
                    segments(m, b, ORDER[1])
                    if not first:
                        check(*before(m, b))
                    segments(m, b, ORDER[2])
                    if not first:
                        for h in range(H):
                            keep_top(*before(m, b), h)
                    segments(m, b, ORDER[3])
                    thresholds(m, b)

                dve.sem_inc(s["e_used"], 2)
                turn(0, 0, first=True)
                with dve.Fori(0, (TILES - 2) // 2) as i:
                    turn(i, 1)
                    turn(i + 1, 0)
                turn(TILES // 2 - 1, 1)
                check(TILES // 2 - 1, 1)
                for h in range(H):
                    keep_top(TILES // 2 - 1, 1, h)

            @block.scalar
            def _(act):
                act.dma_start(ctx[:, 0:GC - 1, :], a["ctx"][0:(GC - 1) * P, :].rearrange("(k p) c -> p k c", p=P)).then_inc(s["ctx_in"], 16)
                act.dma_start(ctx[0:GLAST, GC - 1, :], a["ctx"][(GC - 1) * P:G, :]).then_inc(s["ctx_in"], 16)
                act.sem_inc(s["score_copied"], 2)
                act.sem_inc(s["turn_copied"], 2)
                act.sem_inc(s["u_stored"], 16)
                act.sem_inc(s["u_copied"], 1)

                def copy_scores(m, b, h, groups=range(HALVES)):
                    n = 2 * m + b
                    for k in groups:
                        act.wait_ge(s["score_done"], GROUPS * n + HALVES * ORDER.index(h) + k + 1)
                        w = min(2 * BANK, G - 2 * BANK * k)
                        nc.scalar.activation(S[:, b, h, 2 * BANK * k:2 * BANK * k + w],
                                             score[k % 2][:, :, :].rearrange("p c k -> p (c k)")[:, 0:w],
                                             ACT.Copy).then_inc(s["score_copied"], 1)

                def sums_of_exps(m, b):
                    n = 2 * m + b
                    act.wait_ge(s["tops_final"], n + 1)
                    nc.scalar.mul(nmax[:], tops[:, b, :, 0], -SCALE)
                    act.drain()
                    for h in range(H):
                        nc.scalar.activation(etop[:, h, :], tops[:, b, h, :], ACT.Exp, bias=nmax[:, h:h + 1], scale=SCALE,
                                             accum_out=den[:, h:h + 1])
                    act.drain()
                    nc.scalar.activation(lden[:], den[:], ACT.Ln, scale=float(H)).then_inc(s["lden_ready"], 1)

                def probabilities(m, b, h):
                    n = 2 * m + b
                    if h == 0:
                        act.wait_ge(s["ebias_ready"], n + 1)
                    act.wait_ge(s["e_used"], H * n + h + 1)
                    nc.scalar.activation(E[:, h % 2, :], S[:, b, h, :], ACT.Exp, bias=ebias[:, b, h:h + 1],
                                         scale=SCALE).then_inc(s["e_ready"], 1)

                def copy_turned(m, b, g):
                    n = 2 * m + b
                    act.wait_ge(s["turned"], TURNS * n + g + 1)
                    act.wait_ge(s["times_done"], TURNS * n + g + 1)
                    w = min(4, GC - 4 * g)
                    e = (TURNS * b + g) % 2
                    if g < TURNS - 1:
                        nc.scalar.activation(attnT[:, e], tp[e][:], ACT.Copy).then_inc(s["turn_copied"], 1)
                    else:
                        nc.scalar.activation(attnT[:, e, 0:w - 1, :], tp[e][:, 0:w - 1, :], ACT.Copy)
                        nc.scalar.activation(attnT[0:GLAST, e, w - 1, :], tp[e][0:GLAST, w - 1, :], ACT.Copy).then_inc(s["turn_copied"], 1)

                def copy_context(m, b):
                    n = 2 * m + b
                    act.wait_ge(s["times_done"], TURNS * (n + 1) + 2)
                    act.sem_inc(s["passed"], 1)
                    act.wait_ge(s["u_stored"], 16 * (n + 1))
                    act.sem_inc(s["passed"], 1)
                    nc.scalar.activation(u[:], up[:, 0:DV], ACT.Copy, scale=tmask[:, bass.ds(n, 1)]).then_inc(s["u_copied"], 1)
                    act.wait_ge(s["u_copied"], n + 2)
                    act.sem_inc(s["passed"], 1)
                    act.dma_start(dram["u"][bass.ts(n, P), :], u[:]).then_inc(s["u_stored"], 16)

                act.wait_ge(s["tmask_ready"], 1)
                nc.scalar.preload_act_table_set("natural_log_exp_and_others")
                for h in ORDER:
                    copy_scores(0, 0, h)
                for h in ORDER:
                    copy_scores(0, 1, h)

                def turn(m, b, last=False, beyond=False):
                    if not last:
                        copy_scores(*after(m, b), ORDER[0])
                        copy_scores(*after(m, b), ORDER[1])
                        copy_scores(*after(m, b), ORDER[2])
                    for g in range(TURNS - 2):
                        copy_turned(*before(m, b), g)
                    if not beyond:
                        sums_of_exps(m, b)
                        probabilities(m, b, 0)
                    copy_turned(*before(m, b), TURNS - 2)
                    if not beyond:
                        probabilities(m, b, 1)
                    copy_turned(*before(m, b), TURNS - 1)
                    if not beyond:
                        probabilities(m, b, 2)
                    if not last:
                        copy_scores(*after(m, b), ORDER[3], range(0, 2))
                    if not beyond:
                        probabilities(m, b, 3)
                    if not last:
                        copy_scores(*after(m, b), ORDER[3], range(2, HALVES))
                    copy_context(*before(m, b))

                sums_of_exps(0, 0)
                for h in range(H):
                    probabilities(0, 0, h)
                turn(0, 1)
                with act.Fori(0, (TILES - 4) // 2) as i:
                    turn(i + 1, 0)
                    turn(i + 1, 1)
                turn(TILES // 2 - 1, 0)
                turn(TILES // 2 - 1, 1, last=True)
                turn(TILES // 2, 0, last=True, beyond=True)
                act.wait_ge(s["u_stored"], 16 * (TILES + 1))

            @block.tensor
            def _(pe):
                pe.sem_inc(s["times_done"], 2)
                pe.sem_inc(s["q_free"], 1)

                def scores(m, b, h):
                    n = 2 * m + b
                    at = slice(h % 2 * 2 * DH, (h % 2 + 1) * 2 * DH)
                    if h == ORDER[0]:
                        pe.wait_ge(s["q_in"], 16 * 4 * (n + 1))
                    for k in range(HALVES):
                        pe.wait_ge(s["score_copied"], GROUPS * n + HALVES * ORDER.index(h) + k + 1)
                        for j in range(2 * k, min(2 * k + 2, SCORE_CHUNKS)):
                            w = chunk(j).stop - chunk(j).start
                            for part in range(2):
                                last = nc.tensor.matmul(score[k % 2][:, j % 2, 0:w], lhsT=q[at, part, h // 2, :],
                                                        rhs=KT[at, h // 2, chunk(j)], start=(part == 0), stop=(part == 1))
                        last.then_inc(s["score_done"], 1)

                def scores_end():
                    pe.drain()
                    pe.sem_inc(s["q_free"], 1)

                def flags(m, b):
                    pe.wait_ge(s["flags_wanted"], 2 * m + b + 1)
                    nc.tensor.matmul(fp[0:1, 0:H], lhsT=ones[:, 0:1], rhs=bad[:], start=True, stop=True).then_inc(s["flags_done"], 1)

                def turn_attention(m, b, g):
                    n = 2 * m + b
                    pe.wait_ge(s["summed"], TURNS * n + g + 1)
                    pe.wait_ge(s["turn_copied"], TURNS * n + g + 1)
                    e = (TURNS * b + g) % 2
                    for c in range(4 * g, min(4 * g + 4, GC)):
                        w = P if c < GC - 1 else GLAST
                        last = nc.tensor.transpose(tp[e][0:w, c - 4 * g, :], S[:, b, 0, c * P:c * P + w], ident[:])
                    last.then_inc(s["turned"], 1)

                def times_context(m, b, g):
                    n = 2 * m + b
                    pe.wait_ge(s["turn_copied"], TURNS * n + g + 3)
                    if g == 0:
                        pe.wait_ge(s["u_copied"], n + 1)
                    e = (TURNS * b + g) % 2
                    for c in range(4 * g, min(4 * g + 4, GC)):
                        w = P if c < GC - 1 else GLAST
                        last = nc.tensor.matmul(up[:, 0:DV], lhsT=attnT[0:w, e, c - 4 * g, :], rhs=ctx[0:w, c, :],
                                                start=(c == 0), stop=(c == GC - 1))
                    last.then_inc(s["times_done"], 1)

                def turn(m, b, last=False, beyond=False):
                    old, new = before(m, b), after(m, b)
                    if not last:
                        pe.wait_ge(s["pair_summed"], 2 * (2 * m + b) - 1)
                        scores(*new, ORDER[0])
                        pe.wait_ge(s["pair_summed"], 2 * (2 * m + b))
                        scores(*new, ORDER[1])
                        pe.wait_ge(s["summed"], TURNS * (2 * m + b))
                        scores(*new, ORDER[2])
                    turn_attention(*old, 0)
                    if not beyond:
                        flags(m, b)
                    for g in range(TURNS):
                        if g < TURNS - 1:
                            turn_attention(*old, g + 1)
                        if g == TURNS - 1 and not last:
                            scores(*new, ORDER[3])
                        times_context(*old, g)
                    if not last:
                        scores_end()

                pe.wait_ge(s["ctx_in"], 32)
                for h in ORDER:
                    scores(0, 0, h)
                scores_end()
                for h in ORDER:
                    scores(0, 1, h)
                scores_end()
                flags(0, 0)
                turn(0, 1)
                with pe.Fori(0, (TILES - 4) // 2) as i:
                    turn(i + 1, 0)
                    turn(i + 1, 1)
                turn(TILES // 2 - 1, 0)
                turn(TILES // 2 - 1, 1, last=True)
                turn(TILES // 2, 0, last=True, beyond=True)


def film_weights(nc, sem, const, a, side, wf, fb):
    scope, sb, ps = phase_scope(nc)
    with scope:
        tag = "film_" + side
        wv = sb(tag + "_wv", [P, VC, D])
        wvT = sb(tag + "_wvT", [P, DC, DV])
        w = sb(tag + "_w", [P, DC, 2 * D])
        gate = sb(tag + "_gate", [P, 1])
        tp = ps(tag + "_tp", [P, VC, BANK])
        mp = [ps(f"{tag}_mp{k}", [P, BANK]) for k in range(2)]
        s = {n: sem(f"{tag}_{n}") for n in ("in", "turned", "turn_copied", "multiplied", "copied", "offset")}
        products = [(c, half) for c in range(VC) for half in range(2)]

        with nc.Block() as block:
            @block.sync
            def _(sp):
                sp.dma_start(wv[:], a["Wv"].rearrange("(c p) n -> p c n", p=P)).then_inc(s["in"], 16)
                sp.dma_start(gate[:], a["mod_gate"].partition_broadcast(P)).then_inc(s["in"], 16)
                sp.dma_start(fb[:], a["b_film_" + side].partition_broadcast(P)).then_inc(s["in"], 16)
                sp.dma_start(w[:], a["W_film_" + side].rearrange("(c p) n -> p c n", p=P)).then_inc(s["in"], 16)

            @block.vector
            def _(dve):
                dve.wait_ge(s["in"], 64)
                nc.vector.tensor_scalar(fb[:, 0:D], fb[:, 0:D], gate[:, 0:1], 1.0, ALU.mult, ALU.add)
                nc.vector.tensor_scalar(fb[:, D:2 * D], fb[:, D:2 * D], gate[:, 0:1], None, ALU.mult).then_inc(s["offset"], 1)
                dve.wait_ge(s["offset"], 1)

            @block.tensor
            def _(pe):
                pe.wait_ge(s["in"], 64)
                for c in range(VC):
                    for k in range(DC):
                        last = nc.tensor.transpose(tp[:, c, k * P:(k + 1) * P], wv[:, c, k * P:(k + 1) * P], const["ident"][:])
                last.then_inc(s["turned"], 1)
                pe.wait_ge(s["turn_copied"], 1)
                for j, (c, half) in enumerate(products):
                    if j >= 2:
                        pe.wait_ge(s["copied"], j - 1)
                    for k in range(DC):
                        last = nc.tensor.matmul(mp[j % 2][:], lhsT=wvT[:, k, c * P:(c + 1) * P],
                                                rhs=w[:, k, half * D:(half + 1) * D], start=(k == 0), stop=(k == DC - 1))
                    last.then_inc(s["multiplied"], 1)

            @block.scalar
            def _(act):
                act.wait_ge(s["turned"], 1)
                for c in range(VC):
                    last = nc.scalar.activation(wvT[:, :, c * P:(c + 1) * P], tp[:, c, :].rearrange("p (k q) -> p k q", q=P), ACT.Copy)
                last.then_inc(s["turn_copied"], 1)
                act.wait_ge(s["in"], 64)
                for j, (c, half) in enumerate(products):
                    act.wait_ge(s["multiplied"], j + 1)
                    nc.scalar.activation(wf[:, c, half * D:(half + 1) * D], mp[j % 2][:], ACT.Copy,
                                         scale=gate[:, 0:1]).then_inc(s["copied"], 1)
                act.wait_ge(s["copied"], len(products))


def modulate(nc, sem, const, a, wf, fb, X, dram):
    scope, sb, ps = phase_scope(nc)
    with scope:
        u = sb("mod_u", [P, 2, DV])
        xt = sb("mod_xt", [P, 2, D])
        uT = sb("mod_uT", [P, 2, VC, P])
        xn = sb("mod_xn", [P, 2, D])
        gain = sb("mod_gain", [P, D])
        offset = sb("mod_offset", [P, D])
        sc = sb("mod_scale", [P, D])
        sh = sb("mod_shift", [P, 2, D])
        xm = sb("mod_xm", [P, 2, D])
        stats = sb("mod_stats", [P, 6])
        mv = sb("mod_mv", [P, 2])
        rstd = sb("mod_rstd", [P, 1])
        tp = [ps(f"mod_tp{k}", [P, VC, P]) for k in range(2)]
        fp = [ps(f"mod_film{k}", [P, 2, BANK]) for k in range(2)]
        rp = [ps(f"mod_rev{k}", [P, BANK]) for k in range(2)]
        s = {n: sem("mod_" + n) for n in (
            "rows_in", "in0", "in1", "xt_read", "u_turned", "uT_ready", "film_done", "film_read", "std_wanted", "std_ready",
            "normed", "affine", "xm_ready", "reversed", "X_ready", "passed")}

        with nc.Block() as block:
            @block.sync
            def _(sp):
                sp.dma_start(gain[:], a["g_norm_in"].partition_broadcast(P)).then_inc(s["rows_in"], 16)
                sp.dma_start(offset[:], a["b_norm_in"].partition_broadcast(P)).then_inc(s["rows_in"], 16)
                with sp.Fori(0, TILES // 2) as i:
                    for b in range(2):
                        n = 2 * i + b
                        sp.wait_ge(s["xt_read"], n + 1)
                        sp.dma_start(xt[:, b], dram["xt"][bass.ts(n, P), :]).then_inc(s[f"in{b}"], 16)
                        sp.wait_ge(s["u_turned"], n + 1)
                        sp.dma_start(u[:, b], dram["u"][bass.ts(n, P), :]).then_inc(s[f"in{b}"], 16)

            @block.gpsimd
            def _(pool):
                pool.wait_ge(s["rows_in"], 32)
                with pool.Fori(0, TILES // 2) as i:
                    for b in range(2):
                        pool.wait_ge(s["normed"], 2 * i + b + 1)
                        nc.gpsimd.tensor_tensor(xn[:, b], xn[:, b], gain[:], ALU.mult)
                        pool.drain()
                        nc.gpsimd.tensor_tensor(xn[:, b], xn[:, b], offset[:], ALU.add).then_inc(s["affine"], 1)

            @block.vector
            def _(dve):
                dve.sem_inc(s["xt_read"], 2)

                def normalise(m, b):
                    n = 2 * m + b
                    dve.wait_ge(s[f"in{b}"], 32 * (m + 1))
                    nc.vector.bn_stats(stats[:], xt[:, b, :])
                    dve.drain()
                    nc.vector.bn_aggr(mv[:], stats[:]).then_inc(s["std_wanted"], 1)
                    dve.wait_ge(s["std_ready"], n + 1)
                    nc.vector.reciprocal(rstd[:], rstd[:])
                    dve.drain()
                    nc.vector.tensor_scalar(xn[:, b], xt[:, b], mv[:, 0:1], rstd[:, 0:1], ALU.subtract, ALU.mult).then_inc(s["normed"], 1)
                    dve.drain()
                    dve.sem_inc(s["xt_read"], 1)

                def film(m, b):
                    n = 2 * m + b
                    dve.drain()
                    dve.wait_ge(s["film_done"], n + 1)
                    nc.vector.tensor_tensor(sc[:], fp[b][:, 0, :], fb[:, 0:D], ALU.add)
                    nc.vector.tensor_tensor(sh[:, b], fp[b][:, 1, :], fb[:, D:2 * D], ALU.add).then_inc(s["film_read"], 1)
                    dve.drain()
                    dve.wait_ge(s["affine"], n + 1)
                    nc.vector.tensor_tensor(sc[:], xn[:, b], sc[:], ALU.mult)
                    dve.drain()
                    dve.wait_ge(s["reversed"], n + 1)
                    nc.vector.tensor_tensor(xm[:, b], sc[:], sh[:, b], ALU.add).then_inc(s["xm_ready"], 1)

                normalise(0, 0)
                with dve.Fori(0, TILES // 2 - 1) as i:
                    for b in range(2):
                        normalise(*after(i, b))
                        film(i, b)
                normalise(TILES // 2 - 1, 1)
                film(TILES // 2 - 1, 0)
                film(TILES // 2 - 1, 1)

            @block.scalar
            def _(act):
                act.sem_inc(s["X_ready"], 2)

                def root(m, b):
                    act.wait_ge(s["std_wanted"], 2 * m + b + 1)
                    nc.scalar.activation(rstd[:], mv[:, 1:2], ACT.Sqrt, bias=const["eps"][:, 0:1]).then_inc(s["std_ready"], 1)

                def copy_u(m, b):
                    act.wait_ge(s["u_turned"], 2 * m + b + 3)
                    nc.scalar.activation(uT[:, b], tp[b][:], ACT.Copy).then_inc(s["uT_ready"], 1)

                def copy_x(m, b):
                    n = 2 * m + b
                    act.wait_ge(s["reversed"], n + 3)
                    act.sem_inc(s["passed"], 1)
                    nc.scalar.activation(X[:, bass.ds(n, 1), :], rp[b][:].unsqueeze(1), ACT.Copy).then_inc(s["X_ready"], 1)

                root(0, 0)
                copy_u(0, 0)
                root(0, 1)
                copy_u(0, 1)
                with act.Fori(0, TILES // 2 - 1) as i:
                    for b in range(2):
                        root(i + 1, b)
                        copy_u(i + 1, b)
                        copy_x(i, b)
                copy_x(TILES // 2 - 1, 0)
                copy_x(TILES // 2 - 1, 1)
                act.wait_ge(s["X_ready"], TILES + 2)

            @block.tensor
            def _(pe):
                pe.sem_inc(s["u_turned"], 2)
                pe.sem_inc(s["reversed"], 2)

                def turn_u(m, b):
                    pe.wait_ge(s[f"in{b}"], 32 * (m + 1))
                    for c in range(VC):
                        last = nc.tensor.transpose(tp[b][:, c, :], u[:, b, c * P:(c + 1) * P], const["ident"][:])
                    last.then_inc(s["u_turned"], 1)

                def film(m, b):
                    n = 2 * m + b
                    pe.wait_ge(s["uT_ready"], n + 1)
                    pe.wait_ge(s["film_read"], n + 1)
                    for half in range(2):
                        for c in range(VC):
                            last = nc.tensor.matmul(fp[b][:, half, :], lhsT=uT[:, b, c, :], rhs=wf[:, c, half * D:(half + 1) * D],
                                                    start=(c == 0), stop=(c == VC - 1))
                    last.then_inc(s["film_done"], 1)

                def reverse(m, b):
                    n = 2 * m + b
                    pe.wait_ge(s["xm_ready"], n + 1)
                    pe.wait_ge(s["X_ready"], n + 1)
                    nc.tensor.matmul(rp[b][:], lhsT=const["anti"][:], rhs=xm[:, b], start=True, stop=True).then_inc(s["reversed"], 1)

                pe.sem_inc(s["film_read"], 2)
                turn_u(0, 0)
                turn_u(0, 1)
                film(0, 0)
                with pe.Fori(0, TILES // 2 - 1) as i:
                    for b in range(2):
                        turn_u(i + 1, b)
                        film(*after(i, b))
                        reverse(i, b)
                film(TILES // 2 - 1, 1)
                reverse(TILES // 2 - 1, 0)
                reverse(TILES // 2 - 1, 1)


LOG2E = 1.0 / math.log(2.0)
LN2_HIGH = 0.693359375
LN2_LOW = math.log(2.0) - LN2_HIGH
HALF_PI = [1.5703125, 4.837512969970703125e-4, 7.54978995489188216e-8]
EXP_TERMS = [1.0 / math.factorial(k) for k in range(7, 0, -1)]
SIN_TERMS = [1.0 / 362880, -1.0 / 5040, 1.0 / 120, -1.0 / 6]
COS_TERMS = [-1.0 / 3628800, 1.0 / 40320, -1.0 / 720, 1.0 / 24, -0.5]
LEVELS = 7
PAIRS = D // 2
CHUNKS = TILES
GROUP = 64
KROW = 2 * P


def s4d_scalars(nc, sem, const, a, W, root):
    scope, sb, ps = phase_scope(nc)
    with scope:
        one_row = sb("ss_one_row", [1, NS])
        raw = sb("ss_raw", [P, 4, DC, NS])
        ldt = sb("ss_ldt", [1, D])
        sc = sb("ss_sc", [P, 5, PAIRS])
        wide = {n: sb("ss_" + n, [P, 2, PAIRS]) for n in ("x", "t", "r", "p", "z", "sin", "cos", "m", "o", "b1", "b2", "mag")}
        whole = sb("ss_whole", [P, 2, PAIRS], I32)
        t = [sb(f"ss_t{k}", [P, PAIRS]) for k in range(8)]
        pin = ps("ss_pin", [P, 3, 2, PAIRS])
        s = {n: sem("ss_" + n) for n in ("in", "spread", "sc_ready", "root_wanted", "root_ready", "row_set")}
        names = ("A_re", "A_im", "C_re", "C_im")

        with nc.Block() as block:
            @block.sync
            def _(sp):
                for j, name in enumerate(names):
                    sp.dma_start(raw[:, j], a[name].rearrange("(c p) n -> p c n", p=P)).then_inc(s["in"], 16)
                sp.dma_start(ldt[:], a["log_dt"].unsqueeze(0)).then_inc(s["in"], 16)

            @block.tensor
            def _(pe):
                pe.wait_ge(s["in"], 16 * 5)
                pe.wait_ge(s["row_set"], 1)
                for e in range(2):
                    at = slice(NS * e, NS * (e + 1))
                    for j in range(4):
                        for c in range(DC):
                            nc.tensor.matmul(pin[at, j // 2, j % 2, NS * c:NS * (c + 1)], lhsT=raw[:, j, c, :],
                                             rhs=const["ident"][:, e::2], start=True, stop=True)
                    last = nc.tensor.matmul(pin[at, 2, 0, :], lhsT=one_row[:], rhs=ldt[0:1, e::2],
                                            start=True, stop=True)
                last.then_inc(s["spread"], 1)

            @block.scalar
            def _(act):
                act.wait_ge(s["spread"], 1)
                for j in range(5):
                    last = nc.scalar.activation(sc[:, j], pin[:, j // 2, j % 2, :], ACT.Copy)
                last.then_inc(s["sc_ready"], 1)
                for k in range(2):
                    act.wait_ge(s["root_wanted"], k + 1)
                    nc.scalar.activation(t[1][:], t[0][:], ACT.Sqrt).then_inc(s["root_ready"], 1)

            @block.vector
            def _(dve):
                v = nc.vector
                v.memset(one_row[:], 1.0).then_inc(s["row_set"], 1)

                def then(*_):
                    dve.drain()

                def exp(out, x):
                    tt, r, p = wide["t"][:, 0:1], wide["r"][:, 0:1], wide["p"][:, 0:1]
                    n = whole[:, 0:1]
                    then(v.tensor_scalar(x, x, -87.0, 88.0, ALU.max, ALU.min))
                    then(v.tensor_scalar(tt, x, LOG2E, ROUND, ALU.mult, ALU.add))
                    then(v.tensor_scalar(tt, tt, ROUND, None, ALU.subtract))
                    then(v.scalar_tensor_tensor(r, tt, -LN2_HIGH, x, ALU.mult, ALU.add))
                    then(v.scalar_tensor_tensor(r, tt, -LN2_LOW, r, ALU.mult, ALU.add),
                         v.tensor_scalar(x, tt, 127.0, 2.0 ** 23, ALU.add, ALU.mult))
                    then(v.tensor_scalar(p, r, EXP_TERMS[0], None, ALU.mult),
                         v.tensor_copy(n, x))
                    for c in EXP_TERMS[1:]:
                        then(v.scalar_tensor_tensor(p, p, c, r, ALU.add, ALU.mult))
                    then(v.scalar_tensor_tensor(out, p, 1.0, n.bitcast(F32), ALU.add, ALU.mult))

                def sin_cos():
                    x, tt, r, p, z, m, o = (wide[n][:] for n in ("x", "t", "r", "p", "z", "m", "o"))
                    sin, cos, b1, b2 = (wide[n][:] for n in ("sin", "cos", "b1", "b2"))
                    then(v.tensor_scalar(tt, x, 2.0 / math.pi, ROUND, ALU.mult, ALU.add))
                    then(v.tensor_scalar(tt, tt, ROUND, None, ALU.subtract))
                    then(v.scalar_tensor_tensor(r, tt, -HALF_PI[0], x, ALU.mult, ALU.add),
                         v.tensor_scalar(m, tt, 0.25, -0.375, ALU.mult, ALU.add))
                    then(v.scalar_tensor_tensor(r, tt, -HALF_PI[1], r, ALU.mult, ALU.add),
                         v.tensor_scalar(o, m, ROUND, ROUND, ALU.add, ALU.subtract))
                    then(v.scalar_tensor_tensor(r, tt, -HALF_PI[2], r, ALU.mult, ALU.add),
                         v.scalar_tensor_tensor(m, o, -4.0, tt, ALU.mult, ALU.add))
                    then(v.tensor_tensor(z, r, r, ALU.mult), v.tensor_scalar(o, m, 0.5, -0.25, ALU.mult, ALU.add))
                    then(v.tensor_scalar(p, z, SIN_TERMS[0], None, ALU.mult), v.tensor_scalar(cos, z, COS_TERMS[0], None, ALU.mult),
                         v.tensor_scalar(b1, o, ROUND, ROUND, ALU.add, ALU.subtract))
                    for k in range(1, 5):
                        if k < 4:
                            v.scalar_tensor_tensor(p, p, SIN_TERMS[k], z, ALU.add, ALU.mult)
                        then(v.scalar_tensor_tensor(cos, cos, COS_TERMS[k], z, ALU.add, ALU.mult))
                    then(v.scalar_tensor_tensor(sin, p, 1.0, r, ALU.add, ALU.mult),
                         v.tensor_scalar(cos, cos, 1.0, None, ALU.add),
                         v.scalar_tensor_tensor(o, b1, -2.0, m, ALU.mult, ALU.add))
                    then(v.scalar_tensor_tensor(b1, o, 1.0, sin, ALU.subtract, ALU.mult), v.tensor_tensor(b2, o, cos, ALU.mult),
                         v.scalar_tensor_tensor(p, o, 1.0, cos, ALU.subtract, ALU.mult), v.tensor_tensor(z, o, sin, ALU.mult),
                         v.tensor_scalar(x, m, 1.5, -2.0, ALU.is_ge, ALU.mult),
                         v.tensor_scalar(tt, m, 1.5, None, ALU.subtract))
                    then(v.tensor_tensor(b2, b2, b1, ALU.subtract), v.tensor_tensor(z, z, p, ALU.subtract),
                         v.scalar_tensor_tensor(tt, tt, -1.0, tt, ALU.mult, ALU.max))
                    then(v.tensor_scalar(tt, tt, 1.0, 2.0, ALU.is_ge, ALU.mult))
                    then(v.scalar_tensor_tensor(sin, x, 1.0, b2, ALU.add, ALU.mult),
                         v.scalar_tensor_tensor(cos, tt, 1.0, z, ALU.subtract, ALU.mult))

                def square_root(out, k):
                    dve.sem_inc(s["root_wanted"], 1)
                    dve.wait_ge(s["root_ready"], k + 1)
                    then(v.tensor_scalar(t[2][:], t[1][:], 1e-30, None, ALU.max))
                    then(v.reciprocal(t[2][:], t[2][:]))
                    then(v.tensor_tensor(t[2][:], t[2][:], t[0][:], ALU.mult))
                    then(v.tensor_tensor(t[2][:], t[2][:], t[1][:], ALU.add))
                    then(v.tensor_scalar(out, t[2][:], 0.5, None, ALU.mult))

                dve.wait_ge(s["sc_ready"], 1)
                are, aim, cre, cim = (sc[:, j] for j in range(4))
                x = wide["x"]
                dt = sc[:, 4]
                exp(dt.unsqueeze(1), dt.unsqueeze(1))
                then(v.tensor_tensor(x[:, 0], dt, are, ALU.mult))
                then(v.tensor_scalar(x[:, 1], x[:, 0], float(P), None, ALU.mult))
                exp(wide["mag"][:, 0:1], x[:, 0:1])
                exp(wide["mag"][:, 1:2], x[:, 1:2])
                then(v.tensor_tensor(x[:, 0], dt, aim, ALU.mult))
                then(v.tensor_scalar(x[:, 1], x[:, 0], float(P), None, ALU.mult))
                sin_cos()
                for k, level in ((0, 0), (1, LEVELS)):
                    v.tensor_tensor(W[:, level, 0], wide["mag"][:, k], wide["cos"][:, k], ALU.mult)
                    v.tensor_tensor(W[:, level, 1], wide["mag"][:, k], wide["sin"][:, k], ALU.mult)
                dve.drain()
                for level in range(1, LEVELS):
                    re, im = W[:, level - 1, 0], W[:, level - 1, 1]
                    then(v.tensor_tensor(t[0][:], re, im, ALU.subtract), v.tensor_tensor(t[1][:], re, im, ALU.add))
                    then(v.tensor_tensor(W[:, level, 0], t[0][:], t[1][:], ALU.mult),
                         v.scalar_tensor_tensor(W[:, level, 1], re, 2.0, im, ALU.mult, ALU.mult))
                wr, wi = W[:, 0, 0], W[:, 0, 1]
                then(v.tensor_scalar(t[0][:], wr, 1.0, None, ALU.subtract))
                then(v.tensor_tensor(t[1][:], cre, t[0][:], ALU.mult), v.tensor_tensor(t[2][:], cim, wi, ALU.mult),
                     v.tensor_tensor(t[3][:], cre, wi, ALU.mult), v.tensor_tensor(t[4][:], cim, t[0][:], ALU.mult),
                     v.tensor_tensor(t[5][:], are, are, ALU.mult), v.tensor_tensor(t[6][:], aim, aim, ALU.mult))
                then(v.tensor_tensor(t[1][:], t[1][:], t[2][:], ALU.subtract), v.tensor_tensor(t[3][:], t[3][:], t[4][:], ALU.add),
                     v.tensor_tensor(t[5][:], t[5][:], t[6][:], ALU.add))
                then(v.reciprocal(t[5][:], t[5][:]), v.tensor_tensor(t[0][:], t[1][:], are, ALU.mult),
                     v.tensor_tensor(t[2][:], t[3][:], aim, ALU.mult), v.tensor_tensor(t[4][:], t[3][:], are, ALU.mult),
                     v.tensor_tensor(t[6][:], t[1][:], aim, ALU.mult))
                then(v.tensor_tensor(t[0][:], t[0][:], t[2][:], ALU.add), v.tensor_tensor(t[4][:], t[4][:], t[6][:], ALU.subtract))
                dr, di = t[6], t[7]
                then(v.scalar_tensor_tensor(dr[:], t[0][:], 2.0, t[5][:], ALU.mult, ALU.mult),
                     v.scalar_tensor_tensor(di[:], t[4][:], 2.0, t[5][:], ALU.mult, ALU.mult))
                kr, ki, big = dr[:], di[:], sc[:, 2]
                then(v.tensor_tensor(t[0][:], kr, kr, ALU.mult), v.tensor_tensor(t[1][:], ki, ki, ALU.mult))
                then(v.tensor_tensor(t[0][:], t[0][:], t[1][:], ALU.add))
                square_root(big, 0)
                then(v.scalar_tensor_tensor(t[3][:], kr, -1.0, kr, ALU.mult, ALU.max))
                then(v.tensor_tensor(t[0][:], big, t[3][:], ALU.add))
                then(v.tensor_scalar(t[0][:], t[0][:], 0.5, None, ALU.mult))
                square_root(big, 1)
                then(v.tensor_scalar(t[0][:], big, 1e-30, 2.0, ALU.max, ALU.mult))
                then(v.reciprocal(t[0][:], t[0][:]), v.tensor_scalar(t[3][:], ki, 0.0, 2.0, ALU.is_ge, ALU.mult),
                     v.tensor_scalar(t[4][:], kr, 0.0, None, ALU.is_ge))
                then(v.tensor_tensor(t[0][:], t[0][:], ki, ALU.mult), v.scalar_tensor_tensor(t[3][:], t[3][:], 1.0, big, ALU.subtract, ALU.mult))
                then(v.scalar_tensor_tensor(t[1][:], t[0][:], -1.0, t[0][:], ALU.mult, ALU.max), v.tensor_tensor(t[2][:], t[4][:], big, ALU.mult),
                     v.tensor_tensor(t[5][:], t[4][:], t[0][:], ALU.mult), v.scalar_tensor_tensor(t[3][:], t[4][:], 1.0, t[3][:], ALU.subtract, ALU.mult))
                then(v.scalar_tensor_tensor(t[1][:], t[4][:], 1.0, t[1][:], ALU.subtract, ALU.mult))
                then(v.tensor_tensor(root[:, 0], t[2][:], t[1][:], ALU.subtract), v.tensor_tensor(root[:, 1], t[5][:], t[3][:], ALU.subtract))


def s4d(nc, sem, const, a, W, root, X, dram):
    scope, sb, ps = phase_scope(nc)
    GP = GROUP // 2
    GROUPS = PAIRS // GP
    PIECE = 16
    SHARES = {"dve": [(0, 12)], "pool": [(12, 22), (22, 32)]}
    SIDE = P // CHUNKS
    OUT = 4 * SIDE
    BLOCK = SIDE
    LOADS = 4
    UP = 2 * SIDE
    ROWS = GP // SIDE
    with scope:
        Q = sb("s4_Q", [P, 2, 2, GP, P + 1])
        S = sb("s4_S", [P, 2, 2, CHUNKS + 1, GP])
        Xg = sb("s4_Xg", [P, 2, GROUP, CHUNKS])
        QT = sb("s4_QT", [P, 2, 4, P])
        M = {"dve": sb("s4_M_dve", [P, 2, 2, 12, PIECE]), "pool": sb("s4_M_pool", [P, 2, 2, 10, PIECE])}
        R = sb("s4_R", [P, 2, 2, GP])
        cross = sb("s4_cross", [P, 2, GP])
        hankel = sb("s4_hankel", [P, LOADS, BLOCK, P])
        UT = sb("s4_UT", [P, 2, 2, P])
        yT = sb("s4_yT", [P, 4, P])
        Kz = sb("s4_Kz", [P, 2, ROWS, 16 * SIDE + 1])
        Krow = sb("s4_Krow", [P, KROW])
        skip = sb("s4_skip", [P, GROUPS])
        tp = [ps(f"s4_tp{k}", [P, 4, P]) for k in range(2)]
        utp = ps("s4_utp", [P, 2, 2, P])
        stp = ps("s4_stp", [P, 2, 2, P])
        ytp = [ps(f"s4_ytp{k}", [P, 4, P]) for k in range(2)]
        yp = ps("s4_yp", [P, OUT, CHUNKS])
        ksp = ps("s4_ksp", [P, P])
        s = {n: sem("s4_" + n) for n in (
            "skip_in", "row_set", "Kz_set", "Kz_ready", "Q_dve", "Q_pool", "turned", "QT_ready", "Xg_ready", "U_done", "UT_ready", "U_turned",
            "U_copied", "K_done", "K_row", "K_stored", "h_in0", "h_in1", "h_in2", "h_in3", "h_used", "S_ready", "y_done", "yT_ready", "y_turned",
            "y_copied", "passed")}
        YG = GROUP // OUT
        HG = GROUP // BLOCK
        TG = GP // 2
        UG = GP // UP

        def table(eng, ops, m, b, lo, hi, temp):
            g = 2 * m + b
            count = hi - lo
            eng.wait_ge(s["y_done"], YG * g + -(-2 * hi // OUT))
            eng.sem_inc(s["passed"], 1)

            def factor(level, part):
                return W[:, level, part, bass.ds(GP * g + lo, count)]

            for part in range(2):
                ops.tensor_copy(Q[:, b, part, lo:hi, 0], root[:, part, bass.ds(GP * g + lo, count)])
            eng.drain()
            for level in range(LEVELS + 1):
                n = 1 << level
                for at in range(0, n if level < LEVELS else 1, PIECE):
                    w = min(PIECE, n - at) if level < LEVELS else 1
                    for part in range(2):
                        ops.tensor_tensor(temp[:, part, :, 0:count, 0:w], Q[:, b, :, lo:hi, at:at + w],
                                          factor(level, part).unsqueeze(1).unsqueeze(3).broadcast_to([P, 2, count, w]), ALU.mult)
                    eng.drain()
                    ops.tensor_tensor(Q[:, b, 0, lo:hi, n + at:n + at + w], temp[:, 0, 0, 0:count, 0:w], temp[:, 1, 1, 0:count, 0:w], ALU.subtract)
                    last = ops.tensor_tensor(Q[:, b, 1, lo:hi, n + at:n + at + w], temp[:, 0, 1, 0:count, 0:w], temp[:, 1, 0, 0:count, 0:w], ALU.add)
                    if level < LEVELS:
                        eng.drain()
            return last

        with nc.Block() as block:
            @block.sync
            def _(sp):
                by_row = a["D_skip"].rearrange("(g r x) -> x r g", r=ROWS, x=2 * SIDE)
                for j in range(SIDE):
                    for e in range(2):
                        at = CHUNKS * j + ROWS * e
                        sp.dma_start(skip[at:at + ROWS, :], by_row[2 * j + e], allow_slow_non_contiguous=True).then_inc(s["skip_in"], 16)
                K_by_row = dram["K"].rearrange("(g r x) q -> g x r q", r=ROWS, x=2 * SIDE)
                with sp.Fori(0, GROUPS // 2) as i:
                    for b in range(2):
                        g = 2 * i + b
                        sp.wait_ge(s["K_row"], g + 2)
                        sp.sem_inc(s["passed"], 1)
                        for j in range(SIDE):
                            for e in range(2):
                                at = CHUNKS * j + ROWS * e
                                sp.dma_start(K_by_row[g, 2 * j + e, :, :], Krow[at:at + ROWS, :]).then_inc(s["K_stored"], 16)
                        sp.wait_ge(s["K_stored"], 16 * 2 * SIDE * (g + 1))
                        sp.sem_inc(s["passed"], 1)
                        for j in range(HG):
                            sp.wait_ge(s["h_used"], HG * g + j + 1)
                            sp.sem_inc(s["passed"], 1)
                            rows = dram["K"][bass.ds(GROUP * g + j * BLOCK, BLOCK), :]
                            skewed = bass.AP(tensor=rows.tensor, offset=rows.offset, ap=[[1, P], [KROW, BLOCK], [1, P]])
                            sp.dma_start(hankel[:, j % LOADS], skewed).then_inc(s[f"h_in{j % LOADS}"], 16)

            @block.gpsimd
            def _(pool):
                nc.gpsimd.memset(Krow[:], 0.0).then_inc(s["row_set"], 1)
                nc.gpsimd.memset(S[:, :, :, 0, :], 0.0).then_inc(s["row_set"], 1)
                with pool.Fori(0, GROUPS // 2) as i:
                    for b in range(2):
                        for lo, hi in SHARES["pool"]:
                            table(pool, nc.gpsimd, i, b, lo, hi, M["pool"]).then_inc(s["Q_pool"], 1)
                            pool.drain()

            @block.vector
            def _(dve):
                def kernel_weights(m, b, first=False):
                    g = 2 * m + b
                    if not first:
                        dve.wait_ge(s["K_done"], g)
                        dve.sem_inc(s["passed"], 1)
                    for part in range(2):
                        for e in range(2):
                            at = slice(NS * e, NS * (e + 1))
                            last = nc.vector.tensor_scalar(Kz[at, part, :, ROWS * e:ROWS * e + 16 * (SIDE - 1) + 1:16],
                                                           root[at, part, bass.ds(GP * g, GP)].rearrange("p (r j) -> p r j", j=SIDE),
                                                           -1.0 if part else 1.0, None, ALU.mult)
                    last.then_inc(s["Kz_ready"], 1)

                def carry(m, b):
                    g = 2 * m + b
                    dve.drain()
                    dve.wait_ge(s["U_copied"], UG * (g + 1))
                    dve.sem_inc(s["passed"], 1)
                    real = W[:, LEVELS, 0, bass.ds(GP * g, GP)].unsqueeze(1).broadcast_to([P, 2, GP])
                    for part in range(2):
                        nc.vector.tensor_scalar(cross[:, part], W[:, LEVELS, 1, bass.ds(GP * g, GP)], -1.0 if part else 1.0, None, ALU.mult)
                    dve.drain()
                    for c in range(2, CHUNKS):
                        nc.vector.tensor_tensor(R[:, 0], S[:, b, :, c - 1, :], real, ALU.mult)
                        nc.vector.tensor_tensor(R[:, 1], S[:, b, ::-1, c - 1, :], cross[:], ALU.mult)
                        dve.drain()
                        nc.vector.tensor_tensor(R[:, 0], R[:, 0], R[:, 1], ALU.add)
                        dve.drain()
                        last = nc.vector.tensor_tensor(S[:, b, :, c, :], S[:, b, :, c, :], R[:, 0], ALU.add)
                        if c < CHUNKS - 1:
                            dve.drain()
                    last.then_inc(s["S_ready"], 1)

                def tables(m, b):
                    for lo, hi in SHARES["dve"]:
                        table(dve, nc.vector, m, b, lo, hi, M["dve"]).then_inc(s["Q_dve"], 1)

                dve.sem_inc(s["y_done"], 2 * YG)
                nc.vector.memset(Kz[:], 0.0)
                tables(0, 0)
                dve.drain()
                kernel_weights(0, 0, first=True)
                with dve.Fori(0, GROUPS // 2 - 1) as i:
                    for b in range(2):
                        tables(*after(i, b))
                        kernel_weights(*after(i, b))
                        carry(i, b)
                tables(GROUPS // 2 - 1, 1)
                kernel_weights(GROUPS // 2 - 1, 1)
                carry(GROUPS // 2 - 1, 0)
                carry(GROUPS // 2 - 1, 1)

            @block.scalar
            def _(act):
                act.sem_inc(s["QT_ready"], 2)
                act.sem_inc(s["yT_ready"], 2)
                act.sem_inc(s["K_row"], 1)
                act.wait_ge(s["skip_in"], 16 * 2 * SIDE)
                act.wait_ge(s["row_set"], 2)

                def gather(m, b, first=False):
                    g = 2 * m + b
                    act.wait_ge(s["y_done"], YG * (g + 1))
                    act.sem_inc(s["passed"], 1)
                    nc.scalar.activation(Xg[:, b].rearrange("p d c -> p c d"), X[:, :, bass.ds(GROUP * g, GROUP)],
                                         ACT.Copy).then_inc(s["Xg_ready"], 1)
                    for j in range(TG):
                        act.wait_ge(s["turned"], TG * g + j + 1)
                        nc.scalar.activation(QT[:, j % 2], tp[j % 2][:], ACT.Copy).then_inc(s["QT_ready"], 1)
                        if j % 4 == 1 and j > 4:
                            copy_gathered(g, j // 4 - 1)
                        if j % 4 == 3 and j > 4:
                            copy_states(g, b, j // 4 - 1)
                    copy_gathered(g, UG - 1)
                    act.wait_ge(s["K_done"], g + 1)
                    if not first:
                        act.sem_inc(s["passed"], 1)
                        act.wait_ge(s["K_stored"], 16 * 2 * SIDE * g)
                    act.sem_inc(s["passed"], 1)
                    for j in range(SIDE):
                        at = slice(CHUNKS * j, CHUNKS * j + 2 * ROWS)
                        nc.scalar.activation(Krow[at, P:KROW - 1], ksp[at, 1:P], ACT.Copy)
                        last = nc.scalar.activation(Krow[at, P - 1:P], ksp[at, 0:1], ACT.Identity, bias=skip[at, bass.ds(g, 1)])
                    last.then_inc(s["K_row"], 1)
                    copy_states(g, b, UG - 1)

                def copy_gathered(g, k):
                    act.wait_ge(s["U_done"], UG * g + k + 1)
                    nc.scalar.activation(UT[:], utp[:], ACT.Copy).then_inc(s["UT_ready"], 1)

                def copy_states(g, b, k):
                    act.wait_ge(s["U_turned"], UG * g + k + 1)
                    for part in range(2):
                        last = nc.scalar.activation(S[:, b, part, 1:CHUNKS + 1, UP * k:UP * (k + 1)].rearrange("p c (q k) -> p q k c", k=SIDE),
                                                    stp[:, :, part].rearrange("p q (k c) -> p q k c", k=SIDE), ACT.Copy,
                                                    scale=-1.0 if part else 1.0)
                    last.then_inc(s["U_copied"], 1)

                def spread(m, b):
                    g = 2 * m + b
                    for j in range(YG + 1):
                        if j < YG:
                            act.wait_ge(s["y_done"], YG * g + j + 1 + 2 * YG)
                            if j:
                                act.sem_inc(s["passed"], 1)
                                act.wait_ge(s["y_turned"], YG * g + j)
                            elif not (isinstance(g, int) and g == 0):
                                act.sem_inc(s["passed"], 1)
                                act.wait_ge(s["y_turned"], YG * g)
                            nc.scalar.activation(yT[:], ytp[j % 2][:], ACT.Copy).then_inc(s["yT_ready"], 1)
                        if j:
                            act.wait_ge(s["y_turned"], YG * g + j)
                            act.sem_inc(s["passed"], 1)
                            nc.scalar.activation(X[:, :, bass.ds(GROUP * g + (j - 1) * OUT, OUT)], yp[:].rearrange("p d c -> p c d"),
                                                 ACT.Copy).then_inc(s["y_copied"], 1)

                gather(0, 0, first=True)
                with act.Fori(0, GROUPS // 2 - 1) as i:
                    for b in range(2):
                        gather(*after(i, b))
                        spread(i, b)
                gather(GROUPS // 2 - 1, 1)
                spread(GROUPS // 2 - 1, 0)
                spread(GROUPS // 2 - 1, 1)
                act.wait_ge(s["y_copied"], YG * GROUPS + 1)

            @block.tensor
            def _(pe):
                pe.sem_inc(s["h_used"], LOADS)
                pe.sem_inc(s["y_copied"], 1)

                def gather(m, b):
                    g = 2 * m + b

                    def turn_tables(j):
                        first_pair = 2 * j
                        if first_pair == 0:
                            pe.wait_ge(s["Q_dve"], g + 1)
                        for n, (lo, _) in enumerate(SHARES["pool"]):
                            if first_pair == lo:
                                pe.wait_ge(s["Q_pool"], 2 * g + n + 1)
                        pe.wait_ge(s["QT_ready"], TG * g + j + 1)
                        for k in range(2):
                            for part in range(2):
                                last = nc.tensor.transpose(tp[j % 2][:, 2 * k + part, :], Q[:, b, part, 2 * j + k, 1:P + 1], const["ident"][:])
                        last.then_inc(s["turned"], 1)

                    def sum_kernel(j):
                        if j == 0:
                            pe.wait_ge(s["Kz_ready"], g + 1)
                            pe.wait_ge(s["K_row"], g + 1)
                        for part in range(2):
                            for k in range(2):
                                pair = 2 * j + k
                                at = CHUNKS * (pair % SIDE)
                                last = nc.tensor.matmul(ksp[at:at + 2 * ROWS, :], lhsT=Kz[:, part].rearrange("p r x -> p (r x)")[:, 16 * pair:16 * pair + 16],
                                                        rhs=Q[:, b, part, pair, 0:P], start=(pair < SIDE and part == 0),
                                                        stop=(pair >= GP - SIDE and part == 1))
                        if j == TG - 1:
                            last.then_inc(s["K_done"], 1)

                    def turn_states(k):
                        pe.wait_ge(s["UT_ready"], UG * g + k + 1)
                        if k:
                            pe.wait_ge(s["U_copied"], UG * g + k)
                        for h in range(2):
                            for part in range(2):
                                last = nc.tensor.transpose(stp[:, h, part, :], UT[:, h, part, :], const["ident"][:])
                        last.then_inc(s["U_turned"], 1)

                    turn_tables(0)
                    for j in range(TG):
                        if j < TG - 1:
                            turn_tables(j + 1)
                        sum_kernel(j)
                        pe.wait_ge(s["QT_ready"], TG * g + j + 3)
                        if j == 0:
                            pe.wait_ge(s["Xg_ready"], g + 1)
                        elif j % 4 == 0:
                            pe.wait_ge(s["UT_ready"], UG * g + j // 4)
                        for e in range(2):
                            for k in range(2):
                                pair = 2 * j + k
                                at = CHUNKS * (pair % SIDE)
                                last = nc.tensor.matmul(utp[at:at + CHUNKS, pair // SIDE % 2, :, NS * e:NS * (e + 1)],
                                                        lhsT=Xg[:, b, 2 * pair + e, :], rhs=QT[:, j % 2, 2 * k:2 * k + 2, NS * e:NS * (e + 1)],
                                                        start=True, stop=True)
                        if j % 4 == 3:
                            last.then_inc(s["U_done"], 1)
                        if j % 4 == 2 and j > 4:
                            turn_states(j // 4 - 1)
                    turn_states(UG - 1)

                def spread(m, b):
                    g = 2 * m + b
                    pe.wait_ge(s["S_ready"], g + 1)

                    def products(j):
                        pe.wait_ge(s["yT_ready"], YG * g + j + 1)
                        for q in range(OUT // SIDE):
                            load = j * (OUT // SIDE) + q
                            channels = [SIDE * load + k for k in range(SIDE)]
                            pe.wait_ge(s[f"h_in{load % LOADS}"], 16 * (HG // LOADS * g + load // LOADS + 1))
                            for k, d in enumerate(channels):
                                last = nc.tensor.matmul(ytp[j % 2][CHUNKS * k:CHUNKS * (k + 1), q, :], lhsT=Xg[:, b, d, :],
                                                        rhs=hankel[:, load % LOADS, k, :], start=True, stop=False)
                            last.then_inc(s["h_used"], 1)
                            for part in range(2):
                                for k, d in enumerate(channels):
                                    at = slice(NS * (d % 2), NS * (d % 2 + 1))
                                    last = nc.tensor.matmul(ytp[j % 2][CHUNKS * k:CHUNKS * (k + 1), q, :], lhsT=S[at, b, part, 0:CHUNKS, d // 2],
                                                            rhs=Q[at, b, part, d // 2, 0:P], start=False, stop=(part == 1))
                        last.then_inc(s["y_done"], 1)

                    def turn(j):
                        pe.wait_ge(s["yT_ready"], YG * g + j + 3)
                        pe.wait_ge(s["y_copied"], YG * g + j + 1)
                        for q in range(OUT // SIDE):
                            last = nc.tensor.transpose(yp[:, SIDE * q:SIDE * (q + 1), :].rearrange("p d c -> p (d c)"), yT[:, q, :], const["ident"][:])
                        last.then_inc(s["y_turned"], 1)

                    products(0)
                    for j in range(YG):
                        if j + 1 < YG:
                            products(j + 1)
                        turn(j)

                gather(0, 0)
                with pe.Fori(0, GROUPS // 2 - 1) as i:
                    for b in range(2):
                        gather(*after(i, b))
                        spread(i, b)
                gather(GROUPS // 2 - 1, 1)
                spread(GROUPS // 2 - 1, 0)
                spread(GROUPS // 2 - 1, 1)


LEAST = 1e-5
LEVEL = 127.0


def fold_ffn(nc, sem, const, a, W1, W2, b1):
    scope, sb, ps = phase_scope(nc)
    with scope:
        gain = sb("fold_gain", [P, DC])
        offset = sb("fold_offset", [P, DC])
        bp = ps("fold_bp", [P, HID // P])
        s = {n: sem("fold_" + n) for n in ("in", "offset_done", "gained")}

        with nc.Block() as block:
            @block.sync
            def _(sp):
                sp.dma_start(W1[:], a["W1"].rearrange("(c p) n -> p c n", p=P)).then_inc(s["in"], 16)
                sp.dma_start(gain[:], a["g_ffn"].rearrange("(c p) -> p c", p=P), allow_slow_non_contiguous=True).then_inc(s["in"], 16)
                sp.dma_start(offset[:], a["b_ffn"].rearrange("(c p) -> p c", p=P), allow_slow_non_contiguous=True).then_inc(s["in"], 16)
                sp.dma_start(b1[:], a["b1"].rearrange("(f p) -> p f", p=P), allow_slow_non_contiguous=True).then_inc(s["in"], 16)
                sp.dma_start(W2[:], a["W2"].rearrange("(f p) n -> p f n", p=P)).then_inc(s["in"], 16)

            @block.tensor
            def _(pe):
                pe.wait_ge(s["in"], 16 * 5)
                for f in range(HID // P):
                    for c in range(DC):
                        last = nc.tensor.matmul(bp[:, f:f + 1], lhsT=W1[:, c, f * P:(f + 1) * P], rhs=offset[:, c:c + 1],
                                                start=(c == 0), stop=(c == DC - 1))
                last.then_inc(s["offset_done"], 1)

            @block.vector
            def _(dve):
                dve.wait_ge(s["offset_done"], 1)
                nc.vector.tensor_tensor(b1[:], bp[:], b1[:], ALU.add).then_inc(s["gained"], 1)
                for c in range(DC):
                    nc.vector.tensor_scalar(W1[:, c, :], W1[:, c, :], gain[:, c:c + 1], None, ALU.mult).then_inc(s["gained"], 1)
                dve.wait_ge(s["gained"], DC + 1)


def feed_forward(nc, sem, const, a, wf, fb, W1, W2, b1, Y, qstep, dram):
    scope, sb, ps = phase_scope(nc)
    QUADS = TILES // QUAD
    FC = HID // P
    TURN_U, FILM, TURN_Q = (2, 5, 8, 11), (3, 6, 9, 12), (7, 10, 13, 14)
    with scope:
        rows = {n: sb("ff_" + n, [P, D]) for n in ("b2", "g_norm_out", "b_norm_out")}
        u = sb("ff_u", [P, DV])
        uT = sb("ff_uT", [P, VC, P])
        xt = sb("ff_xt", [P, 2, QUAD, D])
        x = sb("ff_x", [P, QUAD, D])
        h = sb("ff_h", [P, 2, D])
        hT = sb("ff_hT", [P, DC, QUAD * P])
        act_out = sb("ff_gelu", [P, 2, QUAD * P])
        sc = sb("ff_scale", [P, D])
        q = sb("ff_q", [P, QUAD, D], BF16)
        qT = sb("ff_qT", [P, DC, QUAD * P], BF16)
        stats = {n: sb("ff_stats_" + n, [P, QUAD, 6]) for n in ("sum", "out", "x")}
        mv = {n: sb("ff_mv_" + n, [P, QUAD, 2]) for n in ("sum", "out", "x")}
        rstd = {n: sb("ff_rstd_" + n, [P, QUAD]) for n in ("sum", "out", "x")}
        most = sb("ff_most", [P, QUAD])
        steps = sb("ff_steps", [P, QUAD])
        zero = sb("ff_zero", [P, DC], BF16)
        fl = [ps(f"ff_fl{k}", [P, BANK]) for k in range(2)]
        fp = [ps(f"ff_fp{k}", [P, BANK]) for k in range(2)]
        acc = ps("ff_acc", [P, QUAD, BANK])
        s = {n: sem("ff_" + n) for n in (
            "rows_in", "u_in", "xt_in0", "xt_in1", "x_in", "u_turned", "uT_ready", "film_done", "film_read", "factors", "modulated",
            "sum_wanted", "sum_ready", "h_ready", "h_turned", "hT_ready", "hidden", "gelu_done", "acc_done", "acc_read",
            "out_wanted", "out_ready", "out_normed", "x_ready", "xb_ready", "x_wanted", "x_root", "x_read", "q_ready", "q_turned", "qT_ready",
            "xt_free", "qT_stored", "x_stored", "biased", "edges", "passed")}

        with nc.Block() as block:
            @block.sync
            def _(sp):
                for n in rows:
                    sp.dma_start(rows[n][:], a[n].partition_broadcast(P)).then_inc(s["rows_in"], 16)
                xt_q = dram["xt"].rearrange("(q k p) d -> q p k d", k=QUAD, p=P)
                x_q = a["x"].rearrange("(q k p) d -> q p k d", k=QUAD, p=P)
                x2_q = dram["x2"].rearrange("(q k p) d -> q p k d", k=QUAD, p=P)

                def load_u(m, b, tiles):
                    for k in tiles:
                        n = QUAD * (2 * m + b) + k
                        sp.wait_ge(s["u_turned"], n + 1)
                        sp.sem_inc(s["passed"], 1)
                        sp.dma_start(u[:], dram["u"][bass.ts(n, P), :]).then_inc(s["u_in"], 16)

                def load_xt(m, b):
                    g = 2 * m + b
                    sp.wait_ge(s["xt_free"], g + 1)
                    sp.sem_inc(s["passed"], 1)
                    sp.dma_start(xt[:, b], xt_q[g, :, :, :]).then_inc(s[f"xt_in{b}"], 16)

                def load_back(m, b, first=False):
                    g = 2 * m + b
                    if not first:
                        sp.wait_ge(s["x_read"], g)
                        sp.sem_inc(s["passed"], 1)
                        sp.wait_ge(s["x_stored"], 16 * g)
                        sp.sem_inc(s["passed"], 1)
                    sp.dma_start(x[:], x_q[g, :, :, :]).then_inc(s["x_in"], 16)

                def store(m, b):
                    g = 2 * m + b
                    sp.wait_ge(s["x_ready"], QUAD * (g + 1))
                    sp.sem_inc(s["passed"], 1)
                    sp.dma_start(x2_q[g, :, :, :], x[:]).then_inc(s["x_stored"], 16)

                load_xt(0, 0)
                load_u(0, 0, range(QUAD))
                load_xt(0, 1)
                load_back(0, 0, first=True)
                load_u(0, 1, range(QUAD))
                with sp.Fori(0, QUADS // 2 - 1) as i:
                    for b in range(2):
                        load_u(i + 1, b, (0,))
                        store(i, b)
                        load_back(*after(i, b))
                        load_xt(i + 1, b)
                        load_u(i + 1, b, range(1, QUAD))
                store(QUADS // 2 - 1, 0)
                load_back(QUADS // 2 - 1, 1)
                store(QUADS // 2 - 1, 1)
                sp.wait_ge(s["x_stored"], 16 * QUADS)

            @block.gpsimd
            def _(pool):
                nc.gpsimd.memset(zero[:], 0.0).then_inc(s["edges"], 1)
                pool.wait_ge(s["rows_in"], 16 * 3)

                def front(m, b):
                    g = 2 * m + b
                    for k in range(QUAD):
                        n = QUAD * g + k
                        pool.wait_ge(s["factors"], n + 1)
                        pool.sem_inc(s["passed"], 1)
                        nc.gpsimd.tensor_tensor(sc[:].unsqueeze(1), Y[:, bass.ds(n, 1), :], sc[:].unsqueeze(1), ALU.mult)
                        nc.gpsimd.tensor_tensor(xt[:, b, k], xt[:, b, k], fb[:, D:2 * D], ALU.add)
                        pool.drain()
                        nc.gpsimd.tensor_tensor(xt[:, b, k], xt[:, b, k], sc[:], ALU.add).then_inc(s["modulated"], 1)

                def bias(m, b):
                    g = 2 * m + b
                    for k in range(QUAD):
                        pool.wait_ge(s["h_ready"], QUAD * g + k + 1)
                        pool.sem_inc(s["passed"], 1)
                        last = nc.gpsimd.tensor_tensor(xt[:, b, k], xt[:, b, k], rows["b2"][:], ALU.add)
                    last.then_inc(s["biased"], 1)

                def back(m, b):
                    g = 2 * m + b
                    pool.wait_ge(s["x_in"], 16 * (g + 1))
                    pool.sem_inc(s["passed"], 1)
                    nc.gpsimd.tensor_tensor(x[:], x[:], rows["b_norm_out"][:].unsqueeze(1).broadcast_to([P, QUAD, D]), ALU.add)
                    for k in range(QUAD):
                        pool.wait_ge(s["out_normed"], QUAD * g + k + 1)
                        pool.sem_inc(s["passed"], 1)
                        nc.gpsimd.tensor_tensor(xt[:, b, k], xt[:, b, k], rows["g_norm_out"][:], ALU.mult)
                        pool.drain()
                        nc.gpsimd.tensor_tensor(x[:, k], x[:, k], xt[:, b, k], ALU.add).then_inc(s["x_ready"], 1)

                front(0, 0)
                bias(0, 0)
                front(0, 1)
                bias(0, 1)
                with pool.Fori(0, QUADS // 2 - 1) as i:
                    for b in range(2):
                        back(i, b)
                        front(i + 1, b)
                        bias(i + 1, b)
                back(QUADS // 2 - 1, 0)
                back(QUADS // 2 - 1, 1)

            @block.vector
            def _(dve):
                def front(m, b):
                    g = 2 * m + b
                    for k in range(QUAD):
                        n = QUAD * g + k
                        dve.wait_ge(s["film_done"], n + 1)
                        dve.sem_inc(s["passed"], 1)
                        if k:
                            dve.wait_ge(s["modulated"], n)
                        else:
                            dve.wait_ge(s[f"xt_in{b}"], 16 * (m + 1))
                        nc.vector.tensor_tensor(sc[:], fl[0][:], fb[:, 0:D], ALU.add)
                        nc.vector.tensor_tensor(xt[:, b, k], fl[1][:], xt[:, b, k], ALU.add)
                        dve.drain()
                        dve.sem_inc(s["film_read"], 1)
                        dve.sem_inc(s["factors"], 1)
                    for k in range(QUAD):
                        dve.wait_ge(s["modulated"], QUAD * g + k + 1)
                        dve.sem_inc(s["passed"], 1)
                        nc.vector.bn_stats(stats["sum"][:, k, :], xt[:, b, k, :])
                    norm_factors("sum", g)
                    for k in range(QUAD):
                        dve.wait_ge(s["h_turned"], QUAD * g + k + 1)
                        nc.vector.tensor_scalar(h[:, k % 2], xt[:, b, k], mv["sum"][:, k, 0:1], rstd["sum"][:, k:k + 1],
                                                ALU.subtract, ALU.mult).then_inc(s["h_ready"], 1)

                def norm_factors(name, g):
                    dve.drain()
                    for k in range(QUAD):
                        last = nc.vector.bn_aggr(mv[name][:, k, :], stats[name][:, k, :])
                    last.then_inc(s[name + "_wanted"], 1)
                    dve.wait_ge(s[{"sum": "sum_ready", "out": "out_ready", "x": "x_root"}[name]], g + 1)
                    nc.vector.reciprocal(rstd[name][:], rstd[name][:])
                    dve.drain()

                def back(m, b):
                    g = 2 * m + b
                    dve.wait_ge(s["acc_done"], g + 1)
                    dve.sem_inc(s["passed"], 1)
                    dve.wait_ge(s["biased"], g + 1)
                    for k in range(QUAD):
                        last = nc.vector.tensor_tensor(xt[:, b, k], acc[:, k, :], xt[:, b, k], ALU.add)
                    last.then_inc(s["acc_read"], 1)
                    dve.drain()
                    for k in range(QUAD):
                        nc.vector.bn_stats(stats["out"][:, k, :], xt[:, b, k, :])
                    norm_factors("out", g)
                    for k in range(QUAD):
                        nc.vector.tensor_scalar(xt[:, b, k], xt[:, b, k], mv["out"][:, k, 0:1], rstd["out"][:, k:k + 1],
                                                ALU.subtract, ALU.mult).then_inc(s["out_normed"], 1)
                    for k in range(QUAD):
                        dve.wait_ge(s["x_ready"], QUAD * g + k + 1)
                        dve.sem_inc(s["passed"], 1)
                        nc.vector.bn_stats(stats["x"][:, k, :], x[:, k, :])
                    norm_factors("x", g)
                    for k in range(QUAD):
                        nc.vector.tensor_scalar(xt[:, b, k], x[:, k], mv["x"][:, k, 0:1], rstd["x"][:, k:k + 1], ALU.subtract, ALU.mult)
                    dve.drain()
                    dve.sem_inc(s["x_read"], 1)
                    nc.vector.tensor_reduce(most[:], xt[:, b], AX.X, ALU.max, apply_absolute_value=True)
                    dve.drain()
                    nc.vector.tensor_scalar(most[:], most[:], LEAST, None, ALU.max)
                    dve.drain()
                    nc.vector.tensor_scalar(qstep[:, bass.ds(QUAD * g, QUAD)], most[:], 1.0 / LEVEL, None, ALU.mult)
                    nc.vector.reciprocal(steps[:], most[:])
                    dve.drain()
                    nc.vector.tensor_scalar(steps[:], steps[:], LEVEL, None, ALU.mult)
                    dve.drain()
                    for k in range(QUAD):
                        nc.vector.tensor_scalar(xt[:, b, k], xt[:, b, k], steps[:, k:k + 1], ROUND, ALU.mult, ALU.add)
                    dve.drain()
                    for k in range(QUAD):
                        dve.wait_ge(s["q_turned"], QUAD * g + k + 1)
                        nc.vector.tensor_scalar(q[:, k], xt[:, b, k], ROUND, None, ALU.subtract).then_inc(s["q_ready"], 1)
                    dve.drain()
                    dve.sem_inc(s["xt_free"], 1)

                dve.sem_inc(s["xt_free"], 2)
                front(0, 0)
                front(0, 1)
                with dve.Fori(0, QUADS // 2 - 1) as i:
                    for b in range(2):
                        back(i, b)
                        front(i + 1, b)
                back(QUADS // 2 - 1, 0)
                back(QUADS // 2 - 1, 1)

            @block.scalar
            def _(act):
                act.sem_inc(s["qT_ready"], 1)
                act.sem_inc(s["hT_ready"], 2)
                act.wait_ge(s["edges"], 1)
                act.dma_start(dram["qT"][:, :, 0], zero[:], allow_slow_non_contiguous=True).then_inc(s["qT_stored"], 16)
                act.dma_start(dram["qT"][:, :, T + 1], zero[:], allow_slow_non_contiguous=True).then_inc(s["qT_stored"], 16)

                def root(name, ready, g):
                    act.wait_ge(s[name + "_wanted"], g + 1)
                    nc.scalar.activation(rstd[name][:], mv[name][:, :, 1], ACT.Sqrt, bias=const["eps"][:, 0:1]).then_inc(s[ready], 1)

                def copy_u(g, k):
                    act.wait_ge(s["u_turned"], QUAD * g + k + 1 + 1)
                    nc.scalar.activation(uT[:], fl[0][:, 0:DV].rearrange("p (c t) -> p c t", t=P), ACT.Copy).then_inc(s["uT_ready"], 1)

                def copy_h(g, k):
                    act.wait_ge(s["h_turned"], QUAD * g + k + 1 + 2)
                    nc.scalar.activation(hT[:, :, k * P:(k + 1) * P], fl[k % 2][:].rearrange("p (c t) -> p c t", t=P), ACT.Copy).then_inc(s["hT_ready"], 1)

                def copy_q(g, k):
                    if k == 0:
                        act.wait_ge(s["qT_stored"], 16 * (g + 2))
                        act.sem_inc(s["passed"], 1)
                    act.wait_ge(s["q_turned"], QUAD * (g + 1) + k + 1)
                    nc.scalar.activation(qT[:, :, k * P:(k + 1) * P], fl[1][:].bitcast(BF16)[:, 0:D].rearrange("p (c t) -> p c t", t=P),
                                         ACT.Copy).then_inc(s["qT_ready"], 1)
                    if k == QUAD - 1:
                        act.wait_ge(s["qT_ready"], QUAD * (g + 1) + 1)
                        act.sem_inc(s["passed"], 1)
                        act.dma_start(dram["qT"][:, :, bass.ds(QUAD * P * g + 1, QUAD * P)], qT[:]).then_inc(s["qT_stored"], 16)

                def turn(m, b, front=True, back=True):
                    g = 2 * m + b
                    old, new = 2 * before(m, b)[0] + before(m, b)[1], 2 * after(m, b)[0] + after(m, b)[1]
                    for k in range(QUAD):
                        copy_h(g, k)
                    for f in range(FC):
                        if front and f in TURN_U:
                            copy_u(new, TURN_U.index(f))
                        if back and f in TURN_Q:
                            copy_q(old, TURN_Q.index(f))
                        act.wait_ge(s["hidden"], FC * g + f + 1)
                        nc.scalar.activation(act_out[:, f % 2], fp[f % 2][:], ACT.Gelu, bias=b1[:, f:f + 1]).then_inc(s["gelu_done"], 1)
                        if back and f == 1:
                            root("out", "out_ready", old)
                        if back and f == 4:
                            root("x", "x_root", old)
                        if front and f == FC - 2:
                            root("sum", "sum_ready", new)

                for k in range(QUAD):
                    copy_u(0, k)
                root("sum", "sum_ready", 0)
                turn(0, 0, back=False)
                with act.Fori(0, QUADS // 2 - 1) as i:
                    turn(i, 1)
                    turn(i + 1, 0)
                turn(QUADS // 2 - 1, 1, front=False)
                root("out", "out_ready", QUADS - 1)
                root("x", "x_root", QUADS - 1)
                for k in range(QUAD):
                    copy_q(QUADS - 1, k)
                act.wait_ge(s["qT_stored"], 16 * (QUADS + 2))

            @block.tensor
            def _(pe):
                pe.sem_inc(s["u_turned"], 1)
                pe.sem_inc(s["h_turned"], 2)
                pe.sem_inc(s["q_turned"], QUAD)
                pe.sem_inc(s["gelu_done"], 2)

                def turn_u(m, b, k):
                    n = QUAD * (2 * m + b) + k
                    pe.wait_ge(s["u_in"], 16 * (n + 1))
                    if k:
                        pe.wait_ge(s["film_read"], n)
                    for c in range(VC):
                        last = nc.tensor.transpose(fl[0][:, c * P:(c + 1) * P], u[:, c * P:(c + 1) * P], const["ident"][:])
                    last.then_inc(s["u_turned"], 1)

                def film(m, b, k):
                    n = QUAD * (2 * m + b) + k
                    pe.wait_ge(s["uT_ready"], n + 1)
                    for half in range(2):
                        for c in range(VC):
                            last = nc.tensor.matmul(fl[half][:], lhsT=uT[:, c, :], rhs=wf[:, c, half * D:(half + 1) * D],
                                                    start=(c == 0), stop=(c == VC - 1))
                    last.then_inc(s["film_done"], 1)

                def turn_h(m, b, k):
                    n = QUAD * (2 * m + b) + k
                    pe.wait_ge(s["h_ready"], n + 1)
                    if k >= 2:
                        pe.wait_ge(s["hT_ready"], n + 1)
                    for c in range(DC):
                        last = nc.tensor.transpose(fl[k % 2][:, c * P:(c + 1) * P], h[:, k % 2, c * P:(c + 1) * P], const["ident"][:])
                    last.then_inc(s["h_turned"], 1)

                def turn_q(m, b, k):
                    n = QUAD * (2 * m + b) + k
                    pe.wait_ge(s["q_ready"], n + 1)
                    for c in range(DC):
                        last = nc.tensor.transpose(fl[1][:].bitcast(BF16)[:, c * P:(c + 1) * P], q[:, k, c * P:(c + 1) * P],
                                                   const["ident_bf"][:])
                    last.then_inc(s["q_turned"], 1)

                def second(m, b, f):
                    g = 2 * m + b
                    pe.wait_ge(s["gelu_done"], FC * g + f + 1 + 2)
                    if f == 0:
                        pe.wait_ge(s["acc_read"], g + 1)
                    for k in range(QUAD):
                        last = nc.tensor.matmul(acc[:, k, :], lhsT=act_out[:, f % 2, k * P:(k + 1) * P], rhs=W2[:, f, :],
                                                start=(f == 0), stop=(f == FC - 1))
                    if f == FC - 1:
                        last.then_inc(s["acc_done"], 1)

                def turn(m, b, front=True, back=True):
                    g = 2 * m + b
                    for k in range(QUAD):
                        if k == 1 and back:
                            pe.wait_ge(s["qT_ready"], QUAD * (g - 1) + 1)
                        turn_h(m, b, k)
                    pe.wait_ge(s["hT_ready"], QUAD * (g + 1) + 2)
                    for f in range(FC):
                        pe.wait_ge(s["gelu_done"], FC * g + f + 1)
                        for c in range(DC):
                            last = nc.tensor.matmul(fp[f % 2][:], lhsT=W1[:, c, f * P:(f + 1) * P], rhs=hT[:, c, :],
                                                    start=(c == 0), stop=(c == DC - 1))
                        last.then_inc(s["hidden"], 1)
                        if f:
                            second(m, b, f - 1)
                        if front and f in TURN_U:
                            turn_u(*after(m, b), TURN_U.index(f))
                        if front and f in FILM:
                            k = FILM.index(f)
                            if back and f > TURN_Q[0]:
                                done = sum(t < f for t in TURN_Q)
                                pe.wait_ge(s["qT_ready"], QUAD * (2 * before(m, b)[0] + before(m, b)[1]) + done + 1)
                            film(*after(m, b), k)
                        if back and f in TURN_Q:
                            k = TURN_Q.index(f)
                            done = sum(t < f for t in FILM)
                            if front:
                                pe.wait_ge(s["film_read"], QUAD * (2 * after(m, b)[0] + after(m, b)[1]) + done)
                            if k:
                                pe.wait_ge(s["qT_ready"], QUAD * (2 * before(m, b)[0] + before(m, b)[1]) + k + 1)
                            turn_q(*before(m, b), k)
                    second(m, b, FC - 1)

                pe.sem_inc(s["acc_read"], 1)
                pe.wait_ge(s["rows_in"], 16)
                for k in range(QUAD):
                    turn_u(0, 0, k)
                    film(0, 0, k)
                pe.wait_ge(s["film_read"], QUAD)
                turn(0, 0, back=False)
                with pe.Fori(0, QUADS // 2 - 1) as i:
                    turn(i, 1)
                    turn(i + 1, 0)
                turn(QUADS // 2 - 1, 1, front=False)
                for k in range(QUAD):
                    if k:
                        pe.wait_ge(s["qT_ready"], QUAD * (QUADS - 1) + k + 1)
                    turn_q(QUADS // 2 - 1, 1, k)


def quantise_weights(nc, sem, const, a, W1q, W2q, mean, qstep, rowstep):
    scope, sb, ps = phase_scope(nc)
    FC = HID // P
    with scope:
        w1 = sb("qw_w1", [P, FC, D])
        w2 = sb("qw_w2", [P, DC, HID])
        w1b = sb("qw_w1b", [P, FC, D], BF16)
        w2b = sb("qw_w2b", [P, DC, HID], BF16)
        part = sb("qw_part", [P, FC + DC])
        sums = sb("qw_sums", [P, 2])
        inverse = sb("qw_inverse", [P, 2])
        every = sb("qw_every", [P, P])
        diag = sb("qw_diag", [P, 2, QUAD, P])
        total = ps("qw_total", [P, 2])
        tp = [ps(f"qw_tp{k}", [P, 2 * BANK], BF16) for k in range(2)]
        rp = [ps(f"qw_rp{k}", [P, BANK]) for k in range(2)]
        s = {n: sem("qw_" + n) for n in ("in0", "in1", "summed", "totalled", "quantised", "turned", "copied", "diag_ready", "spread", "rows_copied",
                                         "mean_ready")}

        with nc.Block() as block:
            @block.sync
            def _(sp):
                sp.dma_start(w1[:], a["ffn_w1"].rearrange("(f p) d -> p f d", p=P)).then_inc(s["in0"], 16)
                sp.dma_start(w2[:], a["ffn_w2"].rearrange("(c p) f -> p c f", p=P)).then_inc(s["in1"], 16)

            @block.vector
            def _(dve):
                nc.vector.memset(every[:], 1.0)
                nc.vector.memset(rowstep[:, 0:1], 0.0)
                nc.vector.memset(rowstep[:, T + 1:T + 2], 0.0)
                dve.wait_ge(s["in0"], 16)
                nc.vector.tensor_reduce(part[:, 0:FC], w1[:], AX.X, ALU.add, apply_absolute_value=True)
                dve.wait_ge(s["in1"], 16)
                nc.vector.tensor_reduce(part[:, FC:FC + DC], w2[:], AX.X, ALU.add, apply_absolute_value=True)
                dve.drain()
                nc.vector.tensor_reduce(sums[:, 0:1], part[:, 0:FC], AX.X, ALU.add)
                nc.vector.tensor_reduce(sums[:, 1:2], part[:, FC:FC + DC], AX.X, ALU.add).then_inc(s["summed"], 1)
                dve.wait_ge(s["totalled"], 1)
                nc.vector.tensor_scalar(mean[:], total[:], 1.0 / (HID * D), LEAST, ALU.mult, ALU.max)
                dve.drain()
                nc.vector.reciprocal(inverse[:], mean[:]).then_inc(s["mean_ready"], 1)
                for q in range(TILES // QUAD):
                    if q >= 2:
                        dve.wait_ge(s["spread"], q - 1)
                    for k in range(QUAD):
                        n = QUAD * q + k
                        last = nc.vector.tensor_scalar(diag[:, q % 2, k, :], const["ident"][:], qstep[:, n:n + 1], None, ALU.mult)
                    last.then_inc(s["diag_ready"], 1)
                dve.drain()
                for j, (w, wb) in enumerate(((w1, w1b), (w2, w2b))):
                    nc.vector.tensor_scalar(w[:], w[:], inverse[:, j:j + 1], 1.0, ALU.mult, ALU.min)
                    dve.drain()
                    nc.vector.tensor_scalar(w[:], w[:], -1.0, ROUND, ALU.max, ALU.add)
                    dve.drain()
                    nc.vector.tensor_scalar(wb[:], w[:], ROUND, None, ALU.subtract).then_inc(s["quantised"], 1)

            @block.tensor
            def _(pe):
                pe.wait_ge(s["summed"], 1)
                nc.tensor.matmul(total[:], lhsT=every[:], rhs=sums[:], start=True, stop=True).then_inc(s["totalled"], 1)
                for q in range(TILES // QUAD):
                    pe.wait_ge(s["diag_ready"], q + 1)
                    if q >= 2:
                        pe.wait_ge(s["rows_copied"], q - 1)
                    nc.tensor.matmul(rp[q % 2][:], lhsT=every[:], rhs=diag[:, q % 2].rearrange("p k t -> p (k t)"),
                                     start=True, stop=True).then_inc(s["spread"], 1)
                for j in range(2):
                    pe.wait_ge(s["quantised"], j + 1)
                    for f in range(FC):
                        if FC * j + f >= 2:
                            pe.wait_ge(s["copied"], FC * j + f - 1)
                        for c in range(DC):
                            piece = w1b[:, f, c * P:(c + 1) * P] if j == 0 else w2b[:, c, f * P:(f + 1) * P]
                            last = nc.tensor.transpose(tp[f % 2][:, c * P:(c + 1) * P], piece, const["ident_bf"][:])
                        last.then_inc(s["turned"], 1)

            @block.scalar
            def _(act):
                act.wait_ge(s["mean_ready"], 1)
                for q in range(TILES // QUAD):
                    act.wait_ge(s["spread"], q + 1)
                    nc.scalar.activation(rowstep[:, 1 + q * BANK:1 + (q + 1) * BANK], rp[q % 2][:], ACT.Copy,
                                         scale=mean[:, 0:1]).then_inc(s["rows_copied"], 1)
                for j in range(2):
                    for f in range(FC):
                        act.wait_ge(s["turned"], FC * j + f + 1)
                        piece = tp[f % 2][:, 0:D]
                        if j == 0:
                            last = nc.scalar.activation(W1q[:, :, f * P:(f + 1) * P], piece.rearrange("p (c f) -> p c f", f=P), ACT.Copy)
                        else:
                            last = nc.scalar.activation(W2q[:, f, :], piece, ACT.Copy)
                        last.then_inc(s["copied"], 1)
                act.wait_ge(s["copied"], 2 * FC)


def bit_feed_forward(nc, sem, const, a, W1q, W2q, mean, rowstep, dram, out):
    scope, sb, ps = phase_scope(nc)
    FC = HID // P
    BT = 2 * P
    BLOCKS = T // BT
    HALO = BT + 2
    JC = FC // 2
    SCALED_AT = {4: range(0, 2), 5: range(2, 4), 6: range(4, 6), 7: range(6, 8)}
    with scope:
        taps = sb("bf_taps", [P, FC, 3])
        tap_bias = sb("bf_tap_bias", [P, FC])
        qin = sb("bf_qin", [P, 2, DC, HALO], BF16)
        x2 = sb("bf_x2", [P, 2, 2, D])
        hidden = sb("bf_hidden", [P, 2, 2, HALO])
        conv = sb("bf_conv", [P, 2, 2, BT])
        others = sb("bf_others", [P, 2, 2, BT])
        g = sb("bf_silu", [P, 2, FC, BT])
        gq = sb("bf_gq", [P, FC, BT], BF16)
        top = sb("bf_top", [P, BT])
        most = sb("bf_most", [P, 2])
        step = sb("bf_step", [P, 2])
        undo = sb("bf_undo", [P, 2, 2])
        diag = sb("bf_diag", [P, 2, P])
        every = sb("bf_every", [P, P])
        scale = sb("bf_scale", [P, BT])
        y = sb("bf_y", [P, 2, 2, D])
        hp = [ps(f"bf_hp{k}", [P, 2, BANK]) for k in range(2)]
        op = ps("bf_op", [P, 2, BANK])
        mp = ps("bf_mp", [P, 2, P])
        sp_ = ps("bf_sp", [P, BANK])
        s = {n: sem("bf_" + n) for n in (
            "taps_in", "q_in0", "q_in1", "x_in0", "x_in1", "every_set", "first_done", "dequantised", "tapped0", "tapped", "tapped2", "silu_done", "top_done",
            "top_turned", "steps_ready", "steps_spread", "scale_ready", "scaled", "quantised", "second_done", "y_ready", "stored0", "stored1", "passed",
            "block_done")}
        x2_b = dram["x2"].rearrange("(n k p) d -> n p k d", k=2, p=P)
        out_b = out.rearrange("(n k p) d -> n p k d", k=2, p=P)

        with nc.Block() as block:
            @block.sync
            def _(sp):
                sp.dma_start(taps[:], a["conv_w"].rearrange("(f p) o k -> p f (o k)", p=P), allow_slow_non_contiguous=True).then_inc(s["taps_in"], 16)
                sp.dma_start(tap_bias[:], a["conv_b"].rearrange("(f p) -> p f", p=P), allow_slow_non_contiguous=True).then_inc(s["taps_in"], 16)

                def load(m, b):
                    n = 2 * m + b
                    sp.wait_ge(s["block_done"], n + 1)
                    sp.sem_inc(s["passed"], 1)
                    sp.dma_start(qin[:, b], dram["qT"][:, :, bass.ds(BT * n, HALO)]).then_inc(s[f"q_in{b}"], 16)

                def load_x(m, b):
                    n = 2 * m + b
                    sp.wait_ge(s["y_ready"], n + 1)
                    sp.sem_inc(s["passed"], 1)
                    sp.dma_start(x2[:, b], x2_b[n, :, :, :]).then_inc(s[f"x_in{b}"], 16)

                def store(m, b):
                    n = 2 * m + b
                    sp.wait_ge(s["y_ready"], n + 1 + 2)
                    sp.sem_inc(s["passed"], 1)
                    sp.dma_start(out_b[n, :, :, :], y[:, b]).then_inc(s[f"stored{b}"], 16)

                load(0, 0)
                load(0, 1)
                load_x(0, 0)
                load_x(0, 1)
                with sp.Fori(0, BLOCKS // 2 - 1) as i:
                    for b in range(2):
                        load(i + 1, b)
                        store(i, b)
                        load_x(i + 1, b)
                store(BLOCKS // 2 - 1, 0)
                store(BLOCKS // 2 - 1, 1)
                for b in range(2):
                    sp.wait_ge(s[f"stored{b}"], 16 * (BLOCKS // 2 + 1))

            @block.gpsimd
            def _(pool):
                nc.gpsimd.memset(every[:], 1.0).then_inc(s["every_set"], 1)

                def add_taps(m, b, j):
                    pool.wait_ge(s["tapped0"], JC * (2 * m + b) + j + 1)
                    pool.sem_inc(s["passed"], 1)
                    nc.gpsimd.tensor_tensor(conv[:, j % 2, 1], conv[:, j % 2, 1], others[:, j % 2, 0], ALU.add)
                    pool.drain()
                    nc.gpsimd.tensor_tensor(conv[:, j % 2, 1], conv[:, j % 2, 1], others[:, j % 2, 1], ALU.add).then_inc(s["tapped2"], 1)

                def scaling(m, b, pieces):
                    for k in pieces:
                        if k == 0:
                            pool.wait_ge(s["scale_ready"], 2 * m + b + 1)
                            pool.sem_inc(s["passed"], 1)
                        part = g[:, b, 2 * k:2 * k + 2, :]
                        nc.gpsimd.tensor_tensor(part, part, scale[:].unsqueeze(1).broadcast_to([P, 2, BT]),
                                                ALU.mult).then_inc(s["scaled"], 1)

                def turn(m, b, start=False):
                    for j in range(JC):
                        add_taps(m, b, j)
                        if not start and j in SCALED_AT:
                            scaling(*before(m, b), SCALED_AT[j])

                pool.wait_ge(s["taps_in"], 32)
                pool.sem_inc(s["tapped2"], 2)
                turn(0, 0, start=True)
                with pool.Fori(0, BLOCKS // 2 - 1) as i:
                    turn(i, 1)
                    turn(i + 1, 0)
                turn(BLOCKS // 2 - 1, 1)
                scaling(BLOCKS // 2 - 1, 1, range(JC))

            @block.vector
            def _(dve):
                dve.sem_inc(s["y_ready"], 2)
                dve.sem_inc(s["dequantised"], 2)

                def dequantise(m, b, j):
                    n = 2 * m + b
                    dve.drain()
                    dve.wait_ge(s["tapped2"], JC * n + j + 1)
                    dve.sem_inc(s["passed"], 1)
                    dve.wait_ge(s["first_done"], JC * n + j + 1)
                    nc.vector.tensor_tensor(hidden[:, j % 2], hp[j % 2][:, :, 0:HALO],
                                            rowstep[:, bass.ds(BT * n, HALO)].unsqueeze(1).broadcast_to([P, 2, HALO]),
                                            ALU.mult).then_inc(s["dequantised"], 1)

                def add_taps(m, b, j):
                    n = 2 * m + b
                    dve.wait_ge(s["tapped0"], JC * n + j + 1)
                    for k in range(1, 3):
                        last = nc.vector.scalar_tensor_tensor(conv[:, j % 2, 0], hidden[:, j % 2, 0, k:k + BT], taps[:, 2 * j, k:k + 1],
                                                              conv[:, j % 2, 0], ALU.mult, ALU.add)
                        if k == 1:
                            dve.drain()
                    last.then_inc(s["tapped"], 1)

                def largest(m, b):
                    dve.drain()
                    dve.wait_ge(s["silu_done"], JC * (2 * m + b + 1) + 2)
                    nc.vector.tensor_reduce(top[:], g[:, b].rearrange("p f t -> p t f"), AX.X, ALU.max,
                                            apply_absolute_value=True).then_inc(s["top_done"], 1)

                def steps(m, b):
                    n = 2 * m + b
                    dve.wait_ge(s["top_turned"], n + 1)
                    nc.vector.tensor_reduce(most[:], mp[:], AX.X, ALU.max)
                    dve.drain()
                    nc.vector.tensor_scalar(most[:], most[:], LEAST, None, ALU.max)
                    dve.drain()
                    nc.vector.reciprocal(step[:], most[:])
                    nc.vector.tensor_scalar(undo[:, b], most[:], mean[:, 1:2], 1.0 / LEVEL, ALU.mult, ALU.mult)
                    dve.drain()
                    nc.vector.tensor_scalar(step[:], step[:], LEVEL, None, ALU.mult)
                    dve.drain()
                    for k in range(2):
                        last = nc.vector.tensor_scalar(diag[:, k], const["ident"][:], step[:, k:k + 1], None, ALU.mult)
                    last.then_inc(s["steps_ready"], 1)

                def quantise(m, b):
                    n = 2 * m + b
                    dve.wait_ge(s["second_done"], n + 1)
                    dve.sem_inc(s["passed"], 1)
                    for k in range(2):
                        dve.wait_ge(s["scaled"], JC * n + (k + 1) * JC // 2)
                        last = nc.vector.tensor_scalar(gq[:, k * JC:(k + 1) * JC, :], g[:, b, k * JC:(k + 1) * JC, :], ROUND, ROUND,
                                                       ALU.add, ALU.subtract)
                    last.then_inc(s["quantised"], 1)

                def finish(m, b):
                    n = 2 * m + b
                    dve.wait_ge(s["second_done"], n + 2)
                    dve.sem_inc(s["passed"], 1)
                    dve.wait_ge(s[f"stored{b}"], 16 * (m + 1))
                    dve.sem_inc(s["passed"], 1)
                    dve.wait_ge(s[f"x_in{b}"], 16 * (m + 1))
                    for k in range(2):
                        last = nc.vector.scalar_tensor_tensor(y[:, b, k], op[:, k, :], undo[:, b, k:k + 1], x2[:, b, k], ALU.mult, ALU.add)
                    last.then_inc(s["y_ready"], 1)

                def turn(m, b, ends=2):
                    dequantise(m, b, 0)
                    dequantise(m, b, 1)
                    if ends:
                        largest(*before(m, b))
                    for j in range(JC):
                        add_taps(m, b, j)
                        if j + 2 < JC:
                            dequantise(m, b, j + 2)
                        if ends and j == 2:
                            steps(*before(m, b))
                        if ends > 1 and j == 5:
                            finish(m - 1, b)
                    if ends:
                        quantise(*before(m, b))

                turn(0, 0, ends=0)
                turn(0, 1, ends=1)
                with dve.Fori(0, BLOCKS // 2 - 1) as i:
                    turn(i + 1, 0)
                    turn(i + 1, 1)
                largest(BLOCKS // 2 - 1, 1)
                steps(BLOCKS // 2 - 1, 1)
                finish(BLOCKS // 2 - 1, 0)
                quantise(BLOCKS // 2 - 1, 1)
                finish(BLOCKS // 2 - 1, 1)

            @block.scalar
            def _(act):
                act.sem_inc(s["silu_done"], 2)
                act.sem_inc(s["stored0"], 16)
                act.sem_inc(s["stored1"], 16)
                act.wait_ge(s["taps_in"], 32)

                def first_taps(m, b, j):
                    n = 2 * m + b
                    act.wait_ge(s["silu_done"], JC * n + j + 1)
                    act.sem_inc(s["passed"], 1)
                    act.wait_ge(s["dequantised"], JC * n + j + 1 + 2)
                    for e in range(2):
                        f = 2 * j + e
                        nc.scalar.activation(conv[:, j % 2, e], hidden[:, j % 2, e, 0:BT], ACT.Identity, bias=tap_bias[:, f:f + 1],
                                                    scale=taps[:, f, 0:1])
                    for k in range(1, 3):
                        last = nc.scalar.activation(others[:, j % 2, k - 1], hidden[:, j % 2, 1, k:k + BT], ACT.Copy, scale=taps[:, 2 * j + 1, k:k + 1])
                    last.then_inc(s["tapped0"], 1)

                def silu(m, b, j):
                    n = 2 * m + b
                    act.wait_ge(s["tapped"], JC * n + j + 1)
                    act.sem_inc(s["passed"], 1)
                    act.wait_ge(s["tapped2"], JC * n + j + 1 + 2)
                    if j == 0:
                        act.sem_inc(s["passed"], 1)
                        act.wait_ge(s["quantised"], n + 1)
                    nc.scalar.activation(g[:, b, 2 * j:2 * j + 2, :], conv[:, j % 2], ACT.Silu).then_inc(s["silu_done"], 1)

                def copy_scale(m, b):
                    act.wait_ge(s["steps_spread"], 2 * m + b + 1)
                    nc.scalar.activation(scale[:], sp_[:, 0:BT], ACT.Copy).then_inc(s["scale_ready"], 1)

                def turn(m, b, first=False):
                    first_taps(m, b, 0)
                    for j in range(JC):
                        if j + 1 < JC:
                            first_taps(m, b, j + 1)
                        silu(m, b, j)
                        if not first and j == 3:
                            copy_scale(*before(m, b))

                act.sem_inc(s["quantised"], 2)
                turn(0, 0, first=True)
                with act.Fori(0, BLOCKS // 2 - 1) as i:
                    turn(i, 1)
                    turn(i + 1, 0)
                turn(BLOCKS // 2 - 1, 1)
                copy_scale(BLOCKS // 2 - 1, 1)

            @block.tensor
            def _(pe):
                pe.sem_inc(s["block_done"], 2)
                pe.sem_inc(s["second_done"], 1)
                pe.wait_ge(s["every_set"], 1)

                def first(m, b, pairs):
                    n = 2 * m + b
                    for j in pairs:
                        if j == 0:
                            pe.wait_ge(s[f"q_in{b}"], 16 * (m + 1))
                        pe.wait_ge(s["dequantised"], JC * n + j + 1)
                        for e in range(2):
                            f = 2 * j + e
                            for c in range(DC):
                                last = nc.tensor.matmul(hp[j % 2][:, e, 0:HALO], lhsT=W1q[:, c, f * P:(f + 1) * P], rhs=qin[:, b, c, :],
                                                        start=(c == 0), stop=(c == DC - 1))
                        last.then_inc(s["first_done"], 1)

                def turn_top(m, b):
                    pe.wait_ge(s["top_done"], 2 * m + b + 1)
                    for t in range(2):
                        last = nc.tensor.transpose(mp[:, t, :], top[:, t * P:(t + 1) * P], const["ident"][:])
                    last.then_inc(s["top_turned"], 1)

                def spread_steps(m, b):
                    pe.wait_ge(s["steps_ready"], 2 * m + b + 1)
                    nc.tensor.matmul(sp_[:, 0:BT], lhsT=every[:], rhs=diag[:].rearrange("p k t -> p (k t)"), start=True,
                                     stop=True).then_inc(s["steps_spread"], 1)

                def second(m, b, k):
                    n = 2 * m + b
                    if k == 0:
                        pe.wait_ge(s["quantised"], n + 3)
                        pe.sem_inc(s["passed"], 1)
                        pe.wait_ge(s["y_ready"], n + 2)
                    for f in range(FC):
                        last = nc.tensor.matmul(op[:, k, :], lhsT=gq[:, f, k * P:(k + 1) * P], rhs=W2q[:, f, :],
                                                start=(f == 0), stop=(f == FC - 1))
                    if k:
                        last.then_inc(s["second_done"], 1)

                def turn(m, b, ends=2):
                    first(m, b, range(0, 2))
                    if ends > 1:
                        second(m - 1, b, 0)
                    first(m, b, range(2, 4))
                    if ends:
                        turn_top(*before(m, b))
                    if ends > 1:
                        second(m - 1, b, 1)
                    first(m, b, range(4, 6))
                    if ends:
                        spread_steps(*before(m, b))
                    first(m, b, range(6, JC))
                    pe.drain()
                    pe.sem_inc(s["block_done"], 1)

                turn(0, 0, ends=0)
                turn(0, 1, ends=1)
                with pe.Fori(0, BLOCKS // 2 - 1) as i:
                    turn(i + 1, 0)
                    turn(i + 1, 1)
                turn_top(BLOCKS // 2 - 1, 1)
                second(BLOCKS // 2 - 1, 0, 0)
                second(BLOCKS // 2 - 1, 0, 1)
                spread_steps(BLOCKS // 2 - 1, 1)
                second(BLOCKS // 2 - 1, 1, 0)
                second(BLOCKS // 2 - 1, 1, 1)


def xattn_ffn(nc, a, out):
    whole = ExitStack()
    with whole:
        held = []

        def sem(name):
            held.append(nc.alloc_semaphore(name=name))
            return held[-1]

        def end_phase():
            nc.clear_and_free_semaphores(held)
            nc.all_engine_barrier()
            held.clear()

        def sb(name, shape, dt=F32):
            return whole.enter_context(nc.sbuf_tensor(name, shape, dt))

        dram = {
            "xt": nc.dram_tensor("scratch_xt", (T, D), F32).ap(),
            "qt": nc.dram_tensor("scratch_qt", (2, P, T), F32).ap(),
            "u": nc.dram_tensor("scratch_u", (T, DV), F32).ap(),
            "x2": nc.dram_tensor("scratch_x2", (T, D), F32).ap(),
            "qT": nc.dram_tensor("scratch_qT", (P, DC, T + 2), BF16).ap(),
            "K": nc.dram_tensor("scratch_K", (D, KROW), F32).ap(),
        }
        const = {"ident": sb("ident", [P, P]), "anti": sb("anti", [P, P]), "ones": sb("ones", [P, 1]),
                 "eps": sb("eps", [P, 1]),
                 "ident_bf": sb("ident_bf", [P, P], BF16)}
        ident_made = sem("ident_made")
        with nc.Block() as block:
            @block.gpsimd
            def _(pool):
                nc.gpsimd.memset(const["ident"][:], 0.0)
                nc.gpsimd.memset(const["anti"][:], 0.0)
                nc.gpsimd.memset(const["ones"][:], 1.0)
                nc.gpsimd.memset(const["eps"][:], EPS)
                pool.drain()
                nc.gpsimd.affine_select(out=const["ident"][:], in_=const["ident"][:], compare_op=ALU.not_equal, fill=1.0,
                                        base=0, pattern=[[-1, P]], channel_multiplier=1).then_inc(ident_made, 1)
                nc.gpsimd.affine_select(out=const["anti"][:], in_=const["anti"][:], compare_op=ALU.not_equal, fill=1.0,
                                        base=1 - P, pattern=[[1, P]], channel_multiplier=1).then_inc(ident_made, 1)
                pool.wait_ge(ident_made, 2)
                nc.gpsimd.tensor_copy(const["ident_bf"][:], const["ident"][:]).then_inc(ident_made, 1)
                pool.wait_ge(ident_made, 3)
        qstep = sb("qstep", [P, TILES])
        keys = ExitStack()
        with keys:
            KT = keys.enter_context(nc.sbuf_tensor("KT", [P, H // 2, G], F32R))
            prepare_attention(nc, sem, const, a, KT, dram)
            end_phase()
            attention(nc, sem, const, a, KT, dram)
            end_phase()
        rows = ExitStack()
        with rows:
            X = rows.enter_context(nc.sbuf_tensor("X", [P, TILES, D], F32))
            film = ExitStack()
            with film:
                wf = film.enter_context(nc.sbuf_tensor("wf_in", [P, VC, 2 * D], F32))
                fb = film.enter_context(nc.sbuf_tensor("fb_in", [P, 2 * D], F32))
                film_weights(nc, sem, const, a, "in", wf, fb)
                end_phase()
                modulate(nc, sem, const, a, wf, fb, X, dram)
                end_phase()
            layer = ExitStack()
            with layer:
                W = layer.enter_context(nc.sbuf_tensor("W", [P, LEVELS + 1, 2, PAIRS], F32))
                root = layer.enter_context(nc.sbuf_tensor("root", [P, 2, PAIRS], F32))
                s4d_scalars(nc, sem, const, a, W, root)
                end_phase()
                s4d(nc, sem, const, a, W, root, X, dram)
                end_phase()
            second = ExitStack()
            with second:
                W1 = second.enter_context(nc.sbuf_tensor("W1", [P, DC, HID], F32))
                W2 = second.enter_context(nc.sbuf_tensor("W2", [P, HID // P, D], F32))
                b1 = second.enter_context(nc.sbuf_tensor("b1", [P, HID // P], F32))
                wf = second.enter_context(nc.sbuf_tensor("wf_out", [P, VC, 2 * D], F32))
                fb = second.enter_context(nc.sbuf_tensor("fb_out", [P, 2 * D], F32))
                film_weights(nc, sem, const, a, "out", wf, fb)
                end_phase()
                fold_ffn(nc, sem, const, a, W1, W2, b1)
                end_phase()
                feed_forward(nc, sem, const, a, wf, fb, W1, W2, b1, X, qstep, dram)
                end_phase()
        third = ExitStack()
        with third:
            W1q = third.enter_context(nc.sbuf_tensor("W1q", [P, DC, HID], BF16))
            W2q = third.enter_context(nc.sbuf_tensor("W2q", [P, HID // P, D], BF16))
            mean = third.enter_context(nc.sbuf_tensor("mean", [P, 2], F32))
            rowstep = third.enter_context(nc.sbuf_tensor("rowstep", [P, T + 2], F32))
            quantise_weights(nc, sem, const, a, W1q, W2q, mean, qstep, rowstep)
            end_phase()
            bit_feed_forward(nc, sem, const, a, W1q, W2q, mean, rowstep, dram, out)


def kernel(**inputs):
    import concourse.bacc as bacc
    from concourse.bass_utils import run_bass_kernel_spmd

    nc = bacc.Bacc("TRN2", target_bir_lowering=False, num_devices=1)
    arrays, a = {}, {}
    for name, v in inputs.items():
        v = np.ascontiguousarray(v)
        if v.dtype == np.bool_:
            v = v.view(np.uint8)
        if v.ndim == 0:
            v = v.reshape(1)
        elif v.ndim > 1 and v.shape[0] == 1:
            v = v.reshape(v.shape[1:])
        arrays["in_" + name] = v
        short = {"ctx_768": "ctx", "mask_BxS_bf1": "mask1", "mask_BxS2_bf1": "mask2", "L0_ffn_w1": "ffn_w1", "L0_ffn_w2": "ffn_w2"}
        a[short.get(name, name.replace("L0_xattn_", "").replace("L0_ffn_", ""))] = nc.dram_tensor(
            "in_" + name, v.shape, mybir.dt.from_np(v.dtype), kind="ExternalInput").ap()
    out = nc.dram_tensor("out", (T, D), F32, kind="ExternalOutput").ap()
    xattn_ffn(nc, a, out)
    r = run_bass_kernel_spmd(nc, [arrays], core_ids=[0])
    return r.results[0]["out"].reshape(1, T, D)
```

```python
import math
from contextlib import ExitStack

import numpy as np

import concourse.bass as bass
from concourse import mybir

F32 = mybir.dt.float32
BF16 = mybir.dt.bfloat16
F32R = mybir.dt.float32r
I32 = mybir.dt.int32
U8 = mybir.dt.uint8
ALU = mybir.AluOpType
ACT = mybir.ActivationFunctionType
AX = mybir.AxisListType

P = 128
T, D = 4096, 512
G, DV = 3202, 384
H, DH = 4, 32
INNER = H * DH
TOP = 32
HID = 2048
NS = 64
TILES = T // P
GC = -(-G // P)
GLAST = G - (GC - 1) * P
DC = D // P
VC = DV // P
QUAD = 4
EPS = 1e-5
SCALE = 1.0 / math.sqrt(DH)
SEGS = 32
SEG = G // SEGS
CAND = SEGS * 8
LOWEST = -3.0e38
MASKED = 1.0e30
BANK = 512
SCORE_CHUNKS = -(-G // BANK)
ROUND = 1.5 * 2 ** 23


def phase_scope(nc):
    scope = ExitStack()

    def sb(name, shape, dt=F32):
        return scope.enter_context(nc.sbuf_tensor(name, shape, dt))

    def ps(name, shape, dt=F32):
        return scope.enter_context(nc.psum_tensor(name, shape, dt))

    return scope, sb, ps


I8 = mybir.dt.int8


def before(m, b):
    return (m, 0) if b else (m - 1, 1)


def after(m, b):
    return (m + 1, 0) if b else (m, 1)


def normalise_quad(nc, x, out, stats, mv, rstd, std_wanted, std_ready, turn):
    for k in range(QUAD):
        nc.vector.bn_stats(stats[:, k, :], x[:, k, :])
    nc.vector.drain()
    for k in range(QUAD):
        last = nc.vector.bn_aggr(mv[:, k, :], stats[:, k, :])
    last.then_inc(std_wanted, 1)
    nc.vector.wait_ge(std_ready, turn + 1)
    nc.vector.reciprocal(rstd[:], rstd[:])
    nc.vector.drain()
    for k in range(QUAD):
        last = nc.vector.tensor_scalar(out[:, k, :], x[:, k, :], mv[:, k, 0:1], rstd[:, k:k + 1],
                                       ALU.subtract, ALU.mult)
    return last


def key_rows(h):
    at = h % 2 * 2 * DH
    return slice(at, at + DH), slice(at + DH, at + 2 * DH), slice(h * DH, (h + 1) * DH)


def prepare_attention(nc, sem, const, a, KT, dram):
    scope, sb, ps = phase_scope(nc)
    ident, eps = const["ident"], const["eps"]
    x_q = a["x"].rearrange("(q k p) d -> q p k d", k=QUAD, p=P)
    xt_q = dram["xt"].rearrange("(q k p) d -> q p k d", k=QUAD, p=P)
    ctx_q = a["ctx"][0:24 * P, :].rearrange("(q k p) c -> q p k c", k=QUAD, p=P)
    with scope:
        wq = sb("wq", [P, DC, INNER])
        wk = sb("wk", [P, VC, INNER])
        x_in = sb("x_in", [P, 2, QUAD, D])
        xt = sb("xt_prep", [P, 2, QUAD, D])
        xtT = sb("xtT_prep", [P, DC, QUAD * P])
        qt = sb("qt_prep", [P, 2, 2, QUAD * P], F32R)
        stats = sb("stats_prep", [P, QUAD, 6])
        mv = sb("mv_prep", [P, QUAD, 2])
        rstd = sb("rstd_prep", [P, QUAD])
        cx = sb("cx_prep", [P, 2, QUAD, DV])
        cxT = sb("cxT_prep", [P, VC, QUAD * P])
        tp = ps("tp_prep", [P, DC, BANK])
        qp = ps("qp_prep", [P, BANK])
        kp = ps("kp_prep", [P, BANK])
        quads = T // (QUAD * P)
        cquads = 24 // QUAD
        s = {n: sem("prep_" + n) for n in (
            "weights_in", "x_loaded0", "x_loaded1", "x_read", "std_wanted", "std_ready", "xt_ready", "xt_turned", "xtT_ready",
            "q_done", "q_copied", "q_stored", "xt_stored", "xt_free", "qt_free", "cx_loaded0", "cx_loaded1", "cx_turned", "cxT_ready", "k_done",
            "k_high", "k_copied", "xt_transposed")}

        with nc.Block() as block:
            @block.sync
            def _(sp):
                sp.dma_start(wq[:], a["Wq"].rearrange("(c p) n -> p c n", p=P)).then_inc(s["weights_in"], 16)
                sp.dma_start(wk[:], a["Wk"].rearrange("(c p) n -> p c n", p=P)).then_inc(s["weights_in"], 16)

                with sp.Fori(0, quads // 2) as i:
                    for b in range(2):
                        q = 2 * i + b
                        sp.wait_ge(s["x_read"], q + 1)
                        sp.dma_start(x_in[:, b], x_q[q, :, :, :]).then_inc(s[f"x_loaded{b}"], 16)
                with sp.Fori(0, cquads // 2) as i:
                    for b in range(2):
                        sp.wait_ge(s["cx_turned"], 2 * i + b + 1)
                        sp.dma_start(cx[:, b], ctx_q[2 * i + b, :, :, :]).then_inc(s[f"cx_loaded{b}"], 16)
                sp.wait_ge(s["cx_turned"], cquads + 1)
                sp.dma_start(cx[:, 0, 0, :], a["ctx"][24 * P:25 * P, :]).then_inc(s["cx_loaded0"], 16)
                sp.dma_start(cx[0:GLAST, 0, 1, :], a["ctx"][25 * P:G, :]).then_inc(s["cx_loaded0"], 16)

            @block.gpsimd
            def _(pool):
                def store_rows(m, b):
                    q = 2 * m + b
                    pool.wait_ge(s["xt_ready"], q + 1)
                    pool.dma_start(xt_q[q, :, :, :], xt[:, b]).then_inc(s["xt_stored"], 16)

                def rows_stored(m, b):
                    pool.wait_ge(s["xt_stored"], 16 * (2 * m + b + 1))
                    pool.sem_inc(s["xt_free"], 1)

                def store_queries(m, b):
                    q = 2 * m + b
                    pool.wait_ge(s["q_copied"], q + 2)
                    pool.dma_start(dram["qt"][:, :, bass.ts(q, QUAD * P)].rearrange("c p t -> p c t"), qt[:, b].bitcast(F32)).then_inc(s["q_stored"], 16)

                def queries_stored(m, b):
                    pool.wait_ge(s["q_stored"], 16 * (2 * m + b + 1))
                    pool.sem_inc(s["qt_free"], 1)

                store_rows(0, 0)
                rows_stored(0, 0)
                with pool.Fori(0, quads // 2 - 1) as i:
                    for b in range(2):
                        store_rows(*after(i, b))
                        store_queries(i, b)
                        rows_stored(*after(i, b))
                        queries_stored(i, b)
                store_rows(quads // 2 - 1, 1)
                store_queries(quads // 2 - 1, 0)
                rows_stored(quads // 2 - 1, 1)
                queries_stored(quads // 2 - 1, 0)
                store_queries(quads // 2 - 1, 1)
                queries_stored(quads // 2 - 1, 1)

            @block.vector
            def _(dve):
                dve.sem_inc(s["x_read"], 2)
                dve.sem_inc(s["xt_free"], 2)
                dve.sem_inc(s["qt_free"], 2)
                dve.sem_inc(s["q_copied"], 1)

                def normalise(m, b):
                    q = 2 * m + b
                    dve.wait_ge(s[f"x_loaded{b}"], 16 * (m + 1))
                    dve.wait_ge(s["xt_free"], q + 1)
                    normalise_quad(nc, x_in[:, b], xt[:, b], stats, mv, rstd, s["std_wanted"], s["std_ready"],
                                   q).then_inc(s["xt_ready"], 1)
                    dve.drain()
                    dve.sem_inc(s["x_read"], 1)

                def copy_queries(m, b):
                    dve.wait_ge(s["qt_free"], 2 * m + b + 1)
                    dve.wait_ge(s["q_done"], 2 * m + b + 1)
                    nc.vector.tensor_copy(qt[:, b, 0], qp[:])
                    dve.drain()
                    nc.vector.tensor_tensor(qt[:, b, 1], qp[:], qt[:, b, 0].bitcast(F32), ALU.subtract).then_inc(s["q_copied"], 1)

                normalise(0, 0)
                with dve.Fori(0, quads // 2 - 1) as i:
                    for b in range(2):
                        normalise(*after(i, b))
                        copy_queries(i, b)
                normalise(quads // 2 - 1, 1)
                copy_queries(quads // 2 - 1, 0)
                copy_queries(quads // 2 - 1, 1)
                for q in range(cquads + 1):
                    w = QUAD * P if q < cquads else P + GLAST
                    dve.wait_ge(s["k_high"], q + 1)
                    for h in range(H):
                        high, low, src = key_rows(h)
                        last = nc.vector.tensor_tensor(KT[low, h // 2, q * BANK:q * BANK + w], kp[src, 0:w],
                                                       KT[high, h // 2, q * BANK:q * BANK + w].bitcast(F32), ALU.subtract)
                    last.then_inc(s["k_copied"], 1)

            @block.scalar
            def _(act):
                def root(q):
                    act.wait_ge(s["std_wanted"], q + 1)
                    nc.scalar.activation(rstd[:], mv[:, :, 1], ACT.Sqrt, bias=eps[:, 0:1]).then_inc(s["std_ready"], 1)

                def copy_x(q):
                    act.wait_ge(s["xt_turned"], q + 1)
                    nc.scalar.activation(xtT[:], tp[:], ACT.Copy).then_inc(s["xtT_ready"], 1)

                root(0)
                with act.Fori(0, quads - 1) as q:
                    root(q + 1)
                    copy_x(q)
                copy_x(quads - 1)
                for q in range(cquads + 1):
                    w = QUAD * P if q < cquads else P + GLAST
                    act.wait_ge(s["cx_turned"], q + 3)
                    nc.scalar.activation(cxT[:, :, 0:w], tp[:, 0:VC, 0:w], ACT.Copy).then_inc(s["cxT_ready"], 1)
                    act.wait_ge(s["k_done"], q + 1)
                    for h in range(H):
                        high, _, src = key_rows(h)
                        last = nc.scalar.activation(KT[high, h // 2, q * BANK:q * BANK + w], kp[src, 0:w], ACT.Copy)
                    last.then_inc(s["k_high"], 1)

            @block.tensor
            def _(pe):
                pe.sem_inc(s["cx_turned"], 2)
                pe.wait_ge(s["weights_in"], 32)
                with pe.Fori(0, quads // 2) as i:
                    for b in range(2):
                        q = 2 * i + b
                        pe.wait_ge(s["xt_ready"], q + 1)
                        for c in range(DC):
                            for k in range(QUAD):
                                last = nc.tensor.transpose(tp[:, c, k * P:(k + 1) * P], xt[:, b, k, c * P:(c + 1) * P],
                                                           ident[:])
                        last.then_inc(s["xt_turned"], 1)
                        pe.wait_ge(s["xtT_ready"], q + 1)
                        pe.wait_ge(s["q_copied"], q + 1)
                        for c in range(DC):
                            last = nc.tensor.matmul(qp[:], lhsT=wq[:, c, :], rhs=xtT[:, c, :], start=(c == 0),
                                                    stop=(c == DC - 1))
                        last.then_inc(s["q_done"], 1)
                for q in range(cquads + 1):
                    parts = [(k, P) for k in range(QUAD)] if q < cquads else [(0, P), (1, GLAST)]
                    w = sum(n for _, n in parts)
                    pe.wait_ge(s[f"cx_loaded{q % 2}"], 16 * (q // 2 + 1) if q < cquads else 16 * (q // 2 + 2))
                    for c in range(VC):
                        for k, n in parts:
                            last = nc.tensor.transpose(tp[:, c, k * P:k * P + n], cx[0:n, q % 2, k, c * P:(c + 1) * P],
                                                       ident[0:n, 0:n])
                    last.then_inc(s["cx_turned"], 1)
                    pe.wait_ge(s["cxT_ready"], q + 1)
                    if q:
                        pe.wait_ge(s["k_copied"], q)
                    for c in range(VC):
                        last = nc.tensor.matmul(kp[:, 0:w], lhsT=wk[:, c, :], rhs=cxT[:, c, 0:w], start=(c == 0),
                                                stop=(c == VC - 1))
                    last.then_inc(s["k_done"], 1)


def attention(nc, sem, const, a, KT, dram):
    scope, sb, ps = phase_scope(nc)
    ident, ones = const["ident"], const["ones"]
    with scope:
        ctx = sb("ctx", [P, GC, DV])
        hidden = sb("hidden", [P, G], I8)
        S = sb("S", [P, 2, H, G])
        E = sb("E", [P, 2, G])
        attnT = sb("attnT", [P, 2, 4, P])
        q = sb("q", [P, 2, H // 2, P], F32R)
        cand = sb("cand", [P, H, CAND])
        tops = sb("tops", [P, 2, H, TOP])
        seg8 = sb("seg8", [P, H])
        left = sb("left", [P, H])
        bad = sb("bad", [P, H])
        badi = sb("badi", [1, H + 1], I32)
        masked = sb("masked", [1, 1], I32)
        mrow = sb("mrow", [1, 1])
        tmask8 = sb("tmask8", [P, TILES], U8)
        tmask = sb("tmask", [P, TILES])
        nmax = sb("nmax", [P, H])
        etop = sb("etop", [P, H, TOP], BF16)
        den = sb("den", [P, H])
        lden = sb("lden", [P, H])
        ebias = sb("ebias", [P, 2, H])
        u = sb("u", [P, DV])
        score = [ps(f"score{k}", [P, 2, BANK]) for k in range(2)]
        tp = [ps(f"turn{k}", [P, 4, P]) for k in range(2)]
        up = ps("up", [P, BANK])
        fp = ps("fp", [P, BANK])
        mask8 = E[:, 0, :].bitcast(U8)[:, 0:G]
        s = {n: sem("attn_" + n) for n in (
            "ctx_in", "mask_in", "tmask_ready", "q_in", "q_free", "score_done", "score_copied", "flags_wanted",
            "flags_done", "tops_final", "lden_ready", "ebias_ready", "e_ready", "e_used", "pair_summed", "summed", "turned",
            "turn_copied", "times_done", "u_copied", "u_stored", "passed")}
        ORDER = (1, 3, 2, 0)
        HALVES = -(-SCORE_CHUNKS // 2)
        GROUPS = H * HALVES
        TURNS = SCORE_CHUNKS

        def chunk(j):
            return slice(j * BANK, min((j + 1) * BANK, G))

        with nc.Block() as block:
            @block.sync
            def _(sp):
                sp.dma_start(mask8, a["mask2"].partition_broadcast(P)).then_inc(s["mask_in"], 16)
                sp.dma_start(tmask8[:], a["mask1"].rearrange("(n p) -> p n", p=P), allow_slow_non_contiguous=True).then_inc(s["mask_in"], 16)
                qd = dram["qt"].rearrange("c (p e d) t -> e d c p t", e=2, d=DH)
                with sp.Fori(0, TILES) as n:
                    sp.wait_ge(s["q_free"], n + 1)
                    for e in range(2):
                        for r in range(2):
                            at = (2 * e + r) * DH
                            sp.dma_start(q[at:at + DH].bitcast(F32), qd[e, :, :, :, bass.ts(n, P)]).then_inc(s["q_in"], 16)

            @block.gpsimd
            def _(pool):
                def bias(m, b):
                    pool.wait_ge(s["lden_ready"], 2 * m + b + 1)
                    nc.gpsimd.tensor_tensor(ebias[:, b, :], nmax[:], lden[:], ALU.subtract).then_inc(s["ebias_ready"], 1)

                def sums(m, b):
                    n = 2 * m + b
                    pool.wait_ge(s["e_used"], H * n + 4)
                    nc.gpsimd.tensor_tensor(S[:, b, 0, :], S[:, b, 0, :], S[:, b, 1, :], ALU.add).then_inc(s["pair_summed"], 1)
                    pool.wait_ge(s["e_used"], H * n + 6)
                    nc.gpsimd.tensor_tensor(S[:, b, 2, :], S[:, b, 2, :], S[:, b, 3, :], ALU.add).then_inc(s["pair_summed"], 1)
                    pool.drain()
                    for j in range(SCORE_CHUNKS):
                        nc.gpsimd.tensor_tensor(S[:, b, 0, chunk(j)], S[:, b, 0, chunk(j)], S[:, b, 2, chunk(j)],
                                                ALU.add).then_inc(s["summed"], 1)

                def turn(m, b):
                    bias(*before(m, b))
                    sums(*before(m, b))

                turn(0, 1)
                with pool.Fori(0, (TILES - 2) // 2) as i:
                    turn(i + 1, 0)
                    turn(i + 1, 1)
                turn(TILES // 2, 0)

            @block.vector
            def _(dve):
                dve.wait_ge(s["mask_in"], 32)
                nc.vector.tensor_scalar(hidden[:], mask8, 1.0, None, ALU.subtract)
                nc.vector.tensor_reduce(mrow[:], mask8[0:1, :], AX.X, ALU.min)
                nc.vector.tensor_copy(tmask[:], tmask8[:]).then_inc(s["tmask_ready"], 1)
                dve.drain()
                nc.vector.tensor_scalar(mrow[:], mrow[:], -1.0, 1.0, ALU.mult, ALU.add)
                dve.drain()
                nc.vector.tensor_copy(masked[:], mrow[:])
                dve.drain()
                any_masked = dve.value_load(masked[0:1, 0:1], min_val=0, max_val=1)

                def arrived(n, groups):
                    dve.wait_ge(s["score_copied"], GROUPS * n + groups + 2)
                    dve.sem_inc(s["passed"], 1)

                def segments(m, b, h):
                    n = 2 * m + b
                    arrived(n, HALVES * (ORDER.index(h) + 1))
                    with dve.If(any_masked > 0):
                        nc.vector.scalar_tensor_tensor(S[:, b, h, :], hidden[:], MASKED, S[:, b, h, :], ALU.mult, ALU.add)
                        dve.drain()
                    for k in range(SEGS):
                        end = (k + 1) * SEG if k < SEGS - 1 else G
                        nc.vector.max(cand[:, h, 8 * k:8 * k + 8], S[:, b, h, k * SEG:end])

                def keep_top(m, b, h):
                    dve.wait_ge(s["e_ready"], H * (2 * m + b) + h + 1)
                    nc.vector.scalar_tensor_tensor(S[:, b, h, :], S[:, b, h, :], tops[:, b, h, TOP - 1:TOP], E[:, h % 2, :],
                                                   ALU.is_ge, ALU.mult).then_inc(s["e_used"], 1)

                def exact(b, h):
                    src, rest = S[:, b, h, :], E[:, 0, :]
                    for r in range(TOP // 8):
                        nc.vector.max(tops[:, b, h, 8 * r:8 * r + 8], src)
                        dve.drain()
                        nc.vector.match_replace(rest, tops[:, b, h, 8 * r:8 * r + 8], src, LOWEST)
                        dve.drain()
                        src = rest
                    nc.vector.tensor_tensor(rest, rest, S[:, b, h, :], ALU.is_equal)
                    dve.drain()
                    nc.vector.scalar_tensor_tensor(S[:, b, h, :], rest, LOWEST, S[:, b, h, :], ALU.mult, ALU.add)
                    dve.drain()

                def thresholds(m, b):
                    dve.drain()
                    nc.vector.tensor_reduce(seg8[:], cand[:, :, 7::8], AX.X, ALU.max)
                    for r in range(TOP // 8):
                        for h in range(H):
                            nc.vector.max(tops[:, b, h, 8 * r:8 * r + 8], cand[:, h, :])
                        dve.drain()
                        if r < TOP // 8 - 1:
                            for h in range(H):
                                nc.vector.match_replace(cand[:, h, :], tops[:, b, h, 8 * r:8 * r + 8], cand[:, h, :], LOWEST)
                            dve.drain()
                    for h in range(H):
                        nc.vector.tensor_scalar(cand[:, h, :], cand[:, h, :], tops[:, b, h, TOP - 1:TOP], 0.0,
                                                ALU.is_ge, ALU.add, accum_out=left[:, h:h + 1])
                    nc.vector.tensor_tensor(bad[:], seg8[:], tops[:, b, :, TOP - 1], ALU.is_ge)
                    dve.drain()
                    nc.vector.scalar_tensor_tensor(bad[:], left[:], 8.0, bad[:], ALU.not_equal, ALU.add).then_inc(s["flags_wanted"], 1)

                def check(m, b):
                    dve.wait_ge(s["flags_done"], 2 * m + b + 1)
                    nc.vector.tensor_copy(badi[0:1, 0:H], fp[0:1, 0:H])
                    nc.vector.tensor_reduce(badi[0:1, H:H + 1], fp[0:1, 0:H], AX.X, ALU.max)
                    dve.drain()
                    some = dve.value_load(badi[0:1, H:H + 1], min_val=0, max_val=2 * P)
                    with dve.If(some > 0):
                        for h in range(H):
                            this = dve.value_load(badi[0:1, h:h + 1], min_val=0, max_val=2 * P)
                            with dve.If(this > 0):
                                exact(b, h)
                    dve.drain()
                    dve.sem_inc(s["tops_final"], 1)

                def turn(m, b, first=False):
                    segments(m, b, ORDER[0])
                    segments(m, b, ORDER[1])
                    if not first:
                        check(*before(m, b))
                    segments(m, b, ORDER[2])
                    if not first:
                        for h in range(H):
                            keep_top(*before(m, b), h)
                    segments(m, b, ORDER[3])
                    thresholds(m, b)

                dve.sem_inc(s["e_used"], 2)
                turn(0, 0, first=True)
                with dve.Fori(0, (TILES - 2) // 2) as i:
                    turn(i, 1)
                    turn(i + 1, 0)
                turn(TILES // 2 - 1, 1)
                check(TILES // 2 - 1, 1)
                for h in range(H):
                    keep_top(TILES // 2 - 1, 1, h)

            @block.scalar
            def _(act):
                act.wait_ge(s["mask_in"], 32)
                act.wait_ge(s["q_in"], 16 * 4)
                act.dma_start(ctx[:, 0:GC - 1, :], a["ctx"][0:(GC - 1) * P, :].rearrange("(k p) c -> p k c", p=P)).then_inc(s["ctx_in"], 16)
                act.dma_start(ctx[0:GLAST, GC - 1, :], a["ctx"][(GC - 1) * P:G, :]).then_inc(s["ctx_in"], 16)
                act.sem_inc(s["score_copied"], 2)
                act.sem_inc(s["turn_copied"], 2)
                act.sem_inc(s["u_stored"], 16)
                act.sem_inc(s["u_copied"], 1)

                def copy_scores(m, b, h, groups=range(HALVES)):
                    n = 2 * m + b
                    for k in groups:
                        act.wait_ge(s["score_done"], GROUPS * n + HALVES * ORDER.index(h) + k + 1)
                        w = min(2 * BANK, G - 2 * BANK * k)
                        nc.scalar.activation(S[:, b, h, 2 * BANK * k:2 * BANK * k + w],
                                             score[k % 2][:, :, :].rearrange("p c k -> p (c k)")[:, 0:w],
                                             ACT.Copy).then_inc(s["score_copied"], 1)

                def sums_of_exps(m, b):
                    n = 2 * m + b
                    act.wait_ge(s["tops_final"], n + 1)
                    nc.scalar.mul(nmax[:], tops[:, b, :, 0], -SCALE)
                    act.drain()
                    for h in range(H):
                        nc.scalar.activation(etop[:, h, :], tops[:, b, h, :], ACT.Exp, bias=nmax[:, h:h + 1], scale=SCALE,
                                             accum_out=den[:, h:h + 1])
                    act.drain()
                    nc.scalar.activation(lden[:], den[:], ACT.Ln, scale=float(H)).then_inc(s["lden_ready"], 1)

                def probabilities(m, b, h):
                    n = 2 * m + b
                    if h == 0:
                        act.wait_ge(s["ebias_ready"], n + 1)
                    act.wait_ge(s["e_used"], H * n + h + 1)
                    nc.scalar.activation(E[:, h % 2, :], S[:, b, h, :], ACT.Exp, bias=ebias[:, b, h:h + 1],
                                         scale=SCALE).then_inc(s["e_ready"], 1)

                def copy_turned(m, b, g):
                    n = 2 * m + b
                    act.wait_ge(s["turned"], TURNS * n + g + 1)
                    act.wait_ge(s["times_done"], TURNS * n + g + 1)
                    w = min(4, GC - 4 * g)
                    e = (TURNS * b + g) % 2
                    if g < TURNS - 1:
                        nc.scalar.activation(attnT[:, e], tp[e][:], ACT.Copy).then_inc(s["turn_copied"], 1)
                    else:
                        nc.scalar.activation(attnT[:, e, 0:w - 1, :], tp[e][:, 0:w - 1, :], ACT.Copy)
                        nc.scalar.activation(attnT[0:GLAST, e, w - 1, :], tp[e][0:GLAST, w - 1, :], ACT.Copy).then_inc(s["turn_copied"], 1)

                def copy_context(m, b):
                    n = 2 * m + b
                    act.wait_ge(s["times_done"], TURNS * (n + 1) + 2)
                    act.sem_inc(s["passed"], 1)
                    act.wait_ge(s["u_stored"], 16 * (n + 1))
                    act.sem_inc(s["passed"], 1)
                    nc.scalar.activation(u[:], up[:, 0:DV], ACT.Copy, scale=tmask[:, bass.ds(n, 1)]).then_inc(s["u_copied"], 1)
                    act.wait_ge(s["u_copied"], n + 2)
                    act.sem_inc(s["passed"], 1)
                    act.dma_start(dram["u"][bass.ts(n, P), :], u[:]).then_inc(s["u_stored"], 16)

                act.wait_ge(s["tmask_ready"], 1)
                nc.scalar.preload_act_table_set("natural_log_exp_and_others")
                for h in ORDER:
                    copy_scores(0, 0, h)
                for h in ORDER:
                    copy_scores(0, 1, h)

                def turn(m, b, last=False, beyond=False):
                    if not last:
                        copy_scores(*after(m, b), ORDER[0])
                        copy_scores(*after(m, b), ORDER[1])
                        copy_scores(*after(m, b), ORDER[2])
                    for g in range(TURNS - 2):
                        copy_turned(*before(m, b), g)
                    if not beyond:
                        sums_of_exps(m, b)
                        probabilities(m, b, 0)
                    copy_turned(*before(m, b), TURNS - 2)
                    if not beyond:
                        probabilities(m, b, 1)
                    copy_turned(*before(m, b), TURNS - 1)
                    if not beyond:
                        probabilities(m, b, 2)
                    if not last:
                        copy_scores(*after(m, b), ORDER[3], range(0, 2))
                    if not beyond:
                        probabilities(m, b, 3)
                    if not last:
                        copy_scores(*after(m, b), ORDER[3], range(2, HALVES))
                    copy_context(*before(m, b))

                sums_of_exps(0, 0)
                for h in range(H):
                    probabilities(0, 0, h)
                turn(0, 1)
                with act.Fori(0, (TILES - 4) // 2) as i:
                    turn(i + 1, 0)
                    turn(i + 1, 1)
                turn(TILES // 2 - 1, 0)
                turn(TILES // 2 - 1, 1, last=True)
                turn(TILES // 2, 0, last=True, beyond=True)
                act.wait_ge(s["u_stored"], 16 * (TILES + 1))

            @block.tensor
            def _(pe):
                pe.sem_inc(s["times_done"], 2)
                pe.sem_inc(s["q_free"], 1)

                def scores(m, b, h):
                    n = 2 * m + b
                    at = slice(h % 2 * 2 * DH, (h % 2 + 1) * 2 * DH)
                    if h == ORDER[0]:
                        pe.wait_ge(s["q_in"], 16 * 4 * (n + 1))
                    for k in range(HALVES):
                        pe.wait_ge(s["score_copied"], GROUPS * n + HALVES * ORDER.index(h) + k + 1)
                        for j in range(2 * k, min(2 * k + 2, SCORE_CHUNKS)):
                            w = chunk(j).stop - chunk(j).start
                            for part in range(2):
                                last = nc.tensor.matmul(score[k % 2][:, j % 2, 0:w], lhsT=q[at, part, h // 2, :],
                                                        rhs=KT[at, h // 2, chunk(j)], start=(part == 0), stop=(part == 1))
                        last.then_inc(s["score_done"], 1)

                def scores_end():
                    pe.drain()
                    pe.sem_inc(s["q_free"], 1)

                def flags(m, b):
                    pe.wait_ge(s["flags_wanted"], 2 * m + b + 1)
                    nc.tensor.matmul(fp[0:1, 0:H], lhsT=ones[:, 0:1], rhs=bad[:], start=True, stop=True).then_inc(s["flags_done"], 1)

                def turn_attention(m, b, g):
                    n = 2 * m + b
                    pe.wait_ge(s["summed"], TURNS * n + g + 1)
                    pe.wait_ge(s["turn_copied"], TURNS * n + g + 1)
                    e = (TURNS * b + g) % 2
                    for c in range(4 * g, min(4 * g + 4, GC)):
                        w = P if c < GC - 1 else GLAST
                        last = nc.tensor.transpose(tp[e][0:w, c - 4 * g, :], S[:, b, 0, c * P:c * P + w], ident[:])
                    last.then_inc(s["turned"], 1)

                def times_context(m, b, g):
                    n = 2 * m + b
                    pe.wait_ge(s["turn_copied"], TURNS * n + g + 3)
                    if g == 0:
                        pe.wait_ge(s["u_copied"], n + 1)
                    e = (TURNS * b + g) % 2
                    for c in range(4 * g, min(4 * g + 4, GC)):
                        w = P if c < GC - 1 else GLAST
                        last = nc.tensor.matmul(up[:, 0:DV], lhsT=attnT[0:w, e, c - 4 * g, :], rhs=ctx[0:w, c, :],
                                                start=(c == 0), stop=(c == GC - 1))
                    last.then_inc(s["times_done"], 1)

                def turn(m, b, last=False, beyond=False):
                    old, new = before(m, b), after(m, b)
                    if not last:
                        pe.wait_ge(s["pair_summed"], 2 * (2 * m + b) - 1)
                        scores(*new, ORDER[0])
                        pe.wait_ge(s["pair_summed"], 2 * (2 * m + b))
                        scores(*new, ORDER[1])
                        pe.wait_ge(s["summed"], TURNS * (2 * m + b))
                        scores(*new, ORDER[2])
                    turn_attention(*old, 0)
                    if not beyond:
                        flags(m, b)
                    for g in range(TURNS):
                        if g < TURNS - 1:
                            turn_attention(*old, g + 1)
                        if g == TURNS - 1 and not last:
                            scores(*new, ORDER[3])
                        times_context(*old, g)
                    if not last:
                        scores_end()

                for h in ORDER:
                    scores(0, 0, h)
                scores_end()
                for h in ORDER:
                    scores(0, 1, h)
                scores_end()
                pe.wait_ge(s["ctx_in"], 32)
                flags(0, 0)
                turn(0, 1)
                with pe.Fori(0, (TILES - 4) // 2) as i:
                    turn(i + 1, 0)
                    turn(i + 1, 1)
                turn(TILES // 2 - 1, 0)
                turn(TILES // 2 - 1, 1, last=True)
                turn(TILES // 2, 0, last=True, beyond=True)


def modulate(nc, sem, const, a, wf, fb, X, dram):
    scope, sb, ps = phase_scope(nc)
    with scope:
        u = sb("mod_u", [P, 2, DV])
        xt = sb("mod_xt", [P, 2, D])
        uT = sb("mod_uT", [P, 2, 2, VC, P], F32R)
        wf_parts = sb("mod_wf", [P, 2, VC, 2 * D], F32R)
        xm_parts = sb("mod_xm_parts", [P, 2, 2, D], F32R)
        other_diag = sb("mod_other_diag", [P, P])
        anti = sb("mod_anti", [P, P], F32R)
        xn = sb("mod_xn", [P, 2, D])
        gain = sb("mod_gain", [P, D])
        offset = sb("mod_offset", [P, D])
        sc = sb("mod_scale", [P, D])
        sh = sb("mod_shift", [P, 2, D])
        xm = sb("mod_xm", [P, 2, D])
        stats = sb("mod_stats", [P, 6])
        mv = sb("mod_mv", [P, 2])
        rstd = sb("mod_rstd", [P, 1])
        tp = [ps(f"mod_tp{k}", [P, VC, P]) for k in range(2)]
        fp = [ps(f"mod_film{k}", [P, 2, BANK]) for k in range(2)]
        rp = [ps(f"mod_rev{k}", [P, BANK]) for k in range(2)]
        s = {n: sem("mod_" + n) for n in (
            "rows_in", "in0", "in1", "xt_read", "u_turned", "uT_ready", "film_done", "film_read", "std_wanted", "std_ready",
            "normed", "affine", "diag_made", "wf_split", "uT_high", "xm_ready", "xm_high", "xm_split", "reversed", "X_ready", "passed")}

        with nc.Block() as block:
            @block.sync
            def _(sp):
                sp.dma_start(gain[:], a["g_norm_in"].partition_broadcast(P)).then_inc(s["rows_in"], 16)
                sp.dma_start(offset[:], a["b_norm_in"].partition_broadcast(P)).then_inc(s["rows_in"], 16)
                with sp.Fori(0, TILES // 2) as i:
                    for b in range(2):
                        n = 2 * i + b
                        sp.wait_ge(s["xt_read"], n + 1)
                        sp.dma_start(xt[:, b], dram["xt"][bass.ts(n, P), :]).then_inc(s[f"in{b}"], 16)
                        sp.wait_ge(s["u_turned"], n + 1)
                        sp.dma_start(u[:, b], dram["u"][bass.ts(n, P), :]).then_inc(s[f"in{b}"], 16)

            @block.gpsimd
            def _(pool):
                nc.gpsimd.memset(other_diag[:], 0.0)
                pool.drain()
                nc.gpsimd.affine_select(out=other_diag[:], in_=other_diag[:], compare_op=ALU.not_equal, fill=1.0,
                                        base=1 - P, pattern=[[1, P]], channel_multiplier=1).then_inc(s["diag_made"], 1)
                pool.wait_ge(s["rows_in"], 32)

                def affine(m, b):
                    pool.wait_ge(s["normed"], 2 * m + b + 1)
                    nc.gpsimd.tensor_tensor(xn[:, b], xn[:, b], gain[:], ALU.mult)
                    pool.drain()
                    nc.gpsimd.tensor_tensor(xn[:, b], xn[:, b], offset[:], ALU.add).then_inc(s["affine"], 1)

                def low_x(m, b):
                    pool.wait_ge(s["xm_high"], 2 * m + b + 1)
                    nc.gpsimd.tensor_tensor(xm_parts[:, b, 1], xm[:, b], xm_parts[:, b, 0].bitcast(F32), ALU.subtract).then_inc(s["xm_split"], 1)

                pool.sem_inc(s["xm_split"], 2)
                affine(0, 0)
                with pool.Fori(0, TILES // 2 - 1) as i:
                    for b in range(2):
                        affine(*after(i, b))
                        low_x(i, b)
                affine(TILES // 2 - 1, 1)
                low_x(TILES // 2 - 1, 0)
                low_x(TILES // 2 - 1, 1)

            @block.vector
            def _(dve):
                dve.sem_inc(s["xt_read"], 2)

                def normalise(m, b):
                    n = 2 * m + b
                    dve.wait_ge(s[f"in{b}"], 32 * (m + 1))
                    nc.vector.bn_stats(stats[:], xt[:, b, :])
                    dve.drain()
                    nc.vector.bn_aggr(mv[:], stats[:]).then_inc(s["std_wanted"], 1)
                    dve.wait_ge(s["std_ready"], n + 1)
                    nc.vector.reciprocal(rstd[:], rstd[:])
                    dve.drain()
                    nc.vector.tensor_scalar(xn[:, b], xt[:, b], mv[:, 0:1], rstd[:, 0:1], ALU.subtract, ALU.mult).then_inc(s["normed"], 1)
                    dve.drain()
                    dve.sem_inc(s["xt_read"], 1)
                    dve.wait_ge(s["uT_high"], n + 1)
                    nc.vector.tensor_tensor(uT[:, b, 1], tp[b][:], uT[:, b, 0].bitcast(F32), ALU.subtract).then_inc(s["uT_ready"], 1)

                def film(m, b):
                    n = 2 * m + b
                    dve.drain()
                    dve.wait_ge(s["film_done"], n + 1)
                    nc.vector.tensor_tensor(sc[:], fp[b][:, 0, :], fb[:, 0:D], ALU.add)
                    nc.vector.tensor_tensor(sh[:, b], fp[b][:, 1, :], fb[:, D:2 * D], ALU.add).then_inc(s["film_read"], 1)
                    dve.drain()
                    dve.wait_ge(s["affine"], n + 1)
                    nc.vector.tensor_tensor(sc[:], xn[:, b], sc[:], ALU.mult)
                    dve.drain()
                    dve.wait_ge(s["xm_split"], n + 1)
                    nc.vector.tensor_tensor(xm[:, b], sc[:], sh[:, b], ALU.add).then_inc(s["xm_ready"], 1)

                dve.wait_ge(s["diag_made"], 1)
                nc.vector.tensor_copy(anti[:], other_diag[:])
                nc.vector.tensor_copy(wf_parts[:, 0], wf[:])
                dve.drain()
                nc.vector.tensor_tensor(wf_parts[:, 1], wf[:], wf_parts[:, 0].bitcast(F32), ALU.subtract).then_inc(s["wf_split"], 1)
                normalise(0, 0)
                with dve.Fori(0, TILES // 2 - 1) as i:
                    for b in range(2):
                        normalise(*after(i, b))
                        film(i, b)
                normalise(TILES // 2 - 1, 1)
                film(TILES // 2 - 1, 0)
                film(TILES // 2 - 1, 1)

            @block.scalar
            def _(act):
                act.sem_inc(s["X_ready"], 2)

                def root(m, b):
                    act.wait_ge(s["std_wanted"], 2 * m + b + 1)
                    nc.scalar.activation(rstd[:], mv[:, 1:2], ACT.Sqrt, bias=const["eps"][:, 0:1]).then_inc(s["std_ready"], 1)

                def copy_u(m, b):
                    act.wait_ge(s["u_turned"], 2 * m + b + 3)
                    nc.scalar.activation(uT[:, b, 0], tp[b][:], ACT.Copy).then_inc(s["uT_high"], 1)

                def high_x(m, b):
                    n = 2 * m + b
                    act.wait_ge(s["reversed"], n + 1)
                    act.sem_inc(s["passed"], 1)
                    act.wait_ge(s["xm_ready"], n + 1)
                    nc.scalar.activation(xm_parts[:, b, 0], xm[:, b], ACT.Copy).then_inc(s["xm_high"], 1)

                def copy_x(m, b):
                    n = 2 * m + b
                    act.wait_ge(s["reversed"], n + 3)
                    act.sem_inc(s["passed"], 1)
                    nc.scalar.activation(X[:, bass.ds(n, 1), :], rp[b][:].unsqueeze(1), ACT.Copy).then_inc(s["X_ready"], 1)

                root(0, 0)
                copy_u(0, 0)
                root(0, 1)
                copy_u(0, 1)
                with act.Fori(0, TILES // 2 - 1) as i:
                    for b in range(2):
                        root(i + 1, b)
                        copy_u(i + 1, b)
                        high_x(i, b)
                        copy_x(i, b)
                for b in range(2):
                    high_x(TILES // 2 - 1, b)
                    copy_x(TILES // 2 - 1, b)
                act.wait_ge(s["X_ready"], TILES + 2)

            @block.tensor
            def _(pe):
                pe.sem_inc(s["u_turned"], 2)
                pe.sem_inc(s["reversed"], 2)

                def turn_u(m, b):
                    pe.wait_ge(s[f"in{b}"], 32 * (m + 1))
                    for c in range(VC):
                        last = nc.tensor.transpose(tp[b][:, c, :], u[:, b, c * P:(c + 1) * P], const["ident"][:])
                    last.then_inc(s["u_turned"], 1)

                def film(m, b):
                    n = 2 * m + b
                    pe.wait_ge(s["uT_ready"], n + 1)
                    pe.wait_ge(s["film_read"], n + 1)
                    for half in range(2):
                        terms = [(x, w, c) for x, w in ((0, 0), (0, 1), (1, 0)) for c in range(VC)]
                        for k, (x, w, c) in enumerate(terms):
                            last = nc.tensor.matmul(fp[b][:, half, :], lhsT=uT[:, b, x, c, :], rhs=wf_parts[:, w, c, half * D:(half + 1) * D],
                                                    start=(k == 0), stop=(k == len(terms) - 1))
                    last.then_inc(s["film_done"], 1)

                def reverse(m, b):
                    n = 2 * m + b
                    pe.wait_ge(s["xm_split"], n + 1 + 2)
                    pe.wait_ge(s["X_ready"], n + 1)
                    nc.tensor.matmul(rp[b][:], lhsT=anti[:], rhs=xm_parts[:, b, 0], start=True, stop=False)
                    nc.tensor.matmul(rp[b][:], lhsT=anti[:], rhs=xm_parts[:, b, 1], start=False, stop=True).then_inc(s["reversed"], 1)

                pe.sem_inc(s["film_read"], 2)
                pe.wait_ge(s["wf_split"], 1)
                turn_u(0, 0)
                turn_u(0, 1)
                film(0, 0)
                with pe.Fori(0, TILES // 2 - 1) as i:
                    for b in range(2):
                        turn_u(i + 1, b)
                        film(*after(i, b))
                        reverse(i, b)
                film(TILES // 2 - 1, 1)
                reverse(TILES // 2 - 1, 0)
                reverse(TILES // 2 - 1, 1)


LOG2E = 1.0 / math.log(2.0)
LN2_HIGH = 0.693359375
LN2_LOW = math.log(2.0) - LN2_HIGH
HALF_PI = [1.5703125, 4.837512969970703125e-4, 7.54978995489188216e-8]
EXP_TERMS = [1.0 / math.factorial(k) for k in range(7, 0, -1)]
SIN_TERMS = [1.0 / 362880, -1.0 / 5040, 1.0 / 120, -1.0 / 6]
COS_TERMS = [-1.0 / 3628800, 1.0 / 40320, -1.0 / 720, 1.0 / 24, -0.5]
LEVELS = 7
PAIRS = D // 2
CHUNKS = TILES
GROUP = 64
KROW = 2 * P


def layer_weights(nc, sem, const, a, W, root, wf, fb, dram):
    scope, sb, ps = phase_scope(nc)
    SLICES = HID // BANK
    with scope:
        one_row = sb("lw_one_row", [1, NS])
        raw = sb("lw_raw", [P, 4, DC, NS])
        ldt = sb("lw_ldt", [1, D])
        sc = sb("lw_sc", [P, 5, PAIRS])
        wide = {n: sb("lw_" + n, [P, 2, PAIRS]) for n in ("x", "t", "r", "p", "z", "sin", "cos", "m", "o", "b1", "b2", "mag")}
        whole = sb("lw_whole", [P, 2, PAIRS], I32)
        t = [sb(f"lw_t{k}", [P, PAIRS]) for k in range(8)]
        wv = sb("lw_wv", [P, VC, D])
        wvT = sb("lw_wvT", [P, DC, DV])
        film = sb("lw_film", [P, DC, 2 * D])
        gate = sb("lw_gate", [P, 1])
        w1 = sb("lw_w1", [P, 2, DC, BANK])
        offset = sb("lw_offset", [P, DC])
        bias = sb("lw_bias", [1, HID])
        pin = ps("lw_pin", [P, 3, 2, PAIRS])
        tp = ps("lw_tp", [P, VC, BANK])
        mp = [ps(f"lw_mp{k}", [P, BANK]) for k in range(2)]
        s = {n: sem("lw_" + n) for n in (
            "in", "spread", "sc_ready", "root_wanted", "root_ready", "row_set", "wv_in", "film_in0", "film_in1", "fb_in0", "fb_in1", "turned",
            "turn_copied", "multiplied", "copied", "offset_gated", "wf_stored", "fb_stored", "bias_in", "w1_in0", "w1_in1", "biased", "bias_copied",
            "bias_stored")}
        names = ("A_re", "A_im", "C_re", "C_im")
        sides = ("out", "in")
        products = [(c, half) for c in range(VC) for half in range(2)]

        with nc.Block() as block:
            @block.sync
            def _(sp):
                for j, name in enumerate(names):
                    sp.dma_start(raw[:, j], a[name].rearrange("(c p) n -> p c n", p=P)).then_inc(s["in"], 16)
                sp.dma_start(ldt[:], a["log_dt"].unsqueeze(0)).then_inc(s["in"], 16)
                sp.dma_start(wv[:], a["Wv"].rearrange("(c p) n -> p c n", p=P)).then_inc(s["wv_in"], 16)
                sp.dma_start(gate[:], a["mod_gate"].partition_broadcast(P)).then_inc(s["wv_in"], 16)

                def load_film(k):
                    sp.dma_start(film[:], a["W_film_" + sides[k]].rearrange("(c p) n -> p c n", p=P)).then_inc(s[f"film_in{k}"], 16)

                def load_offset(k):
                    sp.dma_start(fb[:], a["b_film_" + sides[k]].partition_broadcast(P)).then_inc(s[f"fb_in{k}"], 16)

                def load_slice(k):
                    sp.dma_start(w1[:, k % 2], a["W1"].rearrange("(c p) n -> p c n", p=P)[:, :, k * BANK:(k + 1) * BANK]).then_inc(s[f"w1_in{k % 2}"], 16)

                load_film(0)
                load_offset(0)
                sp.dma_start(bias[:], a["b1"].unsqueeze(0)).then_inc(s["bias_in"], 16)
                sp.dma_start(offset[:], a["b_ffn"].rearrange("(c p) -> p c", p=P), allow_slow_non_contiguous=True).then_inc(s["bias_in"], 16)
                load_slice(0)
                load_slice(1)
                sp.wait_ge(s["offset_gated"], 1)
                sp.dma_start(dram["fb"][:, :], fb[:]).then_inc(s["fb_stored"], 16)
                sp.wait_ge(s["multiplied"], len(products))
                load_film(1)
                sp.wait_ge(s["fb_stored"], 16)
                load_offset(1)
                sp.wait_ge(s["copied"], len(products))
                sp.dma_start(dram["wf"][:, :, :], wf[:]).then_inc(s["wf_stored"], 16)
                for k in range(2, SLICES):
                    sp.wait_ge(s["biased"], k - 1)
                    load_slice(k)
                sp.wait_ge(s["bias_copied"], SLICES)
                sp.dma_start(dram["b1"].unsqueeze(0), bias[:]).then_inc(s["bias_stored"], 16)
                sp.wait_ge(s["wf_stored"], 16)
                sp.wait_ge(s["bias_stored"], 16)

            @block.gpsimd
            def _(pool):
                pool.wait_ge(s["wv_in"], 32)
                for k in range(2):
                    pool.wait_ge(s[f"fb_in{k}"], 16)
                    nc.gpsimd.tensor_scalar(fb[:, 0:D], fb[:, 0:D], gate[:, 0:1], 1.0, ALU.mult, ALU.add)
                    nc.gpsimd.tensor_scalar(fb[:, D:2 * D], fb[:, D:2 * D], gate[:, 0:1], None, ALU.mult).then_inc(s["offset_gated"], 1)
                pool.wait_ge(s["offset_gated"], 2)

            @block.tensor
            def _(pe):
                pe.wait_ge(s["in"], 16 * 5)
                pe.wait_ge(s["row_set"], 1)
                for e in range(2):
                    at = slice(NS * e, NS * (e + 1))
                    for j in range(4):
                        for c in range(DC):
                            nc.tensor.matmul(pin[at, j // 2, j % 2, NS * c:NS * (c + 1)], lhsT=raw[:, j, c, :],
                                             rhs=const["ident"][:, e::2], start=True, stop=True)
                    last = nc.tensor.matmul(pin[at, 2, 0, :], lhsT=one_row[:], rhs=ldt[0:1, e::2],
                                            start=True, stop=True)
                last.then_inc(s["spread"], 1)

                pe.wait_ge(s["wv_in"], 32)
                for c in range(VC):
                    for k in range(DC):
                        last = nc.tensor.transpose(tp[:, c, k * P:(k + 1) * P], wv[:, c, k * P:(k + 1) * P], const["ident"][:])
                last.then_inc(s["turned"], 1)
                pe.wait_ge(s["turn_copied"], 1)

                def multiply(side):
                    pe.wait_ge(s[f"film_in{side}"], 16)
                    for j, (c, half) in enumerate(products):
                        before = len(products) * side + j - 2
                        if before >= 0:
                            pe.wait_ge(s["copied"], before + 1)
                        for k in range(DC):
                            last = nc.tensor.matmul(mp[j % 2][:], lhsT=wvT[:, k, c * P:(c + 1) * P],
                                                    rhs=film[:, k, half * D:(half + 1) * D], start=(k == 0), stop=(k == DC - 1))
                        last.then_inc(s["multiplied"], 1)

                multiply(0)
                pe.wait_ge(s["bias_in"], 32)
                for k in range(SLICES):
                    pe.wait_ge(s[f"w1_in{k % 2}"], 16 * (k // 2 + 1))
                    if k >= VC:
                        pe.wait_ge(s["bias_copied"], k - VC + 1)
                    bank = tp[0:1, k % VC, :]
                    nc.tensor.matmul(bank, lhsT=one_row[:, 0:1], rhs=bias[:, k * BANK:(k + 1) * BANK], start=True, stop=False)
                    for c in range(DC):
                        last = nc.tensor.matmul(bank, lhsT=offset[:, c:c + 1], rhs=w1[:, k % 2, c, :], start=False, stop=(c == DC - 1))
                    last.then_inc(s["biased"], 1)
                multiply(1)

            @block.scalar
            def _(act):
                act.wait_ge(s["spread"], 1)
                for j in range(5):
                    last = nc.scalar.activation(sc[:, j], pin[:, j // 2, j % 2, :], ACT.Copy)
                last.then_inc(s["sc_ready"], 1)

                act.wait_ge(s["turned"], 1)
                for c in range(VC):
                    last = nc.scalar.activation(wvT[:, :, c * P:(c + 1) * P], tp[:, c, :].rearrange("p (k q) -> p k q", q=P), ACT.Copy)
                last.then_inc(s["turn_copied"], 1)
                act.wait_ge(s["wv_in"], 32)

                def copy(side):
                    for j, (c, half) in enumerate(products):
                        act.wait_ge(s["multiplied"], len(products) * side + j + 1)
                        nc.scalar.activation(wf[:, c, half * D:(half + 1) * D], mp[j % 2][:], ACT.Copy,
                                             scale=gate[:, 0:1]).then_inc(s["copied"], 1)

                copy(0)
                for k in range(SLICES):
                    act.wait_ge(s["biased"], k + 1)
                    nc.scalar.activation(bias[:, k * BANK:(k + 1) * BANK], tp[0:1, k % VC, :], ACT.Copy).then_inc(s["bias_copied"], 1)
                for k in range(2):
                    act.wait_ge(s["root_wanted"], k + 1)
                    nc.scalar.activation(t[1][:], t[0][:], ACT.Sqrt).then_inc(s["root_ready"], 1)
                act.wait_ge(s["wf_stored"], 16)
                copy(1)
                act.wait_ge(s["copied"], 2 * len(products))

            @block.vector
            def _(dve):
                v = nc.vector
                v.memset(one_row[:], 1.0).then_inc(s["row_set"], 1)

                def then(*_):
                    dve.drain()

                def exp(out, x):
                    tt, r, p = wide["t"][:, 0:1], wide["r"][:, 0:1], wide["p"][:, 0:1]
                    n = whole[:, 0:1]
                    then(v.tensor_scalar(x, x, -87.0, 88.0, ALU.max, ALU.min))
                    then(v.tensor_scalar(tt, x, LOG2E, ROUND, ALU.mult, ALU.add))
                    then(v.tensor_scalar(tt, tt, ROUND, None, ALU.subtract))
                    then(v.scalar_tensor_tensor(r, tt, -LN2_HIGH, x, ALU.mult, ALU.add))
                    then(v.scalar_tensor_tensor(r, tt, -LN2_LOW, r, ALU.mult, ALU.add),
                         v.tensor_scalar(x, tt, 127.0, 2.0 ** 23, ALU.add, ALU.mult))
                    then(v.tensor_scalar(p, r, EXP_TERMS[0], None, ALU.mult),
                         v.tensor_copy(n, x))
                    for c in EXP_TERMS[1:]:
                        then(v.scalar_tensor_tensor(p, p, c, r, ALU.add, ALU.mult))
                    then(v.scalar_tensor_tensor(out, p, 1.0, n.bitcast(F32), ALU.add, ALU.mult))

                def sin_cos():
                    x, tt, r, p, z, m, o = (wide[n][:] for n in ("x", "t", "r", "p", "z", "m", "o"))
                    sin, cos, b1, b2 = (wide[n][:] for n in ("sin", "cos", "b1", "b2"))
                    then(v.tensor_scalar(tt, x, 2.0 / math.pi, ROUND, ALU.mult, ALU.add))
                    then(v.tensor_scalar(tt, tt, ROUND, None, ALU.subtract))
                    then(v.scalar_tensor_tensor(r, tt, -HALF_PI[0], x, ALU.mult, ALU.add),
                         v.tensor_scalar(m, tt, 0.25, -0.375, ALU.mult, ALU.add))
                    then(v.scalar_tensor_tensor(r, tt, -HALF_PI[1], r, ALU.mult, ALU.add),
                         v.tensor_scalar(o, m, ROUND, ROUND, ALU.add, ALU.subtract))
                    then(v.scalar_tensor_tensor(r, tt, -HALF_PI[2], r, ALU.mult, ALU.add),
                         v.scalar_tensor_tensor(m, o, -4.0, tt, ALU.mult, ALU.add))
                    then(v.tensor_tensor(z, r, r, ALU.mult), v.tensor_scalar(o, m, 0.5, -0.25, ALU.mult, ALU.add))
                    then(v.tensor_scalar(p, z, SIN_TERMS[0], None, ALU.mult), v.tensor_scalar(cos, z, COS_TERMS[0], None, ALU.mult),
                         v.tensor_scalar(b1, o, ROUND, ROUND, ALU.add, ALU.subtract))
                    for k in range(1, 5):
                        if k < 4:
                            v.scalar_tensor_tensor(p, p, SIN_TERMS[k], z, ALU.add, ALU.mult)
                        then(v.scalar_tensor_tensor(cos, cos, COS_TERMS[k], z, ALU.add, ALU.mult))
                    then(v.scalar_tensor_tensor(sin, p, 1.0, r, ALU.add, ALU.mult),
                         v.tensor_scalar(cos, cos, 1.0, None, ALU.add),
                         v.scalar_tensor_tensor(o, b1, -2.0, m, ALU.mult, ALU.add))
                    then(v.scalar_tensor_tensor(b1, o, 1.0, sin, ALU.subtract, ALU.mult), v.tensor_tensor(b2, o, cos, ALU.mult),
                         v.scalar_tensor_tensor(p, o, 1.0, cos, ALU.subtract, ALU.mult), v.tensor_tensor(z, o, sin, ALU.mult),
                         v.tensor_scalar(x, m, 1.5, -2.0, ALU.is_ge, ALU.mult),
                         v.tensor_scalar(tt, m, 1.5, None, ALU.subtract))
                    then(v.tensor_tensor(b2, b2, b1, ALU.subtract), v.tensor_tensor(z, z, p, ALU.subtract),
                         v.scalar_tensor_tensor(tt, tt, -1.0, tt, ALU.mult, ALU.max))
                    then(v.tensor_scalar(tt, tt, 1.0, 2.0, ALU.is_ge, ALU.mult))
                    then(v.scalar_tensor_tensor(sin, x, 1.0, b2, ALU.add, ALU.mult),
                         v.scalar_tensor_tensor(cos, tt, 1.0, z, ALU.subtract, ALU.mult))

                def square_root(out, k):
                    dve.sem_inc(s["root_wanted"], 1)
                    dve.wait_ge(s["root_ready"], k + 1)
                    then(v.tensor_scalar(t[2][:], t[1][:], 1e-30, None, ALU.max))
                    then(v.reciprocal(t[2][:], t[2][:]))
                    then(v.tensor_tensor(t[2][:], t[2][:], t[0][:], ALU.mult))
                    then(v.tensor_tensor(t[2][:], t[2][:], t[1][:], ALU.add))
                    then(v.tensor_scalar(out, t[2][:], 0.5, None, ALU.mult))

                dve.wait_ge(s["sc_ready"], 1)
                are, aim, cre, cim = (sc[:, j] for j in range(4))
                x = wide["x"]
                dt = sc[:, 4]
                exp(dt.unsqueeze(1), dt.unsqueeze(1))
                then(v.tensor_tensor(x[:, 0], dt, are, ALU.mult))
                then(v.tensor_scalar(x[:, 1], x[:, 0], float(P), None, ALU.mult))
                exp(wide["mag"][:, 0:1], x[:, 0:1])
                exp(wide["mag"][:, 1:2], x[:, 1:2])
                then(v.tensor_tensor(x[:, 0], dt, aim, ALU.mult))
                then(v.tensor_scalar(x[:, 1], x[:, 0], float(P), None, ALU.mult))
                sin_cos()
                for k, level in ((0, 0), (1, LEVELS)):
                    v.tensor_tensor(W[:, level, 0], wide["mag"][:, k], wide["cos"][:, k], ALU.mult)
                    v.tensor_tensor(W[:, level, 1], wide["mag"][:, k], wide["sin"][:, k], ALU.mult)
                dve.drain()
                for level in range(1, LEVELS):
                    re, im = W[:, level - 1, 0], W[:, level - 1, 1]
                    then(v.tensor_tensor(t[0][:], re, im, ALU.subtract), v.tensor_tensor(t[1][:], re, im, ALU.add))
                    then(v.tensor_tensor(W[:, level, 0], t[0][:], t[1][:], ALU.mult),
                         v.scalar_tensor_tensor(W[:, level, 1], re, 2.0, im, ALU.mult, ALU.mult))
                wr, wi = W[:, 0, 0], W[:, 0, 1]
                then(v.tensor_scalar(t[0][:], wr, 1.0, None, ALU.subtract))
                then(v.tensor_tensor(t[1][:], cre, t[0][:], ALU.mult), v.tensor_tensor(t[2][:], cim, wi, ALU.mult),
                     v.tensor_tensor(t[3][:], cre, wi, ALU.mult), v.tensor_tensor(t[4][:], cim, t[0][:], ALU.mult),
                     v.tensor_tensor(t[5][:], are, are, ALU.mult), v.tensor_tensor(t[6][:], aim, aim, ALU.mult))
                then(v.tensor_tensor(t[1][:], t[1][:], t[2][:], ALU.subtract), v.tensor_tensor(t[3][:], t[3][:], t[4][:], ALU.add),
                     v.tensor_tensor(t[5][:], t[5][:], t[6][:], ALU.add))
                then(v.reciprocal(t[5][:], t[5][:]), v.tensor_tensor(t[0][:], t[1][:], are, ALU.mult),
                     v.tensor_tensor(t[2][:], t[3][:], aim, ALU.mult), v.tensor_tensor(t[4][:], t[3][:], are, ALU.mult),
                     v.tensor_tensor(t[6][:], t[1][:], aim, ALU.mult))
                then(v.tensor_tensor(t[0][:], t[0][:], t[2][:], ALU.add), v.tensor_tensor(t[4][:], t[4][:], t[6][:], ALU.subtract))
                dr, di = t[6], t[7]
                then(v.scalar_tensor_tensor(dr[:], t[0][:], 2.0, t[5][:], ALU.mult, ALU.mult),
                     v.scalar_tensor_tensor(di[:], t[4][:], 2.0, t[5][:], ALU.mult, ALU.mult))
                kr, ki, big = dr[:], di[:], sc[:, 2]
                then(v.tensor_tensor(t[0][:], kr, kr, ALU.mult), v.tensor_tensor(t[1][:], ki, ki, ALU.mult))
                then(v.tensor_tensor(t[0][:], t[0][:], t[1][:], ALU.add))
                square_root(big, 0)
                then(v.scalar_tensor_tensor(t[3][:], kr, -1.0, kr, ALU.mult, ALU.max))
                then(v.tensor_tensor(t[0][:], big, t[3][:], ALU.add))
                then(v.tensor_scalar(t[0][:], t[0][:], 0.5, None, ALU.mult))
                square_root(big, 1)
                then(v.tensor_scalar(t[0][:], big, 1e-30, 2.0, ALU.max, ALU.mult))
                then(v.reciprocal(t[0][:], t[0][:]), v.tensor_scalar(t[3][:], ki, 0.0, 2.0, ALU.is_ge, ALU.mult),
                     v.tensor_scalar(t[4][:], kr, 0.0, None, ALU.is_ge))
                then(v.tensor_tensor(t[0][:], t[0][:], ki, ALU.mult), v.scalar_tensor_tensor(t[3][:], t[3][:], 1.0, big, ALU.subtract, ALU.mult))
                then(v.scalar_tensor_tensor(t[1][:], t[0][:], -1.0, t[0][:], ALU.mult, ALU.max), v.tensor_tensor(t[2][:], t[4][:], big, ALU.mult),
                     v.tensor_tensor(t[5][:], t[4][:], t[0][:], ALU.mult), v.scalar_tensor_tensor(t[3][:], t[4][:], 1.0, t[3][:], ALU.subtract, ALU.mult))
                then(v.scalar_tensor_tensor(t[1][:], t[4][:], 1.0, t[1][:], ALU.subtract, ALU.mult))
                then(v.tensor_tensor(root[:, 0], t[2][:], t[1][:], ALU.subtract), v.tensor_tensor(root[:, 1], t[5][:], t[3][:], ALU.subtract))


def s4d(nc, sem, const, a, W, root, X, dram):
    scope, sb, ps = phase_scope(nc)
    GP = GROUP // 2
    GROUPS = PAIRS // GP
    PIECE = 16
    SHARES = {"dve": [(0, 8)], "pool": [(16, 32), (8, 16)]}
    GATHERED = (0, 3, 2, 1)
    PARTS = ((0, 12), (12, 16))
    SPREAD = (3, 2, 0, 1)
    SIDE = P // CHUNKS
    OUT = 4 * SIDE
    BLOCK = SIDE
    LOADS = 4
    UP = 2 * SIDE
    ROWS = GP // SIDE
    NEAR = 10
    HELD = 6
    with scope:
        Q = sb("s4_Q", [P, 2, 2, GP, P + 1])
        S = sb("s4_S", [P, 2, 2, CHUNKS + 1, GP])
        Xg = sb("s4_Xg", [P, 2, GROUP, CHUNKS])
        QT = sb("s4_QT", [P, 2, 4, P])
        M = {n: sb("s4_M_" + n, [P, 2, 2, max(hi - lo for lo, hi in SHARES[n]), PIECE]) for n in SHARES}
        R = M["dve"][:, :, :, 0:GP // PIECE, :].rearrange("p a b k w -> p a b (k w)")
        turn128 = sb("s4_turn128", [P, 2, 2, GP])
        hankel = sb("s4_hankel", [P, LOADS, BLOCK, P])
        UT = sb("s4_UT", [P, 2, 2, P])
        yT = sb("s4_yT", [P, 4, P])
        Kz = sb("s4_Kz", [P, 2, ROWS, 16 * SIDE + 1])
        Krow = sb("s4_Krow", [P, KROW])
        skip = sb("s4_skip", [P, GROUPS])
        tp = [ps(f"s4_tp{k}", [P, 4, P]) for k in range(2)]
        utp = ps("s4_utp", [P, 2, 2, P])
        stp = ps("s4_stp", [P, 2, 2, P])
        ytp = [ps(f"s4_ytp{k}", [P, 4, P]) for k in range(2)]
        yp = ps("s4_yp", [P, OUT, CHUNKS])
        ksp = ps("s4_ksp", [P, P])
        s = {n: sem("s4_" + n) for n in (
            "skip_in", "row_set", "Kz_set", "Kz_ready", "Q_dve", "Q_pool", "Q_first", "turned", "QT_ready", "Xg_ready", "U_done", "UT_ready", "U_turned",
            "U_copied", "K_done", "K_row", "K_stored", "h_in0", "h_in1", "h_in2", "h_in3", "h_used", "S_near", "S_ready", "y_done", "yT_ready", "y_turned",
            "y_copied", "passed")}
        YG = GROUP // OUT
        HG = GROUP // BLOCK
        TG = GP // 2
        UG = GP // UP

        def table(eng, ops, m, b, lo, hi, temp):
            g = 2 * m + b
            count = hi - lo
            used = 1 + max(SPREAD.index(k) for k in range(2 * lo // OUT, -(-2 * hi // OUT)))
            eng.wait_ge(s["y_done"], YG * g + used)
            eng.sem_inc(s["passed"], 1)

            def factor(level, part):
                return W[:, level, part, bass.ds(GP * g + lo, count)]

            for part in range(2):
                ops.tensor_copy(Q[:, b, part, lo:hi, 0], root[:, part, bass.ds(GP * g + lo, count)])
            eng.drain()
            for level in range(LEVELS + 1):
                n = 1 << level
                for at in range(0, n if level < LEVELS else 1, PIECE):
                    w = min(PIECE, n - at) if level < LEVELS else 1
                    for part in range(2):
                        ops.tensor_tensor(temp[:, part, :, 0:count, 0:w], Q[:, b, :, lo:hi, at:at + w],
                                          factor(level, part).unsqueeze(1).unsqueeze(3).broadcast_to([P, 2, count, w]), ALU.mult)
                    eng.drain()
                    ops.tensor_tensor(Q[:, b, 0, lo:hi, n + at:n + at + w], temp[:, 0, 0, 0:count, 0:w], temp[:, 1, 1, 0:count, 0:w], ALU.subtract)
                    last = ops.tensor_tensor(Q[:, b, 1, lo:hi, n + at:n + at + w], temp[:, 0, 1, 0:count, 0:w], temp[:, 1, 0, 0:count, 0:w], ALU.add)
                    if level < LEVELS:
                        eng.drain()
            return last

        with nc.Block() as block:
            @block.sync
            def _(sp):
                by_row = a["D_skip"].rearrange("(g r x) -> x r g", r=ROWS, x=2 * SIDE)
                for j in range(SIDE):
                    for e in range(2):
                        at = CHUNKS * j + ROWS * e
                        sp.dma_start(skip[at:at + ROWS, :], by_row[2 * j + e], allow_slow_non_contiguous=True).then_inc(s["skip_in"], 16)
                K_by_row = dram["K"].rearrange("(g r x) q -> g x r q", r=ROWS, x=2 * SIDE)
                with sp.Fori(0, GROUPS // 2) as i:
                    for b in range(2):
                        g = 2 * i + b
                        sp.wait_ge(s["K_row"], g + 2)
                        sp.sem_inc(s["passed"], 1)
                        for j in range(SIDE):
                            for e in range(2):
                                at = CHUNKS * j + ROWS * e
                                sp.dma_start(K_by_row[g, 2 * j + e, :, :], Krow[at:at + ROWS, :]).then_inc(s["K_stored"], 16)
                        sp.wait_ge(s["K_stored"], 16 * 2 * SIDE * (g + 1))
                        sp.sem_inc(s["passed"], 1)
                        for j in range(HG):
                            sp.wait_ge(s["h_used"], HG * g + j + 1)
                            sp.sem_inc(s["passed"], 1)
                            place = SPREAD[j // (HG // YG)] * (HG // YG) + j % (HG // YG)
                            rows = dram["K"][bass.ds(GROUP * g + place * BLOCK, BLOCK), :]
                            skewed = bass.AP(tensor=rows.tensor, offset=rows.offset, ap=[[1, P], [KROW, BLOCK], [1, P]])
                            sp.dma_start(hankel[:, j % LOADS], skewed).then_inc(s[f"h_in{j % LOADS}"], 16)

            @block.gpsimd
            def _(pool):
                nc.gpsimd.memset(Krow[:], 0.0).then_inc(s["row_set"], 1)
                nc.gpsimd.memset(S[:, :, :, 0, :], 0.0).then_inc(s["row_set"], 1)

                def tables(m, b, shares):
                    for lo, hi in shares:
                        table(pool, nc.gpsimd, m, b, lo, hi, M["pool"]).then_inc(s["Q_pool"], 1)
                        pool.drain()

                tables(0, 0, SHARES["pool"][:1])
                pool.sem_inc(s["Q_pool"], len(SHARES["pool"]) - 1)
                with pool.Fori(0, GROUPS // 2 - 1) as i:
                    for b in range(2):
                        tables(*after(i, b), SHARES["pool"])
                tables(GROUPS // 2 - 1, 1, SHARES["pool"])

            @block.vector
            def _(dve):
                def kernel_weights(m, b, first=False):
                    g = 2 * m + b
                    if not first:
                        dve.wait_ge(s["K_done"], g)
                        dve.sem_inc(s["passed"], 1)
                    for part in range(2):
                        for e in range(2):
                            at = slice(NS * e, NS * (e + 1))
                            last = nc.vector.tensor_scalar(Kz[at, part, :, ROWS * e:ROWS * e + 16 * (SIDE - 1) + 1:16],
                                                           root[at, part, bass.ds(GP * g, GP)].rearrange("p (r j) -> p r j", j=SIDE),
                                                           -1.0 if part else 1.0, None, ALU.mult)
                    last.then_inc(s["Kz_ready"], 1)

                def carry(m, b):
                    g = 2 * m + b
                    dve.drain()
                    dve.wait_ge(s["U_copied"], UG * (g + 1))
                    dve.sem_inc(s["passed"], 1)
                    for part in range(2):
                        nc.vector.tensor_copy(turn128[:, part, part], W[:, LEVELS, 0, bass.ds(GP * g, GP)])
                        nc.vector.tensor_scalar(turn128[:, 1 - part, part], W[:, LEVELS, 1, bass.ds(GP * g, GP)], -1.0 if part else 1.0, None, ALU.mult)
                    dve.drain()
                    for c in range(2, CHUNKS):
                        nc.vector.tensor_tensor(R, S[:, b, :, c - 1, :].unsqueeze(2).broadcast_to([P, 2, 2, GP]), turn128[:], ALU.mult)
                        dve.drain()
                        nc.vector.tensor_tensor(R[:, 0], R[:, 0], R[:, 1], ALU.add)
                        dve.drain()
                        last = nc.vector.tensor_tensor(S[:, b, :, c, :], S[:, b, :, c, :], R[:, 0], ALU.add)
                        if c == CHUNKS - NEAR:
                            dve.sem_inc(s["S_near"], 1)
                        if c < CHUNKS - 1:
                            dve.drain()
                    last.then_inc(s["S_ready"], 1)

                def tables(m, b):
                    for lo, hi in SHARES["dve"]:
                        table(dve, nc.vector, m, b, lo, hi, M["dve"]).then_inc(s["Q_dve"], 1)
                        dve.drain()

                dve.sem_inc(s["y_done"], 2 * YG)
                nc.vector.memset(Kz[:], 0.0)
                tables(0, 0)
                for lo, hi in SHARES["pool"][1:]:
                    table(dve, nc.vector, 0, 0, lo, hi, M["dve"]).then_inc(s["Q_first"], 1)
                    dve.drain()
                kernel_weights(0, 0, first=True)
                with dve.Fori(0, GROUPS // 2 - 1) as i:
                    for b in range(2):
                        tables(*after(i, b))
                        kernel_weights(*after(i, b))
                        carry(i, b)
                tables(GROUPS // 2 - 1, 1)
                kernel_weights(GROUPS // 2 - 1, 1)
                carry(GROUPS // 2 - 1, 0)
                carry(GROUPS // 2 - 1, 1)

            @block.scalar
            def _(act):
                act.sem_inc(s["QT_ready"], 2)
                act.sem_inc(s["yT_ready"], 2)
                act.sem_inc(s["K_row"], 1)
                act.wait_ge(s["skip_in"], 16 * 2 * SIDE)
                act.wait_ge(s["row_set"], 2)

                def gather(m, b, half, first=False):
                    g = 2 * m + b
                    if half == 0:
                        act.wait_ge(s["y_done"], YG * (g + 1))
                        act.sem_inc(s["passed"], 1)
                        nc.scalar.activation(Xg[:, b].rearrange("p d c -> p c d"), X[:, :, bass.ds(GROUP * g, GROUP)],
                                             ACT.Copy).then_inc(s["Xg_ready"], 1)
                    start, end = PARTS[half]
                    for j in range(start, end):
                        act.wait_ge(s["turned"], TG * g + j + 1)
                        nc.scalar.activation(QT[:, j % 2], tp[j % 2][:], ACT.Copy).then_inc(s["QT_ready"], 1)
                        if j % 4 == 1 and j > start + 4:
                            copy_gathered(g, j // 4 - 1)
                        if j % 4 == 3 and j > start + 4:
                            copy_states(g, b, j // 4 - 1)
                    copy_gathered(g, end // 4 - 1)
                    if half:
                        act.wait_ge(s["K_done"], g + 1)
                        if not first:
                            act.sem_inc(s["passed"], 1)
                            act.wait_ge(s["K_stored"], 16 * 2 * SIDE * g)
                        act.sem_inc(s["passed"], 1)
                        for j in range(SIDE):
                            at = slice(CHUNKS * j, CHUNKS * j + 2 * ROWS)
                            nc.scalar.activation(Krow[at, P:KROW - 1], ksp[at, 1:P], ACT.Copy)
                            last = nc.scalar.activation(Krow[at, P - 1:P], ksp[at, 0:1], ACT.Identity, bias=skip[at, bass.ds(g, 1)])
                        last.then_inc(s["K_row"], 1)
                    copy_states(g, b, end // 4 - 1)

                def copy_gathered(g, k):
                    act.wait_ge(s["U_done"], UG * g + k + 1)
                    nc.scalar.activation(UT[:], utp[:], ACT.Copy).then_inc(s["UT_ready"], 1)

                def copy_states(g, b, k):
                    act.wait_ge(s["U_turned"], UG * g + k + 1)
                    for part in range(2):
                        last = nc.scalar.activation(S[:, b, part, 1:CHUNKS + 1, UP * GATHERED[k]:UP * (GATHERED[k] + 1)].rearrange("p c (q k) -> p q k c", k=SIDE),
                                                    stp[:, :, part].rearrange("p q (k c) -> p q k c", k=SIDE), ACT.Copy,
                                                    scale=-1.0 if part else 1.0)
                    last.then_inc(s["U_copied"], 1)

                def spread(m, b):
                    g = 2 * m + b
                    for j in range(YG + 1):
                        if j < YG:
                            act.wait_ge(s["y_done"], YG * g + j + 1 + 2 * YG)
                            act.sem_inc(s["passed"], 1)
                            act.wait_ge(s["y_turned"], YG * g + j + 1)
                            nc.scalar.activation(yT[:], ytp[j % 2][:], ACT.Copy).then_inc(s["yT_ready"], 1)
                        if j:
                            act.wait_ge(s["y_turned"], YG * g + j + 1)
                            act.sem_inc(s["passed"], 1)
                            nc.scalar.activation(X[:, :, bass.ds(GROUP * g + SPREAD[j - 1] * OUT, OUT)], yp[:].rearrange("p d c -> p c d"),
                                                 ACT.Copy).then_inc(s["y_copied"], 1)

                gather(0, 0, 0)
                gather(0, 0, 1, first=True)
                with act.Fori(0, GROUPS // 2 - 1) as i:
                    for b in range(2):
                        gather(*after(i, b), 0)
                        spread(i, b)
                        gather(*after(i, b), 1)
                gather(GROUPS // 2 - 1, 1, 0)
                spread(GROUPS // 2 - 1, 0)
                gather(GROUPS // 2 - 1, 1, 1)
                spread(GROUPS // 2 - 1, 1)
                act.wait_ge(s["y_copied"], YG * GROUPS + 1)

            @block.tensor
            def _(pe):
                pe.sem_inc(s["h_used"], LOADS)
                pe.sem_inc(s["y_copied"], 1)
                pe.sem_inc(s["y_turned"], 1)

                def gather(m, b, half, first=False):
                    g = 2 * m + b
                    start, end = PARTS[half]

                    def first_of(j):
                        return UP * GATHERED[j // 4] + 2 * (j % 4)

                    def turn_tables(j):
                        for name in SHARES:
                            for n, (lo, hi) in enumerate(SHARES[name]):
                                if j == min(k for k in range(TG) if lo <= first_of(k) < hi):
                                    if first and name == "pool" and n:
                                        pe.wait_ge(s["Q_first"], n)
                                    else:
                                        pe.wait_ge(s["Q_" + name], len(SHARES[name]) * g + n + 1)
                        pe.wait_ge(s["QT_ready"], TG * g + j + 1)
                        for k in range(2):
                            for part in range(2):
                                last = nc.tensor.transpose(tp[j % 2][:, 2 * k + part, :], Q[:, b, part, first_of(j) + k, 1:P + 1], const["ident"][:])
                        last.then_inc(s["turned"], 1)

                    def sum_kernel(j):
                        if j == 0:
                            pe.wait_ge(s["Kz_ready"], g + 1)
                            pe.wait_ge(s["K_row"], g + 1)
                        for part in range(2):
                            for k in range(2):
                                pair = first_of(j) + k
                                at = CHUNKS * (pair % SIDE)
                                last = nc.tensor.matmul(ksp[at:at + 2 * ROWS, :], lhsT=Kz[:, part].rearrange("p r x -> p (r x)")[:, 16 * pair:16 * pair + 16],
                                                        rhs=Q[:, b, part, pair, 0:P], start=(j < SIDE // 2 and part == 0),
                                                        stop=(j >= TG - SIDE // 2 and part == 1))
                        if j == TG - 1:
                            last.then_inc(s["K_done"], 1)

                    def turn_states(k):
                        pe.wait_ge(s["UT_ready"], UG * g + k + 1)
                        if k:
                            pe.wait_ge(s["U_copied"], UG * g + k)
                        for h in range(2):
                            for part in range(2):
                                last = nc.tensor.transpose(stp[:, h, part, :], UT[:, h, part, :], const["ident"][:])
                        last.then_inc(s["U_turned"], 1)

                    turn_tables(start)
                    for j in range(start, end):
                        if j == HELD and not first:
                            pe.wait_ge(s["S_near"], g)
                        if j < end - 1:
                            turn_tables(j + 1)
                        sum_kernel(j)
                        pe.wait_ge(s["QT_ready"], TG * g + j + 3)
                        if j == 0:
                            pe.wait_ge(s["Xg_ready"], g + 1)
                        elif j % 4 == 0:
                            pe.wait_ge(s["UT_ready"], UG * g + j // 4)
                        for e in range(2):
                            for k in range(2):
                                pair = first_of(j) + k
                                at = CHUNKS * (pair % SIDE)
                                last = nc.tensor.matmul(utp[at:at + CHUNKS, pair // SIDE % 2, :, NS * e:NS * (e + 1)],
                                                        lhsT=Xg[:, b, 2 * pair + e, :], rhs=QT[:, j % 2, 2 * k:2 * k + 2, NS * e:NS * (e + 1)],
                                                        start=True, stop=True)
                        if j % 4 == 3:
                            last.then_inc(s["U_done"], 1)
                        if j % 4 == 2 and j > start + 4:
                            turn_states(j // 4 - 1)
                    turn_states(end // 4 - 1)

                def spread(m, b):
                    g = 2 * m + b
                    pe.wait_ge(s["S_ready"], g + 1)

                    def products(j):
                        pe.wait_ge(s["yT_ready"], YG * g + j + 1)
                        for q in range(OUT // SIDE):
                            load = j * (OUT // SIDE) + q
                            channels = [SPREAD[j] * OUT + SIDE * q + k for k in range(SIDE)]
                            pe.wait_ge(s[f"h_in{load % LOADS}"], 16 * (HG // LOADS * g + load // LOADS + 1))
                            for k, d in enumerate(channels):
                                last = nc.tensor.matmul(ytp[j % 2][CHUNKS * k:CHUNKS * (k + 1), q, :], lhsT=Xg[:, b, d, :],
                                                        rhs=hankel[:, load % LOADS, k, :], start=True, stop=False)
                            last.then_inc(s["h_used"], 1)
                            for part in range(2):
                                for k, d in enumerate(channels):
                                    at = slice(NS * (d % 2), NS * (d % 2 + 1))
                                    last = nc.tensor.matmul(ytp[j % 2][CHUNKS * k:CHUNKS * (k + 1), q, :], lhsT=S[at, b, part, 0:CHUNKS, d // 2],
                                                            rhs=Q[at, b, part, d // 2, 0:P], start=False, stop=(part == 1))
                        last.then_inc(s["y_done"], 1)

                    def turn(j):
                        pe.wait_ge(s["yT_ready"], YG * g + j + 3)
                        pe.wait_ge(s["y_copied"], YG * g + j + 1)
                        for q in range(OUT // SIDE):
                            last = nc.tensor.transpose(yp[:, SIDE * q:SIDE * (q + 1), :].rearrange("p d c -> p (d c)"), yT[:, q, :], const["ident"][:])
                        last.then_inc(s["y_turned"], 1)

                    products(0)
                    for j in range(YG):
                        if j + 1 < YG:
                            products(j + 1)
                        turn(j)

                gather(0, 0, 0, first=True)
                gather(0, 0, 1, first=True)
                with pe.Fori(0, GROUPS // 2 - 1) as i:
                    for b in range(2):
                        gather(*after(i, b), 0)
                        spread(i, b)
                        gather(*after(i, b), 1)
                gather(GROUPS // 2 - 1, 1, 0)
                spread(GROUPS // 2 - 1, 0)
                gather(GROUPS // 2 - 1, 1, 1)
                spread(GROUPS // 2 - 1, 1)


LEAST = 1e-5
LEVEL = 127.0


def next_weights(Y):
    return Y[:, 0:HID // P, :], Y[:, HID // P:2 * HID // P, :].rearrange("p (c k) d -> p c (k d)", c=DC)


def feed_forward(nc, sem, const, a, wf, fb, W1, W2, b1, Y, qstep, mean, dram):
    scope, sb, ps = phase_scope(nc)
    QUADS = TILES // QUAD
    FC = HID // P
    TURN_U, FILM, TURN_Q = (2, 5, 8, 11), (3, 6, 9, 12), (7, 10, 13, 14)
    with scope:
        gain = sb("ff_gain", [P, DC])
        rows = {n: sb("ff_" + n, [P, D]) for n in ("b2", "g_norm_out", "b_norm_out")}
        u = sb("ff_u", [P, DV])
        uT = sb("ff_uT", [P, VC, P])
        xt = sb("ff_xt", [P, 2, QUAD, D])
        x = sb("ff_x", [P, QUAD, D])
        h = sb("ff_h", [P, 2, D])
        hT = sb("ff_hT", [P, DC, QUAD * P])
        act_out = sb("ff_gelu", [P, 2, QUAD * P])
        sc = sb("ff_scale", [P, D])
        q = sb("ff_q", [P, QUAD, D], BF16)
        qT = sb("ff_qT", [P, DC, QUAD * P], BF16)
        stats = {n: sb("ff_stats_" + n, [P, QUAD, 6]) for n in ("sum", "out", "x")}
        mv = {n: sb("ff_mv_" + n, [P, QUAD, 2]) for n in ("sum", "out", "x")}
        rstd = {n: sb("ff_rstd_" + n, [P, QUAD]) for n in ("sum", "out", "x")}
        most = sb("ff_most", [P, QUAD])
        steps = sb("ff_steps", [P, QUAD])
        zero = sb("ff_zero", [P, DC], BF16)
        every = sb("ff_every", [P, P])
        sizes = sb("ff_sizes", [P, FC + DC])
        sums = sb("ff_sums", [P, 2])
        inverse = sb("ff_inverse", [P, 2])
        fl = [ps(f"ff_fl{k}", [P, BANK]) for k in range(2)]
        fp = [ps(f"ff_fp{k}", [P, BANK]) for k in range(2)]
        acc = ps("ff_acc", [P, QUAD, BANK])
        s = {n: sem("ff_" + n) for n in (
            "rows_in", "u_in", "xt_in0", "xt_in1", "x_in", "u_turned", "uT_ready", "film_done", "film_read", "factors", "modulated",
            "sum_wanted", "sum_ready", "h_ready", "h_turned", "hT_ready", "hidden", "gelu_done", "acc_done", "acc_read",
            "out_wanted", "out_ready", "out_normed", "x_ready", "xb_ready", "x_wanted", "x_root", "x_read", "q_ready", "q_turned", "qT_ready",
            "next_in0", "next_in1", "summed", "totalled", "film_in", "W1_in", "W2_in", "gained", "xt_free", "qT_stored", "x_stored", "biased", "edges", "passed")}

        next_w1, next_w2 = next_weights(Y)

        with nc.Block() as block:
            @block.sync
            def _(sp):
                sp.dma_start(wf[:], dram["wf"][:, :, :]).then_inc(s["film_in"], 16)
                sp.dma_start(fb[:], dram["fb"][:, :]).then_inc(s["film_in"], 16)
                for n in rows:
                    sp.dma_start(rows[n][:], a[n].partition_broadcast(P)).then_inc(s["rows_in"], 16)
                xt_q = dram["xt"].rearrange("(q k p) d -> q p k d", k=QUAD, p=P)
                x_q = a["x"].rearrange("(q k p) d -> q p k d", k=QUAD, p=P)
                x2_q = dram["x2"].rearrange("(q k p) d -> q p k d", k=QUAD, p=P)

                def load_u(m, b, tiles):
                    for k in tiles:
                        n = QUAD * (2 * m + b) + k
                        sp.wait_ge(s["u_turned"], n + 1)
                        sp.sem_inc(s["passed"], 1)
                        sp.dma_start(u[:], dram["u"][bass.ts(n, P), :]).then_inc(s["u_in"], 16)

                def load_xt(m, b):
                    g = 2 * m + b
                    sp.wait_ge(s["xt_free"], g + 1)
                    sp.sem_inc(s["passed"], 1)
                    sp.dma_start(xt[:, b], xt_q[g, :, :, :]).then_inc(s[f"xt_in{b}"], 16)

                def load_back(m, b, first=False):
                    g = 2 * m + b
                    if not first:
                        sp.wait_ge(s["x_read"], g)
                        sp.sem_inc(s["passed"], 1)
                        sp.wait_ge(s["x_stored"], 16 * g)
                        sp.sem_inc(s["passed"], 1)
                    sp.dma_start(x[:], x_q[g, :, :, :]).then_inc(s["x_in"], 16)

                def store(m, b):
                    g = 2 * m + b
                    sp.wait_ge(s["x_ready"], QUAD * (g + 1))
                    sp.sem_inc(s["passed"], 1)
                    sp.dma_start(x2_q[g, :, :, :], x[:]).then_inc(s["x_stored"], 16)

                load_xt(0, 0)
                load_u(0, 0, range(QUAD))
                load_xt(0, 1)
                load_back(0, 0, first=True)
                load_u(0, 1, range(QUAD))
                with sp.Fori(0, QUADS // 2 - 1) as i:
                    for b in range(2):
                        load_u(i + 1, b, (0,))
                        store(i, b)
                        load_back(*after(i, b))
                        load_xt(i + 1, b)
                        load_u(i + 1, b, range(1, QUAD))
                sp.wait_ge(s["modulated"], TILES)
                sp.dma_start(next_w1, a["ffn_w1"].rearrange("(f p) d -> p f d", p=P)).then_inc(s["next_in0"], 16)
                sp.dma_start(next_w2, a["ffn_w2"].rearrange("(c p) f -> p c f", p=P)).then_inc(s["next_in1"], 16)
                store(QUADS // 2 - 1, 0)
                load_back(QUADS // 2 - 1, 1)
                store(QUADS // 2 - 1, 1)
                sp.wait_ge(s["x_stored"], 16 * QUADS)

            @block.gpsimd
            def _(pool):
                nc.gpsimd.memset(zero[:], 0.0).then_inc(s["edges"], 1)
                pool.wait_ge(s["rows_in"], 16 * 3)
                pool.wait_ge(s["film_in"], 32)

                def front(m, b):
                    g = 2 * m + b
                    for k in range(QUAD):
                        n = QUAD * g + k
                        pool.wait_ge(s["factors"], n + 1)
                        pool.sem_inc(s["passed"], 1)
                        nc.gpsimd.tensor_tensor(sc[:].unsqueeze(1), Y[:, bass.ds(n, 1), :], sc[:].unsqueeze(1), ALU.mult)
                        nc.gpsimd.tensor_tensor(xt[:, b, k], xt[:, b, k], fb[:, D:2 * D], ALU.add)
                        pool.drain()
                        nc.gpsimd.tensor_tensor(xt[:, b, k], xt[:, b, k], sc[:], ALU.add).then_inc(s["modulated"], 1)

                def bias(m, b):
                    g = 2 * m + b
                    for k in range(QUAD):
                        pool.wait_ge(s["h_ready"], QUAD * g + k + 1)
                        pool.sem_inc(s["passed"], 1)
                        last = nc.gpsimd.tensor_tensor(xt[:, b, k], xt[:, b, k], rows["b2"][:], ALU.add)
                    last.then_inc(s["biased"], 1)

                def back(m, b):
                    g = 2 * m + b
                    pool.wait_ge(s["x_in"], 16 * (g + 1))
                    pool.sem_inc(s["passed"], 1)
                    nc.gpsimd.tensor_tensor(x[:], x[:], rows["b_norm_out"][:].unsqueeze(1).broadcast_to([P, QUAD, D]), ALU.add)
                    for k in range(QUAD):
                        pool.wait_ge(s["out_normed"], QUAD * g + k + 1)
                        pool.sem_inc(s["passed"], 1)
                        nc.gpsimd.tensor_tensor(xt[:, b, k], xt[:, b, k], rows["g_norm_out"][:], ALU.mult)
                        pool.drain()
                        nc.gpsimd.tensor_tensor(x[:, k], x[:, k], xt[:, b, k], ALU.add).then_inc(s["x_ready"], 1)

                front(0, 0)
                bias(0, 0)
                front(0, 1)
                bias(0, 1)
                with pool.Fori(0, QUADS // 2 - 1) as i:
                    for b in range(2):
                        back(i, b)
                        front(i + 1, b)
                        bias(i + 1, b)
                back(QUADS // 2 - 1, 0)
                back(QUADS // 2 - 1, 1)

            @block.vector
            def _(dve):
                def front(m, b):
                    g = 2 * m + b
                    for k in range(QUAD):
                        n = QUAD * g + k
                        dve.wait_ge(s["film_done"], n + 1)
                        dve.sem_inc(s["passed"], 1)
                        if k:
                            dve.wait_ge(s["modulated"], n)
                        else:
                            dve.wait_ge(s[f"xt_in{b}"], 16 * (m + 1))
                        nc.vector.tensor_tensor(sc[:], fl[0][:], fb[:, 0:D], ALU.add)
                        nc.vector.tensor_tensor(xt[:, b, k], fl[1][:], xt[:, b, k], ALU.add)
                        dve.drain()
                        dve.sem_inc(s["film_read"], 1)
                        dve.sem_inc(s["factors"], 1)
                    for k in range(QUAD):
                        dve.wait_ge(s["modulated"], QUAD * g + k + 1)
                        dve.sem_inc(s["passed"], 1)
                        nc.vector.bn_stats(stats["sum"][:, k, :], xt[:, b, k, :])
                    norm_factors("sum", g)
                    for k in range(QUAD):
                        dve.wait_ge(s["h_turned"], QUAD * g + k + 1)
                        nc.vector.tensor_scalar(h[:, k % 2], xt[:, b, k], mv["sum"][:, k, 0:1], rstd["sum"][:, k:k + 1],
                                                ALU.subtract, ALU.mult).then_inc(s["h_ready"], 1)

                def norm_factors(name, g):
                    dve.drain()
                    for k in range(QUAD):
                        last = nc.vector.bn_aggr(mv[name][:, k, :], stats[name][:, k, :])
                    last.then_inc(s[name + "_wanted"], 1)
                    dve.wait_ge(s[{"sum": "sum_ready", "out": "out_ready", "x": "x_root"}[name]], g + 1)
                    nc.vector.reciprocal(rstd[name][:], rstd[name][:])
                    dve.drain()

                def back(m, b):
                    g = 2 * m + b
                    dve.wait_ge(s["acc_done"], g + 1)
                    dve.sem_inc(s["passed"], 1)
                    dve.wait_ge(s["biased"], g + 1)
                    for k in range(QUAD):
                        last = nc.vector.tensor_tensor(xt[:, b, k], acc[:, k, :], xt[:, b, k], ALU.add)
                    last.then_inc(s["acc_read"], 1)
                    dve.drain()
                    for k in range(QUAD):
                        nc.vector.bn_stats(stats["out"][:, k, :], xt[:, b, k, :])
                    norm_factors("out", g)
                    for k in range(QUAD):
                        nc.vector.tensor_scalar(xt[:, b, k], xt[:, b, k], mv["out"][:, k, 0:1], rstd["out"][:, k:k + 1],
                                                ALU.subtract, ALU.mult).then_inc(s["out_normed"], 1)
                    for k in range(QUAD):
                        dve.wait_ge(s["x_ready"], QUAD * g + k + 1)
                        dve.sem_inc(s["passed"], 1)
                        nc.vector.bn_stats(stats["x"][:, k, :], x[:, k, :])
                    norm_factors("x", g)
                    for k in range(QUAD):
                        nc.vector.tensor_scalar(xt[:, b, k], x[:, k], mv["x"][:, k, 0:1], rstd["x"][:, k:k + 1], ALU.subtract, ALU.mult)
                    dve.drain()
                    dve.sem_inc(s["x_read"], 1)
                    nc.vector.tensor_reduce(most[:], xt[:, b], AX.X, ALU.max, apply_absolute_value=True)
                    dve.drain()
                    nc.vector.tensor_scalar(most[:], most[:], LEAST, None, ALU.max)
                    dve.drain()
                    nc.vector.tensor_scalar(qstep[:, bass.ds(QUAD * g, QUAD)], most[:], 1.0 / LEVEL, None, ALU.mult)
                    nc.vector.reciprocal(steps[:], most[:])
                    dve.drain()
                    nc.vector.tensor_scalar(steps[:], steps[:], LEVEL, None, ALU.mult)
                    dve.drain()
                    for k in range(QUAD):
                        nc.vector.tensor_scalar(xt[:, b, k], xt[:, b, k], steps[:, k:k + 1], ROUND, ALU.mult, ALU.add)
                    dve.drain()
                    for k in range(QUAD):
                        dve.wait_ge(s["q_turned"], QUAD * g + k + 1)
                        nc.vector.tensor_scalar(q[:, k], xt[:, b, k], ROUND, None, ALU.subtract).then_inc(s["q_ready"], 1)
                    dve.drain()
                    dve.sem_inc(s["xt_free"], 1)

                def round_next_weights():
                    dve.wait_ge(s["next_in0"], 16)
                    nc.vector.tensor_reduce(sizes[:, 0:FC], next_w1, AX.X, ALU.add, apply_absolute_value=True)
                    dve.wait_ge(s["next_in1"], 16)
                    nc.vector.tensor_reduce(sizes[:, FC:FC + DC], next_w2, AX.X, ALU.add, apply_absolute_value=True)
                    dve.drain()
                    nc.vector.tensor_reduce(sums[:, 0:1], sizes[:, 0:FC], AX.X, ALU.add)
                    nc.vector.tensor_reduce(sums[:, 1:2], sizes[:, FC:FC + DC], AX.X, ALU.add).then_inc(s["summed"], 1)
                    dve.wait_ge(s["totalled"], 1)
                    nc.vector.tensor_scalar(mean[:], fl[0][:, 0:2], 1.0 / (HID * D), LEAST, ALU.mult, ALU.max)
                    dve.drain()
                    nc.vector.reciprocal(inverse[:], mean[:])
                    dve.drain()
                    for j, w in enumerate((next_w1, next_w2)):
                        nc.vector.tensor_scalar(w, w, inverse[:, j:j + 1], 1.0, ALU.mult, ALU.min)
                    dve.drain()
                    for w in (next_w1, next_w2):
                        nc.vector.tensor_scalar(w, w, -1.0, ROUND, ALU.max, ALU.add)
                    dve.drain()

                nc.vector.memset(every[:], 1.0)
                dve.sem_inc(s["xt_free"], 2)
                dve.wait_ge(s["film_in"], 32)
                front(0, 0)
                dve.wait_ge(s["W1_in"], 16 * 3)
                for c in range(DC):
                    last = nc.vector.tensor_scalar(W1[:, c, :], W1[:, c, :], gain[:, c:c + 1], None, ALU.mult)
                last.then_inc(s["gained"], 1)
                front(0, 1)
                with dve.Fori(0, QUADS // 2 - 1) as i:
                    for b in range(2):
                        back(i, b)
                        front(i + 1, b)
                back(QUADS // 2 - 1, 0)
                round_next_weights()
                back(QUADS // 2 - 1, 1)

            @block.scalar
            def _(act):
                act.wait_ge(s["film_in"], 32)
                act.dma_start(W1[:], a["W1"].rearrange("(c p) n -> p c n", p=P)).then_inc(s["W1_in"], 16)
                act.dma_start(gain[:], a["g_ffn"].rearrange("(c p) -> p c", p=P), allow_slow_non_contiguous=True).then_inc(s["W1_in"], 16)
                act.dma_start(b1[:], dram["b1"].rearrange("(f p) -> p f", p=P), allow_slow_non_contiguous=True).then_inc(s["W1_in"], 16)
                act.dma_start(W2[:], a["W2"].rearrange("(f p) n -> p f n", p=P)).then_inc(s["W2_in"], 16)
                act.sem_inc(s["qT_ready"], 1)
                act.sem_inc(s["hT_ready"], 2)
                act.wait_ge(s["edges"], 1)
                act.dma_start(dram["qT"][:, :, 0], zero[:], allow_slow_non_contiguous=True).then_inc(s["qT_stored"], 16)
                act.dma_start(dram["qT"][:, :, T + 1], zero[:], allow_slow_non_contiguous=True).then_inc(s["qT_stored"], 16)

                def root(name, ready, g):
                    act.wait_ge(s[name + "_wanted"], g + 1)
                    nc.scalar.activation(rstd[name][:], mv[name][:, :, 1], ACT.Sqrt, bias=const["eps"][:, 0:1]).then_inc(s[ready], 1)

                def copy_u(g, k):
                    act.wait_ge(s["u_turned"], QUAD * g + k + 1 + 1)
                    nc.scalar.activation(uT[:], fl[0][:, 0:DV].rearrange("p (c t) -> p c t", t=P), ACT.Copy).then_inc(s["uT_ready"], 1)

                def copy_h(g, k):
                    act.wait_ge(s["h_turned"], QUAD * g + k + 1 + 2)
                    nc.scalar.activation(hT[:, :, k * P:(k + 1) * P], fl[k % 2][:].rearrange("p (c t) -> p c t", t=P), ACT.Copy).then_inc(s["hT_ready"], 1)

                def copy_q(g, k):
                    if k == 0:
                        act.wait_ge(s["qT_stored"], 16 * (g + 2))
                        act.sem_inc(s["passed"], 1)
                    act.wait_ge(s["q_turned"], QUAD * (g + 1) + k + 1)
                    nc.scalar.activation(qT[:, :, k * P:(k + 1) * P], fl[1][:].bitcast(BF16)[:, 0:D].rearrange("p (c t) -> p c t", t=P),
                                         ACT.Copy).then_inc(s["qT_ready"], 1)
                    if k == QUAD - 1:
                        act.wait_ge(s["qT_ready"], QUAD * (g + 1) + 1)
                        act.sem_inc(s["passed"], 1)
                        act.dma_start(dram["qT"][:, :, bass.ds(QUAD * P * g + 1, QUAD * P)], qT[:]).then_inc(s["qT_stored"], 16)

                def turn(m, b, front=True, back=True):
                    g = 2 * m + b
                    old, new = 2 * before(m, b)[0] + before(m, b)[1], 2 * after(m, b)[0] + after(m, b)[1]
                    for k in range(QUAD):
                        copy_h(g, k)
                    for f in range(FC):
                        if front and f in TURN_U:
                            copy_u(new, TURN_U.index(f))
                        if back and f in TURN_Q:
                            copy_q(old, TURN_Q.index(f))
                        act.wait_ge(s["hidden"], FC * g + f + 1)
                        nc.scalar.activation(act_out[:, f % 2], fp[f % 2][:], ACT.Gelu, bias=b1[:, f:f + 1]).then_inc(s["gelu_done"], 1)
                        if back and f == 1:
                            root("out", "out_ready", old)
                        if back and f == 4:
                            root("x", "x_root", old)
                        if front and f == FC - 2:
                            root("sum", "sum_ready", new)

                for k in range(QUAD):
                    copy_u(0, k)
                root("sum", "sum_ready", 0)
                act.wait_ge(s["W1_in"], 16 * 3)
                turn(0, 0, back=False)
                with act.Fori(0, QUADS // 2 - 1) as i:
                    turn(i, 1)
                    turn(i + 1, 0)
                turn(QUADS // 2 - 1, 1, front=False)
                root("out", "out_ready", QUADS - 1)
                root("x", "x_root", QUADS - 1)
                for k in range(QUAD):
                    copy_q(QUADS - 1, k)
                act.wait_ge(s["qT_stored"], 16 * (QUADS + 2))

            @block.tensor
            def _(pe):
                pe.sem_inc(s["u_turned"], 1)
                pe.sem_inc(s["h_turned"], 2)
                pe.sem_inc(s["q_turned"], QUAD)
                pe.sem_inc(s["gelu_done"], 2)

                def turn_u(m, b, k):
                    n = QUAD * (2 * m + b) + k
                    pe.wait_ge(s["u_in"], 16 * (n + 1))
                    if k:
                        pe.wait_ge(s["film_read"], n)
                    for c in range(VC):
                        last = nc.tensor.transpose(fl[0][:, c * P:(c + 1) * P], u[:, c * P:(c + 1) * P], const["ident"][:])
                    last.then_inc(s["u_turned"], 1)

                def film(m, b, k):
                    n = QUAD * (2 * m + b) + k
                    pe.wait_ge(s["uT_ready"], n + 1)
                    for half in range(2):
                        for c in range(VC):
                            last = nc.tensor.matmul(fl[half][:], lhsT=uT[:, c, :], rhs=wf[:, c, half * D:(half + 1) * D],
                                                    start=(c == 0), stop=(c == VC - 1))
                    last.then_inc(s["film_done"], 1)

                def turn_h(m, b, k):
                    n = QUAD * (2 * m + b) + k
                    pe.wait_ge(s["h_ready"], n + 1)
                    if k >= 2:
                        pe.wait_ge(s["hT_ready"], n + 1)
                    for c in range(DC):
                        last = nc.tensor.transpose(fl[k % 2][:, c * P:(c + 1) * P], h[:, k % 2, c * P:(c + 1) * P], const["ident"][:])
                    last.then_inc(s["h_turned"], 1)

                def turn_q(m, b, k):
                    n = QUAD * (2 * m + b) + k
                    pe.wait_ge(s["q_ready"], n + 1)
                    for c in range(DC):
                        last = nc.tensor.transpose(fl[1][:].bitcast(BF16)[:, c * P:(c + 1) * P], q[:, k, c * P:(c + 1) * P],
                                                   const["ident_bf"][:])
                    last.then_inc(s["q_turned"], 1)

                def second(m, b, f):
                    g = 2 * m + b
                    pe.wait_ge(s["gelu_done"], FC * g + f + 1 + 2)
                    if f == 0:
                        pe.wait_ge(s["acc_read"], g + 1)
                    for k in range(QUAD):
                        last = nc.tensor.matmul(acc[:, k, :], lhsT=act_out[:, f % 2, k * P:(k + 1) * P], rhs=W2[:, f, :],
                                                start=(f == 0), stop=(f == FC - 1))
                    if f == FC - 1:
                        last.then_inc(s["acc_done"], 1)

                def turn(m, b, front=True, back=True):
                    g = 2 * m + b
                    for k in range(QUAD):
                        if k == 1 and back:
                            pe.wait_ge(s["qT_ready"], QUAD * (g - 1) + 1)
                        turn_h(m, b, k)
                    pe.wait_ge(s["hT_ready"], QUAD * (g + 1) + 2)
                    if not back:
                        pe.wait_ge(s["gained"], 1)
                        pe.wait_ge(s["W2_in"], 16)
                    for f in range(FC):
                        pe.wait_ge(s["gelu_done"], FC * g + f + 1)
                        for c in range(DC):
                            last = nc.tensor.matmul(fp[f % 2][:], lhsT=W1[:, c, f * P:(f + 1) * P], rhs=hT[:, c, :],
                                                    start=(c == 0), stop=(c == DC - 1))
                        last.then_inc(s["hidden"], 1)
                        if f:
                            second(m, b, f - 1)
                        if not front and f == FC // 2 + 2:
                            pe.wait_ge(s["summed"], 1)
                            nc.tensor.matmul(fl[0][:, 0:2], lhsT=every[:], rhs=sums[:], start=True, stop=True).then_inc(s["totalled"], 1)
                        if front and f in TURN_U:
                            turn_u(*after(m, b), TURN_U.index(f))
                        if front and f in FILM:
                            k = FILM.index(f)
                            if back and f > TURN_Q[0]:
                                done = sum(t < f for t in TURN_Q)
                                pe.wait_ge(s["qT_ready"], QUAD * (2 * before(m, b)[0] + before(m, b)[1]) + done + 1)
                            film(*after(m, b), k)
                        if back and f in TURN_Q:
                            k = TURN_Q.index(f)
                            done = sum(t < f for t in FILM)
                            if front:
                                pe.wait_ge(s["film_read"], QUAD * (2 * after(m, b)[0] + after(m, b)[1]) + done)
                            if k:
                                pe.wait_ge(s["qT_ready"], QUAD * (2 * before(m, b)[0] + before(m, b)[1]) + k + 1)
                            turn_q(*before(m, b), k)
                    second(m, b, FC - 1)

                pe.sem_inc(s["acc_read"], 1)
                pe.wait_ge(s["film_in"], 32)
                for k in range(QUAD):
                    turn_u(0, 0, k)
                    film(0, 0, k)
                pe.wait_ge(s["film_read"], QUAD)
                turn(0, 0, back=False)
                with pe.Fori(0, QUADS // 2 - 1) as i:
                    turn(i, 1)
                    turn(i + 1, 0)
                turn(QUADS // 2 - 1, 1, front=False)
                for k in range(QUAD):
                    if k:
                        pe.wait_ge(s["qT_ready"], QUAD * (QUADS - 1) + k + 1)
                    turn_q(QUADS // 2 - 1, 1, k)


def quantise_weights(nc, sem, const, Y, W1q, W2q, mean, qstep, rowstep):
    scope, sb, ps = phase_scope(nc)
    FC = HID // P
    with scope:
        w1, w2 = next_weights(Y)
        w1b = sb("qw_w1b", [P, FC, D], BF16)
        w2b = sb("qw_w2b", [P, DC, HID], BF16)
        every = sb("qw_every", [P, P])
        diag = sb("qw_diag", [P, 2, QUAD, P])
        tp = [ps(f"qw_tp{k}", [P, 2 * BANK], BF16) for k in range(2)]
        rp = [ps(f"qw_rp{k}", [P, BANK]) for k in range(2)]
        s = {n: sem("qw_" + n) for n in ("quantised", "turned", "copied0", "copied1", "diag_ready", "spread", "rows_copied")}

        with nc.Block() as block:
            @block.vector
            def _(dve):
                nc.vector.memset(every[:], 1.0)
                nc.vector.memset(rowstep[:, 0:1], 0.0)
                nc.vector.memset(rowstep[:, T + 1:T + 2], 0.0)
                for q in range(TILES // QUAD):
                    if q >= 2:
                        dve.wait_ge(s["spread"], q - 1)
                    for k in range(QUAD):
                        n = QUAD * q + k
                        last = nc.vector.tensor_scalar(diag[:, q % 2, k, :], const["ident"][:], qstep[:, n:n + 1], None, ALU.mult)
                    last.then_inc(s["diag_ready"], 1)
                for w, wb in ((w1, w1b), (w2, w2b)):
                    for f in range(0, wb.shape[1], wb.shape[1] // 2):
                        at = slice(f, f + wb.shape[1] // 2)
                        nc.vector.tensor_scalar(wb[:, at], w[:, at], ROUND, None, ALU.subtract).then_inc(s["quantised"], 1)

                for f in range(FC):
                    dve.wait_ge(s["turned"], FC + f + 1)
                    nc.vector.tensor_copy(W2q[:, f, :], tp[f % 2][:, 0:D]).then_inc(s["copied1"], 1)
                dve.wait_ge(s["copied1"], FC)

            @block.tensor
            def _(pe):
                for q in range(TILES // QUAD):
                    pe.wait_ge(s["diag_ready"], q + 1)
                    if q >= 2:
                        pe.wait_ge(s["rows_copied"], q - 1)
                    nc.tensor.matmul(rp[q % 2][:], lhsT=every[:], rhs=diag[:, q % 2].rearrange("p k t -> p (k t)"),
                                     start=True, stop=True).then_inc(s["spread"], 1)
                for j in range(2):
                    for f in range(FC):
                        if f == 0 or f == FC // 2:
                            pe.wait_ge(s["quantised"], 4 if j else 1 + f // (FC // 2))
                        if f >= 2:
                            pe.wait_ge(s[f"copied{j}"], f - 1)
                        elif j:
                            pe.wait_ge(s["copied0"], FC - 1 + f)
                        for c in range(DC):
                            piece = w1b[:, f, c * P:(c + 1) * P] if j == 0 else w2b[:, c, f * P:(f + 1) * P]
                            last = nc.tensor.transpose(tp[f % 2][:, c * P:(c + 1) * P], piece, const["ident_bf"][:])
                        last.then_inc(s["turned"], 1)

            @block.scalar
            def _(act):
                for q in range(TILES // QUAD):
                    act.wait_ge(s["spread"], q + 1)
                    nc.scalar.activation(rowstep[:, 1 + q * BANK:1 + (q + 1) * BANK], rp[q % 2][:], ACT.Copy,
                                         scale=mean[:, 0:1]).then_inc(s["rows_copied"], 1)
                for f in range(FC):
                    act.wait_ge(s["turned"], f + 1)
                    nc.scalar.activation(W1q[:, :, f * P:(f + 1) * P], tp[f % 2][:, 0:D].rearrange("p (c f) -> p c f", f=P),
                                         ACT.Copy).then_inc(s["copied0"], 1)
                act.wait_ge(s["copied0"], FC)


def bit_feed_forward(nc, sem, const, a, W1q, W2q, mean, rowstep, dram, out):
    scope, sb, ps = phase_scope(nc)
    FC = HID // P
    BT = 2 * P
    BLOCKS = T // BT
    HALO = BT + 2
    JC = FC // 2
    DEEP = 4
    with scope:
        taps = sb("bf_taps", [P, FC, 3])
        tap_bias = sb("bf_tap_bias", [P, FC])
        qin = sb("bf_qin", [P, 2, DC, HALO], BF16)
        x2 = sb("bf_x2", [P, 2, 2, D])
        hidden = sb("bf_hidden", [P, DEEP, 2, HALO])
        conv = sb("bf_conv", [P, DEEP, 2, BT])
        others = sb("bf_others", [P, 2, 2, BT])
        g = sb("bf_silu", [P, 2, FC, BT])
        gq = sb("bf_gq", [P, 2, FC, BT], BF16)
        top = sb("bf_top", [P, BT])
        most = sb("bf_most", [P, 2])
        step = sb("bf_step", [P, 2])
        undo = sb("bf_undo", [P, 2, 2])
        undo_late = sb("bf_undo_late", [P, 2, 2])
        diag = sb("bf_diag", [P, 2, P])
        every = sb("bf_every", [P, P])
        scale = sb("bf_scale", [P, 2, BT])
        y = sb("bf_y", [P, 2, 2, D])
        hp = [ps(f"bf_hp{k}", [P, 2, BANK]) for k in range(2)]
        op = ps("bf_op", [P, 2, BANK])
        mp = ps("bf_mp", [P, 2, P])
        sp_ = ps("bf_sp", [P, BANK])
        s = {n: sem("bf_" + n) for n in (
            "taps_in", "q_in0", "q_in1", "x_in0", "x_in1", "every_set", "first_done", "dequantised", "tapped0", "tapped", "tapped2", "silu_done", "top_done",
            "top_turned", "steps_ready", "steps_spread", "scale_ready", "scaled", "quantised", "second_done", "y_ready", "stored0", "stored1", "passed",
            "block_done")}
        x2_b = dram["x2"].rearrange("(n k p) d -> n p k d", k=2, p=P)
        out_b = out.rearrange("(n k p) d -> n p k d", k=2, p=P)

        with nc.Block() as block:
            @block.sync
            def _(sp):
                sp.dma_start(taps[:], a["conv_w"].rearrange("(f p) o k -> p f (o k)", p=P), allow_slow_non_contiguous=True).then_inc(s["taps_in"], 16)
                sp.dma_start(tap_bias[:], a["conv_b"].rearrange("(f p) -> p f", p=P), allow_slow_non_contiguous=True).then_inc(s["taps_in"], 16)

                def load(m, b):
                    n = 2 * m + b
                    sp.wait_ge(s["block_done"], n + 1)
                    sp.sem_inc(s["passed"], 1)
                    sp.dma_start(qin[:, b], dram["qT"][:, :, bass.ds(BT * n, HALO)]).then_inc(s[f"q_in{b}"], 16)

                def load_x(m, b):
                    n = 2 * m + b
                    sp.wait_ge(s["y_ready"], n + 1)
                    sp.sem_inc(s["passed"], 1)
                    sp.dma_start(x2[:, b], x2_b[n, :, :, :]).then_inc(s[f"x_in{b}"], 16)

                def store(m, b):
                    n = 2 * m + b
                    sp.wait_ge(s["y_ready"], n + 1 + 2)
                    sp.sem_inc(s["passed"], 1)
                    sp.dma_start(out_b[n, :, :, :], y[:, b]).then_inc(s[f"stored{b}"], 16)

                half = BLOCKS // 2
                load(0, 0)
                load(0, 1)
                load_x(0, 0)
                load_x(0, 1)
                load(1, 0)
                load(1, 1)
                with sp.Fori(0, half - 2) as i:
                    for b in range(2):
                        load(i + 2, b)
                        store(i, b)
                        load_x(i + 1, b)
                for b in range(2):
                    store(half - 2, b)
                    load_x(half - 1, b)
                store(half - 1, 0)
                store(half - 1, 1)
                for b in range(2):
                    sp.wait_ge(s[f"stored{b}"], 16 * (BLOCKS // 2 + 1))

            @block.gpsimd
            def _(pool):
                nc.gpsimd.memset(every[:], 1.0).then_inc(s["every_set"], 1)

                def add_taps(m, b, j):
                    pool.wait_ge(s["tapped0"], JC * (2 * m + b) + j + 1)
                    pool.sem_inc(s["passed"], 1)
                    nc.gpsimd.tensor_tensor(conv[:, j % DEEP, 1], conv[:, j % DEEP, 1], others[:, j % 2, 0], ALU.add)
                    pool.drain()
                    nc.gpsimd.tensor_tensor(conv[:, j % DEEP, 1], conv[:, j % DEEP, 1], others[:, j % 2, 1], ALU.add).then_inc(s["tapped2"], 1)

                def scaling(m, b, j):
                    if j == 0:
                        pool.wait_ge(s["scale_ready"], 2 * m + b + 1)
                        pool.sem_inc(s["passed"], 1)
                    part = g[:, b, 2 * j:2 * j + 2, :]
                    nc.gpsimd.tensor_tensor(part, part, scale[:, b].unsqueeze(1).broadcast_to([P, 2, BT]),
                                            ALU.mult).then_inc(s["scaled"], 1)

                def turn(m, b, scales=True):
                    if scales:
                        scaling(m - 1, b, 0)
                        scaling(m - 1, b, 1)
                    for j in range(JC):
                        add_taps(m, b, j)
                        if scales and j + 2 < JC:
                            scaling(m - 1, b, j + 2)

                pool.wait_ge(s["taps_in"], 32)
                pool.sem_inc(s["tapped2"], DEEP)
                turn(0, 0, scales=False)
                turn(0, 1, scales=False)
                with pool.Fori(0, BLOCKS // 2 - 1) as i:
                    turn(i + 1, 0)
                    turn(i + 1, 1)
                for b in range(2):
                    for j in range(JC):
                        scaling(BLOCKS // 2 - 1, b, j)

            @block.vector
            def _(dve):
                dve.sem_inc(s["y_ready"], 2)
                dve.sem_inc(s["dequantised"], 2)

                def dequantise(m, b, j):
                    n = 2 * m + b
                    dve.drain()
                    dve.wait_ge(s["tapped2"], JC * n + j + 1)
                    dve.sem_inc(s["passed"], 1)
                    dve.wait_ge(s["first_done"], JC * n + j + 1)
                    nc.vector.tensor_tensor(hidden[:, j % DEEP], hp[j % 2][:, :, 0:HALO],
                                            rowstep[:, bass.ds(BT * n, HALO)].unsqueeze(1).broadcast_to([P, 2, HALO]),
                                            ALU.mult).then_inc(s["dequantised"], 1)

                def add_taps(m, b, j):
                    n = 2 * m + b
                    dve.wait_ge(s["tapped0"], JC * n + j + 1)
                    for k in range(1, 3):
                        last = nc.vector.scalar_tensor_tensor(conv[:, j % DEEP, 0], hidden[:, j % DEEP, 0, k:k + BT], taps[:, 2 * j, k:k + 1],
                                                              conv[:, j % DEEP, 0], ALU.mult, ALU.add)
                        if k == 1:
                            dve.drain()
                    last.then_inc(s["tapped"], 1)

                def largest(m, b, k):
                    if k == 0:
                        dve.drain()
                        dve.wait_ge(s["silu_done"], JC * (2 * m + b + 1) + DEEP)
                    nc.vector.tensor_reduce(top[:, k * P:(k + 1) * P], g[:, b, :, k * P:(k + 1) * P].rearrange("p f t -> p t f"), AX.X, ALU.max,
                                            apply_absolute_value=True).then_inc(s["top_done"], 1)

                def steps(m, b):
                    n = 2 * m + b
                    dve.wait_ge(s["top_turned"], n + 1)
                    nc.vector.tensor_reduce(most[:], mp[:], AX.X, ALU.max)
                    dve.drain()
                    nc.vector.tensor_scalar(most[:], most[:], LEAST, None, ALU.max)
                    dve.drain()
                    nc.vector.reciprocal(step[:], most[:])
                    nc.vector.tensor_scalar(undo[:, b], most[:], mean[:, 1:2], 1.0 / LEVEL, ALU.mult, ALU.mult)
                    dve.drain()
                    nc.vector.tensor_scalar(step[:], step[:], LEVEL, None, ALU.mult)
                    dve.drain()
                    for k in range(2):
                        last = nc.vector.tensor_scalar(diag[:, k], const["ident"][:], step[:, k:k + 1], None, ALU.mult)
                    last.then_inc(s["steps_ready"], 1)

                def quantise(m, b, j):
                    dve.wait_ge(s["scaled"], JC * (2 * m + b) + j + 1)
                    nc.vector.tensor_scalar(gq[:, b, 2 * j:2 * j + 2, :], g[:, b, 2 * j:2 * j + 2, :], ROUND, ROUND,
                                            ALU.add, ALU.subtract).then_inc(s["quantised"], 1)
                    if j == 0:
                        nc.vector.tensor_scalar(undo_late[:, b], undo[:, b], 1.0, None, ALU.mult)

                def finish(m, b):
                    n = 2 * m + b
                    dve.wait_ge(s["second_done"], n + 1)
                    dve.sem_inc(s["passed"], 1)
                    dve.wait_ge(s[f"stored{b}"], 16 * (m + 1))
                    dve.sem_inc(s["passed"], 1)
                    dve.wait_ge(s[f"x_in{b}"], 16 * (m + 1))
                    for k in range(2):
                        last = nc.vector.scalar_tensor_tensor(y[:, b, k], op[:, k, :], undo_late[:, b, k:k + 1], x2[:, b, k], ALU.mult, ALU.add)
                    last.then_inc(s["y_ready"], 1)

                def turn(m, b, ends=3):
                    dequantise(m, b, 0)
                    dequantise(m, b, 1)
                    dequantise(m, b, 2)
                    if ends > 1:
                        quantise(m - 1, b, 0)
                    for j in range(JC):
                        add_taps(m, b, j)
                        if j + 3 < JC:
                            dequantise(m, b, j + 3)
                        if ends > 1 and j + 1 < JC:
                            quantise(m - 1, b, j + 1)
                        if ends and 1 <= j < 3:
                            largest(*before(m, b), j - 1)
                        if ends and j == 6:
                            steps(*before(m, b))
                        if ends > 2 and j == 7:
                            finish(*before(m - 1, b))

                half = BLOCKS // 2
                for n in range(4):
                    turn(n // 2, n % 2, ends=n)
                with dve.Fori(0, half - 2) as i:
                    turn(i + 2, 0)
                    turn(i + 2, 1)
                largest(half - 1, 1, 0)
                largest(half - 1, 1, 1)
                steps(half - 1, 1)
                for j in range(JC):
                    quantise(half - 1, 0, j)
                finish(half - 2, 1)
                dve.drain()
                for j in range(JC):
                    quantise(half - 1, 1, j)
                finish(half - 1, 0)
                finish(half - 1, 1)

            @block.scalar
            def _(act):
                act.sem_inc(s["silu_done"], DEEP)
                act.sem_inc(s["stored0"], 16)
                act.sem_inc(s["stored1"], 16)
                act.wait_ge(s["taps_in"], 32)

                def first_taps(m, b, j):
                    n = 2 * m + b
                    act.wait_ge(s["silu_done"], JC * n + j + 1)
                    act.sem_inc(s["passed"], 1)
                    act.wait_ge(s["dequantised"], JC * n + j + 1 + 2)
                    for e in range(2):
                        f = 2 * j + e
                        nc.scalar.activation(conv[:, j % DEEP, e], hidden[:, j % DEEP, e, 0:BT], ACT.Identity, bias=tap_bias[:, f:f + 1],
                                                    scale=taps[:, f, 0:1])
                    for k in range(1, 3):
                        last = nc.scalar.activation(others[:, j % 2, k - 1], hidden[:, j % DEEP, 1, k:k + BT], ACT.Copy, scale=taps[:, 2 * j + 1, k:k + 1])
                    last.then_inc(s["tapped0"], 1)

                def silu(m, b, j):
                    n = 2 * m + b
                    act.wait_ge(s["tapped"], JC * n + j + 1)
                    act.sem_inc(s["passed"], 1)
                    act.wait_ge(s["tapped2"], JC * n + j + 1 + DEEP)
                    act.sem_inc(s["passed"], 1)
                    act.wait_ge(s["quantised"], JC * n + j + 1)
                    nc.scalar.activation(g[:, b, 2 * j:2 * j + 2, :], conv[:, j % DEEP], ACT.Silu).then_inc(s["silu_done"], 1)

                def copy_scale(m, b):
                    act.wait_ge(s["steps_spread"], 2 * m + b + 1)
                    nc.scalar.activation(scale[:, b], sp_[:, 0:BT], ACT.Copy).then_inc(s["scale_ready"], 1)

                def turn(m, b, first=False):
                    first_taps(m, b, 0)
                    for j in range(JC):
                        if j + 1 < JC:
                            first_taps(m, b, j + 1)
                        silu(m, b, j)
                        if not first and j == 6:
                            copy_scale(*before(m, b))

                act.sem_inc(s["quantised"], 2 * JC)
                turn(0, 0, first=True)
                with act.Fori(0, BLOCKS // 2 - 1) as i:
                    turn(i, 1)
                    turn(i + 1, 0)
                turn(BLOCKS // 2 - 1, 1)
                copy_scale(BLOCKS // 2 - 1, 1)

            @block.tensor
            def _(pe):
                pe.sem_inc(s["block_done"], 2)
                pe.wait_ge(s["every_set"], 1)

                def first(m, b, j):
                    n = 2 * m + b
                    if j == 0:
                        pe.wait_ge(s[f"q_in{b}"], 16 * (m + 1))
                    pe.wait_ge(s["dequantised"], JC * n + j + 1)
                    for e in range(2):
                        f = 2 * j + e
                        for c in range(DC):
                            last = nc.tensor.matmul(hp[j % 2][:, e, 0:HALO], lhsT=W1q[:, c, f * P:(f + 1) * P], rhs=qin[:, b, c, :],
                                                    start=(c == 0), stop=(c == DC - 1))
                    last.then_inc(s["first_done"], 1)

                def turn_top(m, b):
                    pe.wait_ge(s["top_done"], 2 * (2 * m + b) + 2)
                    for t in range(2):
                        last = nc.tensor.transpose(mp[:, t, :], top[:, t * P:(t + 1) * P], const["ident"][:])
                    last.then_inc(s["top_turned"], 1)

                def spread_steps(m, b):
                    pe.wait_ge(s["steps_ready"], 2 * m + b + 1)
                    nc.tensor.matmul(sp_[:, 0:BT], lhsT=every[:], rhs=diag[:].rearrange("p k t -> p (k t)"), start=True,
                                     stop=True).then_inc(s["steps_spread"], 1)

                def second(m, b, part):
                    n, k = 2 * m + b, part // 2
                    if part == 0:
                        pe.wait_ge(s["quantised"], JC * (n + 3))
                        pe.sem_inc(s["passed"], 1)
                        pe.wait_ge(s["y_ready"], n + 2)
                    for f in range(part % 2 * JC, (part % 2 + 1) * JC):
                        last = nc.tensor.matmul(op[:, k, :], lhsT=gq[:, b, f, k * P:(k + 1) * P], rhs=W2q[:, f, :],
                                                start=(f == 0), stop=(f == FC - 1))
                    if part == 3:
                        last.then_inc(s["second_done"], 1)

                def turn(m, b, ends=3):
                    for j in range(JC):
                        first(m, b, j)
                        if ends > 2 and 2 <= j < 6:
                            second(*before(m - 1, b), j - 2)
                        if ends and j == 6:
                            turn_top(*before(m, b))
                        if ends and j == JC - 1:
                            spread_steps(*before(m, b))
                    pe.drain()
                    pe.sem_inc(s["block_done"], 1)

                half = BLOCKS // 2
                for n in range(4):
                    turn(n // 2, n % 2, ends=n)
                with pe.Fori(0, half - 2) as i:
                    turn(i + 2, 0)
                    turn(i + 2, 1)
                turn_top(half - 1, 1)
                spread_steps(half - 1, 1)
                for m, b in ((half - 2, 1), (half - 1, 0), (half - 1, 1)):
                    for part in range(4):
                        second(m, b, part)


def xattn_ffn(nc, a, out):
    whole = ExitStack()
    with whole:
        held = []

        def sem(name):
            held.append(nc.alloc_semaphore(name=name))
            return held[-1]

        def end_phase():
            nc.clear_and_free_semaphores(held)
            nc.all_engine_barrier()
            held.clear()

        def sb(name, shape, dt=F32):
            return whole.enter_context(nc.sbuf_tensor(name, shape, dt))

        dram = {
            "xt": nc.dram_tensor("scratch_xt", (T, D), F32).ap(),
            "qt": nc.dram_tensor("scratch_qt", (2, P, T), F32).ap(),
            "u": nc.dram_tensor("scratch_u", (T, DV), F32).ap(),
            "x2": nc.dram_tensor("scratch_x2", (T, D), F32).ap(),
            "qT": nc.dram_tensor("scratch_qT", (P, DC, T + 2), BF16).ap(),
            "wf": nc.dram_tensor("scratch_wf", (P, VC, 2 * D), F32).ap(),
            "fb": nc.dram_tensor("scratch_fb", (P, 2 * D), F32).ap(),
            "b1": nc.dram_tensor("scratch_b1", (HID,), F32).ap(),
            "K": nc.dram_tensor("scratch_K", (D, KROW), F32).ap(),
        }
        const = {"ident": sb("ident", [P, P]), "ones": sb("ones", [P, 1]),
                 "eps": sb("eps", [P, 1]),
                 "ident_bf": sb("ident_bf", [P, P], BF16)}
        ident_made = sem("ident_made")
        with nc.Block() as block:
            @block.gpsimd
            def _(pool):
                nc.gpsimd.memset(const["ident"][:], 0.0)
                nc.gpsimd.memset(const["ones"][:], 1.0)
                nc.gpsimd.memset(const["eps"][:], EPS)
                pool.drain()
                nc.gpsimd.affine_select(out=const["ident"][:], in_=const["ident"][:], compare_op=ALU.not_equal, fill=1.0,
                                        base=0, pattern=[[-1, P]], channel_multiplier=1).then_inc(ident_made, 1)
                pool.wait_ge(ident_made, 1)
                nc.gpsimd.tensor_copy(const["ident_bf"][:], const["ident"][:]).then_inc(ident_made, 1)
                pool.wait_ge(ident_made, 2)
        qstep = sb("qstep", [P, TILES])
        mean = sb("mean", [P, 2])
        keys = ExitStack()
        with keys:
            KT = keys.enter_context(nc.sbuf_tensor("KT", [P, H // 2, G], F32R))
            prepare_attention(nc, sem, const, a, KT, dram)
            end_phase()
            attention(nc, sem, const, a, KT, dram)
            end_phase()
        rows = ExitStack()
        with rows:
            X = rows.enter_context(nc.sbuf_tensor("X", [P, TILES, D], F32))
            layer = ExitStack()
            with layer:
                W = layer.enter_context(nc.sbuf_tensor("W", [P, LEVELS + 1, 2, PAIRS], F32))
                root = layer.enter_context(nc.sbuf_tensor("root", [P, 2, PAIRS], F32))
                film = ExitStack()
                with film:
                    wf = film.enter_context(nc.sbuf_tensor("wf_in", [P, VC, 2 * D], F32))
                    fb = film.enter_context(nc.sbuf_tensor("fb_in", [P, 2 * D], F32))
                    layer_weights(nc, sem, const, a, W, root, wf, fb, dram)
                    end_phase()
                    modulate(nc, sem, const, a, wf, fb, X, dram)
                    end_phase()
                s4d(nc, sem, const, a, W, root, X, dram)
                end_phase()
            second = ExitStack()
            with second:
                W1 = second.enter_context(nc.sbuf_tensor("W1", [P, DC, HID], F32))
                W2 = second.enter_context(nc.sbuf_tensor("W2", [P, HID // P, D], F32))
                b1 = second.enter_context(nc.sbuf_tensor("b1", [P, HID // P], F32))
                wf = second.enter_context(nc.sbuf_tensor("wf_out", [P, VC, 2 * D], F32))
                fb = second.enter_context(nc.sbuf_tensor("fb_out", [P, 2 * D], F32))
                feed_forward(nc, sem, const, a, wf, fb, W1, W2, b1, X, qstep, mean, dram)
                end_phase()
            third = ExitStack()
            with third:
                W1q = third.enter_context(nc.sbuf_tensor("W1q", [P, DC, HID], BF16))
                W2q = third.enter_context(nc.sbuf_tensor("W2q", [P, HID // P, D], BF16))
                rowstep = third.enter_context(nc.sbuf_tensor("rowstep", [P, T + 2], F32))
                quantise_weights(nc, sem, const, X, W1q, W2q, mean, qstep, rowstep)
                end_phase()
                bit_feed_forward(nc, sem, const, a, W1q, W2q, mean, rowstep, dram, out)


def kernel(**inputs):
    import concourse.bacc as bacc
    from concourse.bass_utils import run_bass_kernel_spmd

    nc = bacc.Bacc("TRN2", target_bir_lowering=False, num_devices=1)
    arrays, a = {}, {}
    for name, v in inputs.items():
        v = np.ascontiguousarray(v)
        if v.dtype == np.bool_:
            v = v.view(np.uint8)
        if v.ndim == 0:
            v = v.reshape(1)
        elif v.ndim > 1 and v.shape[0] == 1:
            v = v.reshape(v.shape[1:])
        arrays["in_" + name] = v
        short = {"ctx_768": "ctx", "mask_BxS_bf1": "mask1", "mask_BxS2_bf1": "mask2", "L0_ffn_w1": "ffn_w1", "L0_ffn_w2": "ffn_w2"}
        a[short.get(name, name.replace("L0_xattn_", "").replace("L0_ffn_", ""))] = nc.dram_tensor(
            "in_" + name, v.shape, mybir.dt.from_np(v.dtype), kind="ExternalInput").ap()
    out = nc.dram_tensor("out", (T, D), F32, kind="ExternalOutput").ap()
    xattn_ffn(nc, a, out)
    r = run_bass_kernel_spmd(nc, [arrays], core_ids=[0])
    return r.results[0]["out"].reshape(1, T, D)
```
